# Optimizing a Trainium2 kernel written in Bass

```python
import numpy as np
import jax
import jax.numpy as jnp

def _softmax(x, axis=-1):
    return jax.nn.softmax(x, axis=axis)

def _gelu(x):
    return jax.nn.gelu(x, approximate=True)

def _silu(x):
    return jax.nn.silu(x)

def _sigmoid(x):
    return jax.nn.sigmoid(x)

def _layernorm(x, axis=-1, eps=1e-05):
    m = jnp.mean(x, axis=axis, keepdims=True)
    v = jnp.var(x, axis=axis, keepdims=True)
    return (x - m) / jnp.sqrt(v + eps)

def _scatter_add(tgt, idx, src, axis=0):
    return tgt.at[idx].add(src)

def _segment_sum(src, seg, n):
    return jax.ops.segment_sum(src, seg, n)
kernel_name = 'mk_xattn_ffn_d4_seqx_r4_ce9ecb'

def setup_inputs(seed: int=0):
    np.random.seed(seed)
    _w = jnp.asarray

    def _rec_inputs():
        import jax
        import jax.numpy as jnp
        _rk = jax.random.key(seed)
        x = 7.22e-05 + 1 * jax.random.normal(jax.random.fold_in(_rk, 1), (8, 256, 256), jnp.float32)
        _lenS = 256 - jax.random.randint(jax.random.fold_in(_rk, 7), (8,), 0, max(1, 256 // 4) + 1, jnp.int32)
        _lenS2 = 256 - jax.random.randint(jax.random.fold_in(_rk, 8), (8,), 0, max(1, 256 // 4) + 1, jnp.int32)
        _ctx_1024P = jax.random.normal(jax.random.fold_in(_rk, 11), (8, 16, 256), jnp.float32)
        _ctx_1024c = jax.random.dirichlet(jax.random.fold_in(_rk, 511), 0.3 * jnp.ones((16,), jnp.float32), (8, 256))
        _ctx_1024t = jnp.einsum('bsk,bkd->bsd', _ctx_1024c, _ctx_1024P)
        _ctx_1024t = _ctx_1024t * jax.lax.rsqrt(jnp.mean(jnp.square(_ctx_1024t)) + 1e-12) * 0.953939
        ctx_1024 = 4.13588e-05 + 0.999923 * (_ctx_1024t + 0.3 * jax.random.normal(jax.random.fold_in(_rk, 611), (8, 256, 256), jnp.float32))
        _validS = jnp.arange(256)[None, :] < _lenS[:, None]
        _validS2 = jnp.arange(256)[None, :] < _lenS2[:, None]
        _causal = jnp.tril(jnp.ones((256, 256), dtype=bool))
        mask_Bx1xSxS2_if1 = jnp.where(jnp.ones((8, 1, 256, 256), dtype=bool), 1, 0).astype(jnp.int32)
        mask_BxSxS2_if1 = jnp.where(jnp.ones((8, 256, 256), dtype=bool), 1, 0).astype(jnp.int32)
        return (x, ctx_1024, mask_Bx1xSxS2_if1, mask_BxSxS2_if1)
    x, ctx_1024, mask_Bx1xSxS2_if1, mask_BxSxS2_if1 = _rec_inputs()

    def _L0_xattn_setup():
        import jax, jax.numpy as jnp
        import numpy as np
        D_MODEL = 256
        H = 16
        D_K = D_MODEL // H
        B, S = (4, 512)
        key = jax.random.key(seed)
        ks = jax.random.split(key, 8)
        scale = 1.0 / np.sqrt(D_MODEL)
        return {'q': jax.random.normal(ks[0], (B, S, D_MODEL), jnp.float32), 'k': jax.random.normal(ks[1], (B, S, D_MODEL), jnp.float32), 'v': jax.random.normal(ks[2], (B, S, D_MODEL), jnp.float32), 'mask': jnp.ones((B, 1, S, S), jnp.int32), 'wq': jax.random.normal(ks[3], (D_MODEL, D_MODEL), jnp.float32) * scale, 'bq': jnp.zeros((D_MODEL,), jnp.float32), 'wk': jax.random.normal(ks[4], (D_MODEL, D_MODEL), jnp.float32) * scale, 'bk': jnp.zeros((D_MODEL,), jnp.float32), 'wv': jax.random.normal(ks[5], (D_MODEL, D_MODEL), jnp.float32) * scale, 'bv': jnp.zeros((D_MODEL,), jnp.float32), 'wo': jax.random.normal(ks[6], (D_MODEL, D_MODEL), jnp.float32) * scale, 'bo': jnp.zeros((D_MODEL,), jnp.float32)}
    _L0_xattn_all = _L0_xattn_setup()
    _L0_xattn_in = {k: v for k, v in _L0_xattn_all.items() if k in ('wq', 'bq', 'wk', 'bk', 'wv', 'bv', 'wo', 'bo')}
    del _L0_xattn_all

    def _L0_ffn_setup():
        import jax, jax.numpy as jnp
        import numpy as np
        B, S, D, F, E = (4, 512, 256, 1024, 8)
        key = jax.random.key(seed)
        ks = jax.random.split(key, 7)
        s1 = 1.0 / np.sqrt(D)
        s2 = 1.0 / np.sqrt(F)
        x = jax.random.normal(ks[0], (B, S, D), dtype=jnp.float32)
        W1 = jax.random.uniform(ks[1], (E, D, F), jnp.float32, -s1, s1)
        b1 = jax.random.uniform(ks[2], (E, F), jnp.float32, -s1, s1)
        W2 = jax.random.uniform(ks[3], (E, F, D), jnp.float32, -s2, s2)
        b2 = jax.random.uniform(ks[4], (E, D), jnp.float32, -s2, s2)
        Wr = jax.random.uniform(ks[5], (D, E), jnp.float32, -s1, s1)
        br = jax.random.uniform(ks[6], (E,), jnp.float32, -s1, s1)
        return {'x': x, 'W1': W1, 'b1': b1, 'W2': W2, 'b2': b2, 'Wr': Wr, 'br': br}
    _L0_ffn_all = _L0_ffn_setup()
    _L0_ffn_in = {k: v for k, v in _L0_ffn_all.items() if k in ('W1', 'b1', 'W2', 'b2', 'Wr', 'br')}
    del _L0_ffn_all

    def _L1_xattn_setup():
        import jax, jax.numpy as jnp
        import numpy as np
        from jax import lax
        BIG = jnp.float32(1e+30)

        def _pairwise_euclidean(a, b):
            aa = jnp.sum(a * a, axis=-1)[:, None]
            bb = jnp.sum(b * b, axis=-1)[None, :]
            ab = a @ b.T
            return jnp.sqrt(jnp.maximum(aa + bb - 2.0 * ab, 0.0))

        def _dtw_cost(D):
            row0 = jnp.cumsum(D[0])

            def row_step(prev_row, d_row):
                first = d_row[0] + prev_row[0]

                def col_step(left, inp):
                    d_ij, up, diag = inp
                    r = d_ij + jnp.minimum(jnp.minimum(up, left), diag)
                    return (r, r)
                _, rest = lax.scan(col_step, first, (d_row[1:], prev_row[1:], prev_row[:-1]))
                row = jnp.concatenate([first[None], rest])
                return (row, row)
            _, rows = lax.scan(row_step, row0, D[1:])
            return jnp.concatenate([row0[None], rows], axis=0)

        def _backtrack(R, T1, T2):
            L = T1 + T2 - 1

            def step(carry, _):
                i, j, done = carry
                valid = jnp.logical_not(done)
                cd = jnp.where((i > 0) & (j > 0), R[jnp.maximum(i - 1, 0), jnp.maximum(j - 1, 0)], BIG)
                cu = jnp.where(i > 0, R[jnp.maximum(i - 1, 0), j], BIG)
                cl = jnp.where(j > 0, R[i, jnp.maximum(j - 1, 0)], BIG)
                choice = jnp.argmin(jnp.stack([cd, cu, cl]))
                ni = jnp.where(choice <= 1, i - 1, i)
                nj = jnp.where((choice == 0) | (choice == 2), j - 1, j)
                at_origin = (i == 0) & (j == 0)
                ni = jnp.where(at_origin, 0, ni)
                nj = jnp.where(at_origin, 0, nj)
                return ((ni, nj, done | at_origin), (i, j, valid))
            init = (jnp.int32(T1 - 1), jnp.int32(T2 - 1), jnp.bool_(False))
            _, (i_idx, j_idx, valid) = lax.scan(step, init, None, length=L)
            return (i_idx, j_idx, valid)

        def _align_one(small, large):
            T_small, d = small.shape
            T_large = large.shape[0]
            D = _pairwise_euclidean(small, large)
            R = _dtw_cost(D)
            i_idx, j_idx, valid = _backtrack(R, T_small, T_large)
            contrib = small[i_idx] * valid[:, None].astype(small.dtype)
            expanded = jnp.zeros((T_large, d), dtype=small.dtype).at[j_idx].add(contrib)
            return expanded
        key = jax.random.key(seed)
        k1, k2 = jax.random.split(key)
        teacher = jax.random.normal(k1, (16, 100, 256), dtype=jnp.float32)
        student = jax.random.normal(k2, (16, 150, 256), dtype=jnp.float32)
        return {'teacher_features': teacher, 'student_features': student}
    _L1_xattn_all = _L1_xattn_setup()
    _L1_xattn_in = {k: v for k, v in _L1_xattn_all.items() if k in ()}
    del _L1_xattn_all

    def _L1_ffn_setup():
        import jax, jax.numpy as jnp
        import numpy as np
        DIM = 256
        HIDDEN = 768
        SCALE = 1.0 / 127.0

        def _dequant(w_int, dtype):
            return w_int.astype(dtype) * jnp.asarray(SCALE, dtype)
        key = jax.random.key(seed)
        k_x, k_g, k_u, k_d = jax.random.split(key, 4)
        x = jax.random.normal(k_x, (4, 512, DIM), dtype=jnp.float32)
        w_gate = jax.random.randint(k_g, (HIDDEN, DIM), -127, 128, dtype=jnp.int32)
        w_up = jax.random.randint(k_u, (HIDDEN, DIM), -127, 128, dtype=jnp.int32)
        w_down = jax.random.randint(k_d, (DIM, HIDDEN), -127, 128, dtype=jnp.int32)
        return {'x': x, 'w_gate': w_gate, 'w_up': w_up, 'w_down': w_down}
    _L1_ffn_all = _L1_ffn_setup()
    _L1_ffn_in = {k: v for k, v in _L1_ffn_all.items() if k in ('w_gate', 'w_up', 'w_down')}
    del _L1_ffn_all

    def _L2_xattn_setup():
        import jax, jax.numpy as jnp
        import numpy as np
        HIDDEN = 256
        N_HEAD = 16
        HEAD_DIM = HIDDEN // N_HEAD

        def _rope(x):
            L, d = (x.shape[-2], x.shape[-1])
            pos = jnp.arange(L, dtype=x.dtype)[:, None]
            ids = jnp.arange(d // 2, dtype=x.dtype)
            theta = jnp.power(jnp.asarray(10000.0, x.dtype), 2.0 * ids / d)
            ang = pos / theta
            sin = jnp.repeat(jnp.sin(ang), 2, axis=-1)
            cos = jnp.repeat(jnp.cos(ang), 2, axis=-1)
            x_rot = jnp.stack([-x[..., 1::2], x[..., 0::2]], axis=-1).reshape(x.shape)
            return x * cos + x_rot * sin
        key = jax.random.key(seed)
        ks = jax.random.split(key, 5)
        B, LQ, LK = (8, 256, 512)
        scale = 1.0 / np.sqrt(HIDDEN)
        return {'x': jax.random.normal(ks[0], (B, LQ, HIDDEN), dtype=jnp.float32), 'y': jax.random.normal(ks[1], (B, LK, HIDDEN), dtype=jnp.float32), 'Wq': jax.random.normal(ks[2], (HIDDEN, HIDDEN), dtype=jnp.float32) * scale, 'Wkv': jax.random.normal(ks[3], (2 * HIDDEN, HIDDEN), dtype=jnp.float32) * scale, 'Wo': jax.random.normal(ks[4], (HIDDEN, HIDDEN), dtype=jnp.float32) * scale}
    _L2_xattn_all = _L2_xattn_setup()
    _L2_xattn_in = {k: v for k, v in _L2_xattn_all.items() if k in ('Wq', 'Wkv', 'Wo')}
    del _L2_xattn_all

    def _L2_ffn_setup():
        import jax, jax.numpy as jnp
        import numpy as np
        B, M, D, E, K = (1024, 4, 256, 8, 2)
        H = 4 * D
        key = jax.random.key(seed)
        k0, k1, k2, k3 = jax.random.split(key, 4)
        x = jax.random.normal(k0, (B, M, D), jnp.float32)
        Wg = jax.random.normal(k1, (D, E), jnp.float32) * D ** (-0.5)
        bg = jnp.zeros((E,), jnp.float32)
        W1 = jax.random.normal(k2, (E, D, H), jnp.float32) * D ** (-0.5)
        b1 = jnp.zeros((E, H), jnp.float32)
        W2 = jax.random.normal(k3, (E, H, D), jnp.float32) * H ** (-0.5)
        b2 = jnp.zeros((E, D), jnp.float32)
        return {'x': x, 'Wg': Wg, 'bg': bg, 'W1': W1, 'b1': b1, 'W2': W2, 'b2': b2}
    _L2_ffn_all = _L2_ffn_setup()
    _L2_ffn_in = {k: v for k, v in _L2_ffn_all.items() if k in ('Wg', 'bg', 'W1', 'b1', 'W2', 'b2')}
    del _L2_ffn_all

    def _L3_xattn_setup():
        import jax, jax.numpy as jnp
        import numpy as np
        B, S, D, H = (2, 512, 256, 16)
        DK = D // H
        K = 32
        NEG = -1000000000.0
        rng = jax.random.key(seed)
        ks = jax.random.split(rng, 12)

        def w(k):
            return jax.random.normal(k, (D, D), jnp.float32) * 0.02

        def b(k):
            return jax.random.normal(k, (D,), jnp.float32) * 0.02
        return {'query': jax.random.normal(ks[0], (B, S, D), jnp.float32), 'key': jax.random.normal(ks[1], (B, S, D), jnp.float32), 'value': jax.random.normal(ks[2], (B, S, D), jnp.float32), 'Wq': w(ks[3]), 'bq': b(ks[4]), 'Wk': w(ks[5]), 'bk': b(ks[6]), 'Wv': w(ks[7]), 'bv': b(ks[8]), 'Wo': w(ks[9]), 'bo': b(ks[10]), 'mask': jnp.ones((B, S, S), jnp.int32), 'topk': K}
    _L3_xattn_all = _L3_xattn_setup()
    _L3_xattn_in = {k: v for k, v in _L3_xattn_all.items() if k in ('Wq', 'bq', 'Wk', 'bk', 'Wv', 'bv', 'Wo', 'bo')}
    del _L3_xattn_all

    def _L3_ffn_setup():
        import jax, jax.numpy as jnp
        import numpy as np
        B, N, C, H, REG = (1, 2309, 256, 16, 5)
        D = C // H
        key = jax.random.key(seed)
        k0, k1, k2, k3 = jax.random.split(key, 4)
        x = jax.random.normal(k0, (B, N, C), dtype=jnp.float32)
        g_info = jax.random.normal(k1, (12, 2, C), dtype=jnp.float32)
        W_qkv = jax.random.normal(k2, (C, 3 * C), dtype=jnp.float32) * 0.02
        W_proj = jax.random.normal(k3, (C, C), dtype=jnp.float32) * 0.02
        b_proj = jnp.zeros((C,), dtype=jnp.float32)
        return {'x': x, 'g_info': g_info, 'W_qkv': W_qkv, 'W_proj': W_proj, 'b_proj': b_proj}
    _L3_ffn_all = _L3_ffn_setup()
    _L3_ffn_in = {k: v for k, v in _L3_ffn_all.items() if k in ('g_info', 'W_qkv', 'W_proj', 'b_proj')}
    del _L3_ffn_all
    return {'x': x, 'ctx_1024': ctx_1024, 'mask_Bx1xSxS2_if1': mask_Bx1xSxS2_if1, 'mask_BxSxS2_if1': mask_BxSxS2_if1, 'L0_xattn_wq': _L0_xattn_in['wq'], 'L0_xattn_bq': _L0_xattn_in['bq'], 'L0_xattn_wk': _L0_xattn_in['wk'], 'L0_xattn_bk': _L0_xattn_in['bk'], 'L0_xattn_wv': _L0_xattn_in['wv'], 'L0_xattn_bv': _L0_xattn_in['bv'], 'L0_xattn_wo': _L0_xattn_in['wo'], 'L0_xattn_bo': _L0_xattn_in['bo'], 'L0_ffn_W1': _L0_ffn_in['W1'], 'L0_ffn_b1': _L0_ffn_in['b1'], 'L0_ffn_W2': _L0_ffn_in['W2'], 'L0_ffn_b2': _L0_ffn_in['b2'], 'L0_ffn_Wr': _L0_ffn_in['Wr'], 'L0_ffn_br': _L0_ffn_in['br'], 'L1_ffn_w_gate': _L1_ffn_in['w_gate'], 'L1_ffn_w_up': _L1_ffn_in['w_up'], 'L1_ffn_w_down': _L1_ffn_in['w_down'], 'L2_xattn_Wq': _L2_xattn_in['Wq'], 'L2_xattn_Wkv': _L2_xattn_in['Wkv'], 'L2_xattn_Wo': _L2_xattn_in['Wo'], 'L2_ffn_Wg': _L2_ffn_in['Wg'], 'L2_ffn_bg': _L2_ffn_in['bg'], 'L2_ffn_W1': _L2_ffn_in['W1'], 'L2_ffn_b1': _L2_ffn_in['b1'], 'L2_ffn_W2': _L2_ffn_in['W2'], 'L2_ffn_b2': _L2_ffn_in['b2'], 'L3_xattn_Wq': _L3_xattn_in['Wq'], 'L3_xattn_bq': _L3_xattn_in['bq'], 'L3_xattn_Wk': _L3_xattn_in['Wk'], 'L3_xattn_bk': _L3_xattn_in['bk'], 'L3_xattn_Wv': _L3_xattn_in['Wv'], 'L3_xattn_bv': _L3_xattn_in['bv'], 'L3_xattn_Wo': _L3_xattn_in['Wo'], 'L3_xattn_bo': _L3_xattn_in['bo'], 'L3_ffn_g_info': _L3_ffn_in['g_info'], 'L3_ffn_W_qkv': _L3_ffn_in['W_qkv'], 'L3_ffn_W_proj': _L3_ffn_in['W_proj'], 'L3_ffn_b_proj': _L3_ffn_in['b_proj']}

def reference(x, ctx_1024, mask_Bx1xSxS2_if1, mask_BxSxS2_if1, L0_xattn_wq, L0_xattn_bq, L0_xattn_wk, L0_xattn_bk, L0_xattn_wv, L0_xattn_bv, L0_xattn_wo, L0_xattn_bo, L0_ffn_W1, L0_ffn_b1, L0_ffn_W2, L0_ffn_b2, L0_ffn_Wr, L0_ffn_br, L1_ffn_w_gate, L1_ffn_w_up, L1_ffn_w_down, L2_xattn_Wq, L2_xattn_Wkv, L2_xattn_Wo, L2_ffn_Wg, L2_ffn_bg, L2_ffn_W1, L2_ffn_b1, L2_ffn_W2, L2_ffn_b2, L3_xattn_Wq, L3_xattn_bq, L3_xattn_Wk, L3_xattn_bk, L3_xattn_Wv, L3_xattn_bv, L3_xattn_Wo, L3_xattn_bo, L3_ffn_g_info, L3_ffn_W_qkv, L3_ffn_W_proj, L3_ffn_b_proj):
    import jax
    import jax.numpy as jnp

    def _L0_xattn_ref(q, k, v, mask, wq, bq, wk, bk, wv, bv, wo, bo):
        import jax, jax.numpy as jnp
        import numpy as np
        D_MODEL = 256
        H = 16
        D_K = D_MODEL // H
        B, S = (4, 512)
        query = q @ wq.T + bq
        key_p = k @ wk.T + bk
        value = v @ wv.T + bv
        b, s = (query.shape[0], query.shape[1])
        query = query.reshape(b, s, H, D_K).transpose(0, 2, 1, 3)
        key_p = key_p.reshape(b, s, H, D_K).transpose(0, 2, 1, 3)
        value = value.reshape(b, s, H, D_K).transpose(0, 2, 1, 3)
        scores = jnp.einsum('bhqd,bhkd->bhqk', query, key_p) / jnp.sqrt(jnp.asarray(D_K, query.dtype))
        attn = jax.nn.softmax(scores, axis=-1)
        x = jnp.einsum('bhqk,bhkd->bhqd', attn, value)
        x = x.transpose(0, 2, 1, 3).reshape(b, s, D_MODEL)
        return x @ wo.T + bo

    def _L0_ffn_ref(x, W1, b1, W2, b2, Wr, br):
        import jax, jax.numpy as jnp
        import numpy as np
        B, S, D, F, E = (4, 512, 256, 1024, 8)
        b, s, d = x.shape
        e = Wr.shape[1]
        logits = x @ Wr + br
        idx = jnp.argmax(logits, axis=-1)
        probs = jax.nn.softmax(logits, axis=-1)
        gates = jnp.take_along_axis(probs, idx[..., None], axis=-1)[..., 0]
        xf = x.reshape(-1, d)
        idxf = idx.reshape(-1)
        gf = gates.reshape(-1)
        out = jnp.zeros_like(xf)
        for ei in range(e):
            h = jax.nn.gelu(xf @ W1[ei] + b1[ei], approximate=False)
            y = h @ W2[ei] + b2[ei]
            mask = (idxf == ei).astype(xf.dtype)
            out = out + y * (gf * mask)[:, None]
        return out.reshape(b, s, d)

    def _L1_xattn_ref(teacher_features, student_features):
        import jax, jax.numpy as jnp
        import numpy as np
        from jax import lax
        BIG = jnp.float32(1e+30)

        def _pairwise_euclidean(a, b):
            aa = jnp.sum(a * a, axis=-1)[:, None]
            bb = jnp.sum(b * b, axis=-1)[None, :]
            ab = a @ b.T
            return jnp.sqrt(jnp.maximum(aa + bb - 2.0 * ab, 0.0))

        def _dtw_cost(D):
            row0 = jnp.cumsum(D[0])

            def row_step(prev_row, d_row):
                first = d_row[0] + prev_row[0]

                def col_step(left, inp):
                    d_ij, up, diag = inp
                    r = d_ij + jnp.minimum(jnp.minimum(up, left), diag)
                    return (r, r)
                _, rest = lax.scan(col_step, first, (d_row[1:], prev_row[1:], prev_row[:-1]))
                row = jnp.concatenate([first[None], rest])
                return (row, row)
            _, rows = lax.scan(row_step, row0, D[1:])
            return jnp.concatenate([row0[None], rows], axis=0)

        def _backtrack(R, T1, T2):
            L = T1 + T2 - 1

            def step(carry, _):
                i, j, done = carry
                valid = jnp.logical_not(done)
                cd = jnp.where((i > 0) & (j > 0), R[jnp.maximum(i - 1, 0), jnp.maximum(j - 1, 0)], BIG)
                cu = jnp.where(i > 0, R[jnp.maximum(i - 1, 0), j], BIG)
                cl = jnp.where(j > 0, R[i, jnp.maximum(j - 1, 0)], BIG)
                choice = jnp.argmin(jnp.stack([cd, cu, cl]))
                ni = jnp.where(choice <= 1, i - 1, i)
                nj = jnp.where((choice == 0) | (choice == 2), j - 1, j)
                at_origin = (i == 0) & (j == 0)
                ni = jnp.where(at_origin, 0, ni)
                nj = jnp.where(at_origin, 0, nj)
                return ((ni, nj, done | at_origin), (i, j, valid))
            init = (jnp.int32(T1 - 1), jnp.int32(T2 - 1), jnp.bool_(False))
            _, (i_idx, j_idx, valid) = lax.scan(step, init, None, length=L)
            return (i_idx, j_idx, valid)

        def _align_one(small, large):
            T_small, d = small.shape
            T_large = large.shape[0]
            D = _pairwise_euclidean(small, large)
            R = _dtw_cost(D)
            i_idx, j_idx, valid = _backtrack(R, T_small, T_large)
            contrib = small[i_idx] * valid[:, None].astype(small.dtype)
            expanded = jnp.zeros((T_large, d), dtype=small.dtype).at[j_idx].add(contrib)
            return expanded
        return jax.vmap(_align_one)(teacher_features, student_features)

    def _L1_ffn_ref(x, w_gate, w_up, w_down):
        import jax, jax.numpy as jnp
        import numpy as np
        DIM = 256
        HIDDEN = 768
        SCALE = 1.0 / 127.0

        def _dequant(w_int, dtype):
            return w_int.astype(dtype) * jnp.asarray(SCALE, dtype)
        wg = _dequant(w_gate, x.dtype)
        wu = _dequant(w_up, x.dtype)
        wd = _dequant(w_down, x.dtype)
        gate = jnp.einsum('bsd,hd->bsh', x, wg)
        up = jnp.einsum('bsd,hd->bsh', x, wu)
        h = jax.nn.silu(gate) * up
        return jnp.einsum('bsh,dh->bsd', h, wd)

    def _L2_xattn_ref(x, y, Wq, Wkv, Wo):
        import jax, jax.numpy as jnp
        import numpy as np
        HIDDEN = 256
        N_HEAD = 16
        HEAD_DIM = HIDDEN // N_HEAD

        def _rope(x):
            L, d = (x.shape[-2], x.shape[-1])
            pos = jnp.arange(L, dtype=x.dtype)[:, None]
            ids = jnp.arange(d // 2, dtype=x.dtype)
            theta = jnp.power(jnp.asarray(10000.0, x.dtype), 2.0 * ids / d)
            ang = pos / theta
            sin = jnp.repeat(jnp.sin(ang), 2, axis=-1)
            cos = jnp.repeat(jnp.cos(ang), 2, axis=-1)
            x_rot = jnp.stack([-x[..., 1::2], x[..., 0::2]], axis=-1).reshape(x.shape)
            return x * cos + x_rot * sin
        B, LQ, _ = x.shape
        LK = y.shape[1]
        q = (x @ Wq.T).reshape(B, LQ, N_HEAD, HEAD_DIM).transpose(0, 2, 1, 3)
        kv = (y @ Wkv.T).reshape(B, LK, N_HEAD, 2 * HEAD_DIM).transpose(0, 2, 1, 3)
        k, v = jnp.split(kv, 2, axis=-1)
        q = _rope(q)
        k = _rope(k)
        scores = jnp.einsum('bhqd,bhkd->bhqk', q, k)
        probs = jax.nn.softmax(scores, axis=-1)
        out = jnp.einsum('bhqk,bhkd->bhqd', probs, v)
        out = out.transpose(0, 2, 1, 3).reshape(B, LQ, HIDDEN)
        return out @ Wo.T

    def _L2_ffn_ref(x, Wg, bg, W1, b1, W2, b2):
        import jax, jax.numpy as jnp
        import numpy as np
        B, M, D, E, K = (1024, 4, 256, 8, 2)
        H = 4 * D
        Bn, Mn, Dn = x.shape
        xf = x.reshape(-1, Dn)
        logits = xf @ Wg + bg
        topv, topi = jax.lax.top_k(logits, K)
        topw = jax.nn.softmax(topv, axis=-1)
        gates = jnp.sum(jax.nn.one_hot(topi, E, dtype=xf.dtype) * topw[..., None], axis=1)

        def body(acc, p):
            W1e, b1e, W2e, b2e, ge = p
            y = jax.nn.gelu(xf @ W1e + b1e, approximate=False) @ W2e + b2e
            return (acc + ge[:, None] * y, None)
        out, _ = jax.lax.scan(body, jnp.zeros_like(xf), (W1, b1, W2, b2, gates.T))
        return out.reshape(Bn, Mn, Dn)

    def _L3_xattn_ref(query, key, value, Wq, bq, Wk, bk, Wv, bv, Wo, bo, mask, topk):
        import jax, jax.numpy as jnp
        import numpy as np
        B, S, D, H = (2, 512, 256, 16)
        DK = D // H
        K = 32
        NEG = -1000000000.0
        Bn, Sq, Dm = query.shape
        q = (query @ Wq.T + bq).reshape(Bn, Sq, H, DK).transpose(0, 2, 1, 3)
        k = (key @ Wk.T + bk).reshape(Bn, -1, H, DK).transpose(0, 2, 1, 3)
        v = (value @ Wv.T + bv).reshape(Bn, -1, H, DK).transpose(0, 2, 1, 3)
        scores = jnp.einsum('bhqd,bhkd->bhqk', q, k) / jnp.asarray(np.sqrt(DK), (scores_dtype := q.dtype))
        scores = jnp.where(mask[:, None] == 0, jnp.asarray(NEG, scores.dtype), scores)
        kk = min(topk, scores.shape[-1])
        vals, idx = jax.lax.top_k(scores, kk)
        p = jax.nn.softmax(vals, axis=-1)
        vg = jnp.take_along_axis(v[:, :, None, :, :], idx[..., None], axis=3)
        ctx = jnp.einsum('bhqk,bhqkd->bhqd', p, vg)
        x = ctx.transpose(0, 2, 1, 3).reshape(Bn, Sq, Dm)
        return x @ Wo.T + bo

    def _L3_ffn_ref(x, g_info, W_qkv, W_proj, b_proj):
        import jax, jax.numpy as jnp
        import numpy as np
        B, N, C, H, REG = (1, 2309, 256, 16, 5)
        D = C // H
        Bx, Nx, Cx = x.shape
        scale = D ** (-0.5)
        qkv = (x @ W_qkv).reshape(Bx, Nx, 3, H, D)
        q, k, v = (qkv[:, :, 0], qkv[:, :, 1], qkv[:, :, 2])
        g_layer = g_info[0].reshape(-1, H, D)
        q_g = g_layer[0]
        q_pure = q[:, REG:]
        q_n = q_pure / jnp.linalg.norm(q_pure, axis=-1, keepdims=True)
        qg_n = q_g / jnp.linalg.norm(q_g, axis=-1, keepdims=True)
        sim = (qg_n[None, None] * q_n).sum(-1).mean(-1)
        sim = (sim - sim.min()) / (sim.max() - sim.min())
        pos = sim > 0.9
        logits = jnp.einsum('bqhd,bkhd->bhqk', q * scale, k)

        def masked_attn(tok_mask):
            key_mask = jnp.concatenate([jnp.ones((Bx, REG), bool), tok_mask], axis=1)
            l = jnp.where(key_mask[:, None, None, :], logits, -jnp.inf)
            a = jax.nn.softmax(l, axis=-1)
            return jnp.einsum('bhqk,bkhd->bqhd', a, v)
        x_pos = masked_attn(pos)
        x_neg = masked_attn(~pos)
        reg_out = (x_pos[:, :REG] + x_neg[:, :REG]) * 0.5
        tok_out = jnp.where(pos[:, :, None, None], x_pos[:, REG:], x_neg[:, REG:])
        out = jnp.concatenate([reg_out, tok_out], axis=1).reshape(Bx, Nx, Cx)
        return out @ W_proj + b_proj
    x = x + _L0_xattn_ref(_layernorm(x, axis=-1), ctx_1024, ctx_1024, mask_Bx1xSxS2_if1, L0_xattn_wq, L0_xattn_bq, L0_xattn_wk, L0_xattn_bk, L0_xattn_wv, L0_xattn_bv, L0_xattn_wo, L0_xattn_bo)
    x = x + _L0_ffn_ref(_layernorm(x, axis=-1), L0_ffn_W1, L0_ffn_b1, L0_ffn_W2, L0_ffn_b2, L0_ffn_Wr, L0_ffn_br)
    x = x + _L1_xattn_ref(ctx_1024, _layernorm(x, axis=-1))
    x = x + _L1_ffn_ref(_layernorm(x, axis=-1), L1_ffn_w_gate, L1_ffn_w_up, L1_ffn_w_down)
    x = x + _L2_xattn_ref(_layernorm(x, axis=-1), ctx_1024, L2_xattn_Wq, L2_xattn_Wkv, L2_xattn_Wo)
    x = x + _L2_ffn_ref(_layernorm(x, axis=-1), L2_ffn_Wg, L2_ffn_bg, L2_ffn_W1, L2_ffn_b1, L2_ffn_W2, L2_ffn_b2)
    x = x + _L3_xattn_ref(_layernorm(x, axis=-1), ctx_1024, ctx_1024, L3_xattn_Wq, L3_xattn_bq, L3_xattn_Wk, L3_xattn_bk, L3_xattn_Wv, L3_xattn_bv, L3_xattn_Wo, L3_xattn_bo, mask_BxSxS2_if1, 32)
    x = x + _L3_ffn_ref(_layernorm(x, axis=-1), L3_ffn_g_info, L3_ffn_W_qkv, L3_ffn_W_proj, L3_ffn_b_proj)
    return x

_drawn_inputs = setup_inputs


def setup_inputs(seed=0):
    import zlib

    import numpy as np

    out = dict(_drawn_inputs(seed))
    spreads = {'L0_xattn_bq': (0.0, 0.352),
     'L0_xattn_bk': (0.0, 2.0),
     'L0_xattn_bv': (0.0, 0.1),
     'L0_xattn_bo': (0.0, 0.1),
     'L2_ffn_bg': (0.0, 2.0),
     'L2_ffn_b1': (0.0, 2.0),
     'L2_ffn_b2': (0.0, 2.0),
     'L3_ffn_b_proj': (0.0, 2.0)}
    factors = {'L0_ffn_b1': 8.0,
     'L0_ffn_b2': 8.0,
     'L0_ffn_br': 4.674,
     'L2_xattn_Wq': 8.0,
     'L2_xattn_Wkv': 8.0,
     'L2_xattn_Wo': 8.0,
     'L2_ffn_Wg': 8.0,
     'L2_ffn_W1': 8.0,
     'L2_ffn_W2': 8.0,
     'L3_xattn_Wq': 64.0,
     'L3_xattn_bq': 64.0,
     'L3_xattn_Wk': 64.0,
     'L3_xattn_Wv': 63.551,
     'L3_xattn_bv': 64.0,
     'L3_xattn_Wo': 63.06,
     'L3_xattn_bo': 64.0,
     'L3_ffn_g_info': 64.0,
     'L3_ffn_W_qkv': 64.0,
     'L3_ffn_W_proj': 64.0,
     'L3_xattn_bk': 8.0}
    for name, (base, spread) in spreads.items():
        noise = np.random.default_rng([zlib.crc32(name.encode()), seed]).standard_normal(out[name].shape)
        drawn = base * np.exp(spread * noise) if base else spread * noise
        out[name] = jnp.asarray(drawn.astype(out[name].dtype))
    for name, factor in factors.items():
        out[name] = (out[name] * factor).astype(out[name].dtype)
    return out
```

```python
from contextlib import ExitStack

import numpy as np

import concourse.bass as bass
from concourse import mybir

F32 = mybir.dt.float32
BF16 = mybir.dt.bfloat16
I32 = mybir.dt.int32
U32 = mybir.dt.uint32
ALU = mybir.AluOpType
ACT = mybir.ActivationFunctionType
AX = mybir.AxisListType

P = 128
B, S, D = 8, 256, 256
TOK = B * S
NT = TOK // P
DC = D // P
H, DK = 16, 16
QT = S // P
EPS = 1e-5
STEPS = H
PER_QT = STEPS // QT
BIG = 1.0e30
NEG = -1.0e9
TOPK = 32
REG = 5
PAIRS_OF_PARTS = [(a, b) for a in range(3) for b in range(3) if a + b < 4]
FIRST_AT, KEEP_AT, SECOND_AT, LAST_AT = (0, 1), (0, 1), (2, 3), (2, 3)
RG = H * REG
GONE = -3.0e38


class Scope:

    def __init__(self, nc, name):
        self.nc, self.name, self.ctx, self.sems, self.blocks = nc, name, ExitStack(), [], ExitStack()

    def __enter__(self):
        self.ctx.__enter__()
        return self

    def __exit__(self, *what):
        self.blocks.__exit__(*what)
        if what[0] is None:
            numbers = sorted(x.num for x in self.sems) if self.name != "all" else []
            while numbers:
                n = 1
                while n < len(numbers) and numbers[n] == numbers[0] + n:
                    n += 1
                self.nc.all_engine_barrier(sems_to_clear=range(numbers[0], numbers[0] + n))
                numbers = numbers[n:]
        return self.ctx.__exit__(*what)

    def sb(self, name, shape, dt=F32):
        return self.ctx.enter_context(self.nc.sbuf_tensor(f"{self.name}_{name}", shape, dt))

    def ps(self, name, shape, dt=F32):
        return self.ctx.enter_context(self.nc.psum_tensor(f"{self.name}_{name}", shape, dt))

    def sem(self, name):
        self.sems.append(self.ctx.enter_context(self.nc.semaphore(f"{self.name}_{name}")))
        return self.sems[-1]

    def block(self):
        return self.blocks.enter_context(self.nc.Block())


def layernorm_stats(nc, x, rstd, mean, name):
    with Scope(nc, f"{name}_ln") as s:
        st = s.sb("st", [P, NT, 6])
        mv = s.sb("mv", [P, NT, 2])
        std = s.sb("std", [P, NT])
        epst = s.sb("eps", [P, 1])
        eps_set, stats, moments, rooted, done = (s.sem(n) for n in ("eps_set", "stats", "moments", "rooted", "done"))
        block = s.block()

        @block.vector
        def _(dve):
            nc.vector.memset(epst[:], EPS).then_inc(eps_set, 1)
            for t in range(NT):
                nc.vector.bn_stats(st[:, t, :], x[:, t, :]).then_inc(stats, 1)
            dve.wait_ge(stats, NT)
            for t in range(NT):
                nc.vector.bn_aggr(mv[:, t, :], st[:, t, :]).then_inc(moments, 1)
            dve.wait_ge(moments, NT)
            nc.vector.tensor_copy(mean[:], mv[:, :, 0])
            dve.wait_ge(rooted, 1)
            nc.vector.reciprocal(rstd[:], std[:]).then_inc(done, 1)

        @block.scalar
        def _(act):
            act.wait_ge(eps_set, 1)
            act.wait_ge(moments, NT)
            nc.scalar.activation(std[:], mv[:, :, 1], ACT.Sqrt, bias=epst[:, 0:1]).then_inc(rooted, 1)


def attention(nc, name, x, ident, rstd, mean, scale, w, parts_at, ctxT=None, rope=None, topk=None, groups=None):
    with Scope(nc, name) as s:
        names = ["wq", "wk", "wv", "wo"] + (["wq_swap", "wk_swap"] if rope is not None else [])
        W = {n: s.sb(n, [P, DC, D]) for n in names}
        Bc = {n: s.sb(n, [P, DC]) for n in ("bq", "bk") if w.get(n) is not None}
        Br = {n: s.sb(n, [P, D]) for n in ("bv", "bo") if w.get(n) is not None}
        xn = s.sb("xn", [P, 2, QT, D])
        xnT = s.sb("xnT", [P, 2, DC, S])
        kvT = s.sb("kvT", [P, 2, DC, S]) if ctxT is not None else xnT
        qf = s.sb("qf", [P, 2, DC, S])
        part = s.sb("part", [P, 2, 3, DC, S], BF16)
        rest_of = s.sb("rest_of", [P, 2, DC, S])
        stack = s.sb("stack", [P, 2, 2, H, S], BF16)
        kT = s.sb("kT", [P, 2, DC, S])
        v = s.sb("v", [P, 2, QT, D])
        prob = s.sb("prob", [P, 4, 2, S])
        probT = s.sb("probT", [P, 2, 2, 2, P])
        nmax = s.sb("nmax", [P, QT, H])
        rsum = s.sb("rsum", [P, 2, QT, H])
        rinv = s.sb("rinv", [P, QT, H])
        on = s.sb("on", [P, QT, H, DK])
        oT = s.sb("oT", [P, DC, P])
        if rope is not None:
            cosT, sinT = s.sb("cosT", [P, S]), s.sb("sinT", [P, S])
            rot = s.sb("rot", [P, 2, DC, S])
            krot = s.sb("krot", [P, 2, DC, S])
        if topk is not None:
            mraw = s.sb("mraw", [P, 2, QT, S], I32)
            mlow = s.sb("mlow", [P, 2, QT, S])
            mone = s.sb("mone", [P, 2, QT, S])
            raw_sc = s.sb("raw_sc", [P, 2, 2, S])
            kept = s.sb("kept", [P, 2, S])
            bound = s.sb("bound", [P, 1])
            sc_sb = s.sb("sc_sb", [P, 2, 2, S])
            left = s.sb("left", [P, 2, 2, S])
            top8 = s.sb("top8", [P, 2, 2, TOPK])
            expd = s.sb("expd", [P, 2, 2, S])
            rest = s.sb("rest", [P, 2, 2, S])
            top_exp = s.sb("top_exp", [P, 2, TOPK])
        if groups is not None:
            mq, mk = s.sb("mq", [P, 2, S], BF16), s.sb("mk", [P, 2, S], BF16)
            rg_sel, rg_own, rg_fold, rg_one = (s.sb(n, sh) for n, sh in (
                ("rg_sel", [P, DC, H]), ("rg_own", [RG, D]), ("rg_fold", [RG, REG]), ("rg_one", [2, RG])))
            rg_two = s.sb("rg_two", [2, RG], BF16)
            rg_q = s.sb("rg_q", [P, DC, H, REG])
            rg_nmax, rg_sum, rg_inv = (s.sb(n, [RG, 1]) for n in ("rg_nmax", "rg_sum", "rg_inv"))
            rg_e, rg_p = s.sb("rg_e", [RG, S]), s.sb("rg_p", [RG, S])
            rg_pT, rg_o = s.sb("rg_pT", [P, QT, RG]), s.sb("rg_o", [RG, D])
            rg_x = s.sb("rg_x", [REG, D])
            m_zero = s.sem("m_zero")
            (rg_step, rg_set, rg_sc, rg_max, rg_exp, rg_prob, rg_tr, rg_read, rg_pv, rg_cut, rg_sum_ps, rg_mix) = (
                s.sem(n) for n in ("rg_step", "rg_set", "rg_sc", "rg_max", "rg_exp", "rg_prob", "rg_tr", "rg_read",
                                   "rg_pv", "rg_cut", "rg_sum_ps", "rg_mix"))

        bqs = s.sb("bqs", [P, DC]) if "bq" in Bc else None
        obias = s.sb("obias", [P, D]) if "bo" in Br else None
        bank = [s.ps(f"bank{g}", [P, 512]) for g in range(4)]
        psT = [s.ps(f"psT{i}", [P, 2, 2, P]) for i in range(2)]
        psO = s.ps("psO", [P, 512])
        psX = s.ps("psX", [P, 512])

        q_set = s.sem("q_set")
        cast_0, rest_set, cast_1, split = (s.sem(n) for n in ("cast_0", "rest_set", "cast_1", "split"))
        parts_out, stack_in = s.sem("parts_out"), [s.sem(f"stack_in{p}") for p in range(2)]
        n_in = 2 * len(PAIRS_OF_PARTS)
        w_in, x_norm = s.sem("w_in"), s.sem("x_norm")
        kv_in = [s.sem(f"kv_in{p}") for p in range(2)]
        m_in = [s.sem(f"m_in{p}") for p in range(2)]
        m_cap, raw_set, kept_set = s.sem("m_cap"), s.sem("raw_set"), s.sem("kept_set")
        xT_ps, q_ps, k_ps, v_ps = (s.sem(n) for n in ("xT_ps", "q_ps", "k_ps", "v_ps"))
        xT_ev, q_ev, k_ev, v_ev = (s.sem(n) for n in ("xT_ev", "q_ev", "k_ev", "v_ev"))
        kt_set = s.sem("kt_set")
        qs_ps, ks_ps, qs_ev, ks_ev, rot_step = (s.sem(n) for n in ("qs_ps", "ks_ps", "qs_ev", "ks_ev", "rot_step"))
        sc_done, max_done, exp_done, tr_done, pT_done, pv_done = (
            s.sem(n) for n in ("sc_done", "max_done", "exp_done", "tr_done", "pT_done", "pv_done"))
        bqs_set, on_half = s.sem("bqs_set"), s.sem("on_half")
        picked, pick_step = s.sem("picked"), s.sem("pick_step")
        capped, marked, rest_done, sum_done = s.sem("capped"), s.sem("marked"), s.sem("rest_done"), s.sem("sum_done")
        prob_done = exp_done if topk is None else picked
        inv_done, on_done, ot_done, oT_done, out_ps, out_b, x_done = (
            s.sem(n) for n in ("inv_done", "on_done", "ot_done", "oT_done", "out_ps", "out_b", "x_done"))
        n_w = len(W) + len(Bc) + len(Br) + (2 if rope is not None else 0) + (4 if groups is not None else 0)
        bank_free = raw_set if topk is not None else exp_done
        block = s.block()

        @block.sync
        def _(sp):
            for n, t in W.items():
                sp.dma_start(t[:], w[n].rearrange("(c p) n -> p c n", p=P)).then_inc(w_in, 16)
            for n, t in list(Bc.items()) + list(Br.items()):
                sp.dma_start(t[:], w[n]).then_inc(w_in, 16)
            if groups is not None:
                for n, t in (("sel", rg_sel), ("own", rg_own), ("fold", rg_fold), ("one", rg_one)):
                    sp.dma_start(t[:], w[n]).then_inc(w_in, 16)
            if rope is not None:
                sp.dma_start(cosT[:], rope[0]).then_inc(w_in, 16)
                sp.dma_start(sinT[:], rope[1]).then_inc(w_in, 16)

            def load(b, p, reuse):
                if ctxT is not None:
                    if reuse:
                        sp.wait_ge(v_ps if rope is None else ks_ps, b - 1)
                    sp.dma_start(kvT[:, p, :, :], ctxT[:, :, bass.ds(b * S, S)].rearrange("c p n -> p c n"))\
                        .then_inc(kv_in[p], 16)
                if topk is not None:
                    if reuse:
                        sp.wait_ge(m_cap, b - 1)
                    sp.dma_start(mraw[:, p, :, :], topk[bass.ds(b * QT, QT), :, :].rearrange("q p n -> p q n"))\
                        .then_inc(m_in[p], 16)

                if groups is not None:
                    if reuse:
                        sp.wait_ge(sc_done, STEPS * (b - 1))
                        sp.wait_ge(rg_sc, b - 1)
                    else:
                        sp.wait_ge(m_zero, 2)
                    for dst, row in ((mq, 0), (mk, 2)):
                        sp.dma_start(dst[0:2, p, :], groups[row:row + 2, bass.ds(b * S, S)]).then_inc(m_in[p], 16)

            def spread(b, p):
                sp.wait_ge(split, 2 * (b + 1))
                for t in range(2):
                    sp.dma_start(parts_at[p, t].rearrange("m (c r) n -> r m c n", r=P), part[:, t, :, :, :])\
                        .then_inc(parts_out, 16)
                sp.wait_ge(parts_out, 32 * (b + 1))
                for row, of in enumerate(PAIRS_OF_PARTS):
                    for t in range(2):
                        sp.dma_start(stack[DK * row:DK * row + DK, p, t, :, :],
                                     parts_at[p, t, of[1 - t]].rearrange("(h d) n -> d h n", d=DK)).then_inc(stack_in[p], 16)

            load(0, 0, False)
            load(1, 1, False)
            spread(0, 0)
            spread(1, 1)
            with sp.Fori(1, B // 2) as i:
                for k in range(2):
                    load(i * 2 + k, k, True)
                    spread(i * 2 + k, k)

        @block.tensor
        def _(pe):
            def product(out, lhs, rhs):
                for c in range(DC):
                    mm = nc.tensor.matmul(out, lhs[c], rhs[c], start=(c == 0), stop=(c == DC - 1))
                return mm

            def project(b, p, pair, again, reuse):
                pe.wait_ge(x_norm, b + 1)
                if reuse:
                    pe.wait_ge(bank_free, STEPS * (b - 1))
                if again:
                    pe.wait_ge(xT_ev, b)
                    if rope is not None:
                        pe.wait_ge(qs_ev, b)
                for c in range(DC):
                    for t in range(QT):
                        mm = nc.tensor.transpose(bank[0][:, c * S + t * P:c * S + t * P + P],
                                                 xn[:, p, t, c * P:c * P + P], ident[:])
                mm.then_inc(xT_ps, 1)
                if again:
                    pe.wait_ge(q_ev if rope is not None else q_set, b)
                    pe.wait_ge(k_ev, b)
                    pe.wait_ge(v_ev, b)
                    if rope is not None:
                        pe.wait_ge(ks_ev, b)
                if ctxT is not None:
                    pe.wait_ge(kv_in[p], (pair + 1) * 16)
                else:
                    pe.wait_ge(xT_ev, b + 1)
                for o in range(DC):
                    mm = product(bank[2][:, o * S:o * S + S], [W["wk"][:, c, o * P:o * P + P] for c in range(DC)],
                                 [kvT[:, p, c, :] for c in range(DC)])
                mm.then_inc(k_ps, 1)
                for t in range(QT):
                    mm = product(bank[3][:, t * D:t * D + D], [kvT[:, p, c, t * P:t * P + P] for c in range(DC)],
                                 [W["wv"][:, c, :] for c in range(DC)])
                mm.then_inc(v_ps, 1)
                pe.wait_ge(xT_ev, b + 1)
                for o in range(DC):
                    mm = product(bank[1][:, o * S:o * S + S], [W["wq"][:, c, o * P:o * P + P] for c in range(DC)],
                                 [xnT[:, p, c, :] for c in range(DC)])
                mm.then_inc(q_ps, 1)
                if rope is not None:
                    for o in range(DC):
                        mm = product(bank[0][:, o * S:o * S + S],
                                     [W["wq_swap"][:, c, o * P:o * P + P] for c in range(DC)],
                                     [xnT[:, p, c, :] for c in range(DC)])
                    mm.then_inc(qs_ps, 1)
                    pe.wait_ge(k_ev, b + 1)
                    for o in range(DC):
                        mm = product(bank[2][:, o * S:o * S + S],
                                     [W["wk_swap"][:, c, o * P:o * P + P] for c in range(DC)],
                                     [kvT[:, p, c, :] for c in range(DC)])
                    mm.then_inc(ks_ps, 1)

            def score(b, p, pair, n, last):
                qt, h0, g = n // PER_QT, n % PER_QT * 2, n % 4
                if n == 0:
                    pe.wait_ge(stack_in[p], 16 * n_in * (pair + 1))
                    if rope is None:
                        pe.wait_ge(q_set, b + (1 if last else 2))
                    pe.wait_ge(k_ev, b + (1 if last else 2))
                    pe.wait_ge(v_ev, b + (1 if last else 2))
                    pe.wait_ge(xT_ev, b + (1 if last else 2))
                    if rope is not None:
                        pe.wait_ge(qs_ev, b + (1 if last else 2))
                        pe.wait_ge(kt_set, b + (1 if last else 2))
                if n == 0 and groups is not None:
                    pe.wait_ge(m_in[p], 16 * 2 * (pair + 1))
                if n >= 4 or last:
                    pe.wait_ge(bank_free, STEPS * b + n - 3)
                for e in range(2):
                    mm = nc.tensor.matmul(bank[g][:, e * S:e * S + S], stack[:, p, 1, h0 + e, qt * P:qt * P + P],
                                          stack[:, p, 0, h0 + e, :], start=True, stop=(groups is None))
                    if groups is not None:
                        mm = nc.tensor.matmul(bank[g][:, e * S:e * S + S], mq[:, p, qt * P:qt * P + P], mk[:, p, :],
                                              start=False, stop=True)
                mm.then_inc(sc_done, 1)

            def transposes(b, p, n):
                pe.wait_ge(prob_done, STEPS * b + n + 1)
                if n >= 2:
                    pe.wait_ge(pT_done, STEPS * b + n - 1)
                for kc in range(2):
                    for e in range(2):
                        mm = nc.tensor.transpose(psT[n % 2][:, kc, e, :], prob[:, n % 4, e, kc * P:kc * P + P],
                                                 ident[:])
                mm.then_inc(tr_done, 1)

            def values(b, p, n):
                qt, h0 = n // PER_QT, n % PER_QT * 2
                pe.wait_ge(pT_done, STEPS * b + n + 1)
                if n == PER_QT:
                    pe.wait_ge(on_done, QT * b + 1)
                for e in range(2):
                    h = h0 + e
                    for kc in range(2):
                        mm = nc.tensor.matmul(psO[:, h * DK:h * DK + DK], probT[:, n % 2, kc, e, :],
                                              v[:, p, kc, h * DK:h * DK + DK], start=(kc == 0), stop=(kc == 1))
                mm.then_inc(pv_done, 1)

            def registers_pe(b, p, n):
                if n == 1:
                    pe.wait_ge(rg_set, b + 1)
                    for c in range(DC):
                        nc.tensor.matmul(psX[0:RG, 0:S], rg_q[:, c, :, :].rearrange("p h r -> p (h r)"), kT[:, p, c, :],
                                         start=(c == 0), stop=False)
                    nc.tensor.matmul(psX[0:RG, 0:S], rg_two[:], mk[0:2, p, :], start=False, stop=True).then_inc(rg_sc, 1)
                if n == 4:
                    pe.wait_ge(rg_prob, b + 1)
                    for kc in range(QT):
                        mm = nc.tensor.transpose(psX[:, D + kc * RG:D + kc * RG + RG], rg_p[:, kc * P:kc * P + P],
                                                 ident[0:RG, 0:RG])
                    mm.then_inc(rg_tr, 1)
                if n == 6:
                    pe.wait_ge(rg_read, b + 1)
                    for kc in range(QT):
                        mm = nc.tensor.matmul(psX[0:RG, 0:D], rg_pT[:, kc, :], v[:, p, kc, :], start=(kc == 0), stop=(kc == 1))
                    mm.then_inc(rg_pv, 1)
                if n == 8:
                    pe.wait_ge(rg_cut, b + 1)
                    nc.tensor.matmul(psX[0:REG, D:2 * D], rg_fold[:], rg_o[:], start=True, stop=True).then_inc(rg_sum_ps, 1)

            def out_transposes(b, qt):
                pe.wait_ge(on_done, QT * b + qt + 1)
                if qt:
                    pe.wait_ge(x_done, QT * b + 1)
                for c in range(DC):
                    mm = nc.tensor.transpose(psX[:, c * P:c * P + P],
                                             on[:, qt, c * 8:c * 8 + 8, :].rearrange("p h d -> p (h d)"), ident[:])
                mm.then_inc(ot_done, 1)

            def out_project(b, qt):
                pe.wait_ge(oT_done, QT * b + qt + 1)
                product(psX[:, D:2 * D], [oT[:, c, :] for c in range(DC)],
                        [W["wo"][:, c, :] for c in range(DC)]).then_inc(out_ps, 1)

            def attend(b, p, pair, last=False):
                for n in range(STEPS + 3):
                    if n < STEPS:
                        score(b, p, pair, n, last)
                    if 2 <= n < STEPS + 2:
                        transposes(b, p, n - 2)
                    if n >= 3:
                        values(b, p, n - 3)
                    if groups is not None:
                        registers_pe(b, p, n)
                    if n == 12:
                        out_transposes(b, 0)
                    if n == 14:
                        out_project(b, 0)

            def finish(b):
                out_transposes(b, 1)
                out_project(b, 1)

            pe.wait_ge(w_in, 16 * n_w)
            if groups is not None:
                pe.wait_ge(rg_mix, 1)
            project(0, 0, 0, False, False)
            project(1, 1, 0, True, False)
            with pe.Fori(0, B // 2 - 1) as i:
                for k in range(2):
                    attend(i * 2 + k, k, i)
                    project(i * 2 + k + 2, k, i + 1, True, True)
                    finish(i * 2 + k)
            attend(B - 2, 0, B // 2 - 1)
            finish(B - 2)
            attend(B - 1, 1, B // 2 - 1, True)
            finish(B - 1)

        @block.gpsimd
        def _(pool):
            def whole(p, t):
                return (kT, qf)[t][:, p, :, :]

            def keep_rest(b, p, t):
                pool.wait_ge(cast_0, 2 * b + t + 1)
                nc.gpsimd.tensor_tensor(rest_of[:, t, :, :], whole(p, t), part[:, t, 0, :, :], ALU.subtract)\
                    .then_inc(rest_set, 1)

            def last_part(b, t):
                pool.wait_ge(cast_1, 2 * b + t + 1)
                nc.gpsimd.tensor_tensor(part[:, t, 2, :, :], rest_of[:, t, :, :], part[:, t, 1, :, :],
                                        ALU.subtract).then_inc(split, 1)

            def split_parts(b, p, step):
                if step in KEEP_AT:
                    keep_rest(b, p, KEEP_AT.index(step))
                if step in LAST_AT:
                    last_part(b, LAST_AT.index(step))

            def cap_scores(b, p, n):
                qt = n // PER_QT
                if n == 0:
                    pool.wait_ge(m_cap, b + 1)
                pool.wait_ge(capped, STEPS * b + n)
                pool.wait_ge(raw_set, STEPS * b + n + 1)
                nc.gpsimd.tensor_tensor(kept[:], raw_sc[:, n % 2, :, :],
                                        mone[:, p, qt, :].unsqueeze(1).to_broadcast([P, 2, S]), ALU.mult)\
                    .then_inc(kept_set, 1)
                pool.wait_ge(kept_set, STEPS * b + n + 1)
                if n >= 2:
                    pool.wait_ge(exp_done, STEPS * b + n - 1)
                    pool.wait_ge(marked, STEPS * b + n - 1)
                nc.gpsimd.tensor_tensor(sc_sb[:, n % 2, :, :], kept[:],
                                        mlow[:, p, qt, :].unsqueeze(1).to_broadcast([P, 2, S]), ALU.add)\
                    .then_inc(capped, 1)

            def pick(b, n):
                pool.wait_ge(rest_done, STEPS * b + n + 1)
                if n >= 4:
                    pool.wait_ge(tr_done, STEPS * b + n - 3)
                nc.gpsimd.tensor_tensor(prob[:, n % 4, :, :], expd[:, n % 2, :, :], rest[:, n % 2, :, :],
                                        ALU.subtract).then_inc(picked, 1)

            def attend(b, p, following=True):
                for n in range(STEPS + 1):
                    if topk is not None and n < STEPS:
                        cap_scores(b, p, n)
                    if following:
                        split_parts(b + 1, 1 - p, n)
                    if topk is not None and n >= 1:
                        pick(b, n - 1)

            if groups is not None:
                for m in (mq, mk):
                    nc.gpsimd.memset(m[:], 0.0).then_inc(m_zero, 1)
            for n in range(STEPS):
                split_parts(0, 0, n)
            with pool.Fori(0, B // 2 - 1) as i:
                for k in range(2):
                    attend(i * 2 + k, k)
            attend(B - 2, 0)
            attend(B - 1, 1, False)

        @block.scalar
        def _(act):
            def read_q(b, p):
                if rope is not None:
                    return
                act.wait_ge(q_ps, b + 1)
                for c in range(DC):
                    if "bq" in Bc:
                        last = nc.scalar.activation(qf[:, p, c, :], bank[1][:, c * S:c * S + S], ACT.Identity,
                                                    bias=bqs[:, c:c + 1], scale=scale)
                    else:
                        last = nc.scalar.activation(qf[:, p, c, :], bank[1][:, c * S:c * S + S], ACT.Copy, scale=scale)
                last.then_inc(q_set, 1)

            def split_parts(b, p, step):
                for t, at in enumerate(FIRST_AT):
                    if step == at:
                        act.wait_ge((k_ev if rope is None else kt_set, q_set if rope is None else rot_step)[t], b + 1)
                        act.wait_ge(parts_out, 32 * b)
                        nc.scalar.activation(part[:, t, 0, :, :], (kT, qf)[t][:, p, :, :], ACT.Copy).then_inc(cast_0, 1)
                for t, at in enumerate(SECOND_AT):
                    if step == at:
                        act.wait_ge(rest_set, 2 * b + t + 1)
                        nc.scalar.activation(part[:, t, 1, :, :], rest_of[:, t, :, :], ACT.Copy).then_inc(cast_1, 1)

            def copy_transposes(b, n):
                act.wait_ge(tr_done, STEPS * b + n + 1)
                if n >= 2:
                    act.wait_ge(pv_done, STEPS * b + n - 1)
                nc.scalar.activation(probT[:, n % 2, :, :, :].rearrange("p k e q -> p (k e q)"),
                                     psT[n % 2][:].rearrange("p k e q -> p (k e q)"), ACT.Copy).then_inc(pT_done, 1)

            def copy_scores(b, n):
                act.wait_ge(sc_done, STEPS * b + n + 1)
                if n >= 2:
                    act.wait_ge(kept_set, STEPS * b + n - 1)
                nc.scalar.activation(raw_sc[:, n % 2, :, :].rearrange("p e k -> p (e k)"), bank[n % 4][:], ACT.Copy)\
                    .then_inc(raw_set, 1)

            def attend(b, p, following=True):
                if topk is not None:
                    copy_scores(b, 0)
                for n in range(STEPS):
                    if following:
                        split_parts(b + 1, 1 - p, n)
                    qt, h0 = n // PER_QT, n % PER_QT * 2
                    if topk is not None and n + 1 < STEPS:
                        copy_scores(b, n + 1)
                    act.wait_ge(max_done, STEPS * b + n + 1)
                    if topk is not None:
                        if n >= 2:
                            act.wait_ge(picked, STEPS * b + n - 1)
                        for e in range(2):
                            h = h0 + e
                            last = nc.scalar.activation(expd[:, n % 2, e, :], sc_sb[:, n % 2, e, :], ACT.Exp,
                                                        bias=nmax[:, qt, h:h + 1])
                        last.then_inc(exp_done, 1)
                        if n >= 2:
                            copy_transposes(b, n - 2)
                        act.wait_ge(marked, STEPS * b + n + 1)
                        for e in range(2):
                            h = h0 + e
                            last = nc.scalar.activation(rest[:, n % 2, e, :], left[:, n % 2, e, :], ACT.Exp,
                                                        bias=nmax[:, qt, h:h + 1])
                        last.then_inc(rest_done, 1)
                        act.wait_ge(sum_done, STEPS * b + n)
                        for e in range(2):
                            h = h0 + e
                            last = nc.scalar.activation(top_exp[:, e, :], top8[:, n % 2, e, :], ACT.Exp,
                                                        bias=nmax[:, qt, h:h + 1], accum_out=rsum[:, p, qt, h:h + 1])
                        last.then_inc(sum_done, 1)
                        continue
                    if n >= 4:
                        act.wait_ge(tr_done, STEPS * b + n - 3)
                    for e in range(2):
                        h = h0 + e
                        last = nc.scalar.activation(prob[:, n % 4, e, :], bank[n % 4][:, e * S:e * S + S], ACT.Exp,
                                                    bias=nmax[:, qt, h:h + 1], accum_out=rsum[:, p, qt, h:h + 1])
                    last.then_inc(exp_done, 1)
                    if groups is not None and n == 1:
                        act.wait_ge(rg_max, b + 1)
                        nc.scalar.activation(rg_e[:], psX[0:RG, 0:S], ACT.Exp, bias=rg_nmax[:, 0:1],
                                             accum_out=rg_sum[:, 0:1]).then_inc(rg_exp, 1)
                if topk is not None:
                    copy_transposes(b, STEPS - 2)
                    copy_transposes(b, STEPS - 1)

            if "bq" in Bc:
                act.wait_ge(w_in, 16 * n_w)
                nc.scalar.activation(bqs[:], Bc["bq"][:], ACT.Copy, scale=scale).then_inc(bqs_set, 1)
                act.wait_ge(bqs_set, 1)
            read_q(0, 0)
            for n in range(STEPS):
                split_parts(0, 0, n)
            read_q(1, 1)
            with act.Fori(0, B // 2 - 1) as i:
                for k in range(2):
                    attend(i * 2 + k, k)
                    read_q(i * 2 + k + 2, k)
            attend(B - 2, 0)
            attend(B - 1, 1, False)

        @block.vector
        def _(dve):
            def read_mask(b, p, pair):
                if topk is None:
                    return
                dve.wait_ge(m_in[p], 16 * (pair + 1))
                raw, one, low = (a[:, p, :, :].rearrange("p q n -> p (q n)") for a in (mraw, mone, mlow))
                nc.vector.tensor_scalar(low, raw, 0.0, NEG, ALU.is_equal, ALU.mult)
                nc.vector.tensor_scalar(one, raw, 0.0, 1.0, ALU.not_equal, ALU.mult).then_inc(m_cap, 1)

            def normalise(b, p, reuse):
                if reuse:
                    dve.wait_ge(xT_ps, b - 1)
                for t in range(QT):
                    last = nc.vector.tensor_scalar(xn[:, p, t, :], x[:, b * QT + t, :], mean[:, bass.ds(b * QT + t, 1)],
                                                   rstd[:, bass.ds(b * QT + t, 1)], ALU.subtract, ALU.mult)
                last.then_inc(x_norm, 1)

            def read_projections(b, p, reuse):
                dve.wait_ge(xT_ps, b + 1)
                if reuse:
                    dve.wait_ge(q_ps if rope is None else qs_ps, b - 1)
                nc.vector.tensor_copy(xnT[:, p, :, :].rearrange("p c n -> p (c n)"), bank[0][:]).then_inc(xT_ev, 1)
                dve.wait_ge(k_ps, b + 1)
                if rope is not None:
                    turn_and_read(b, p, reuse)
                    return
                if reuse:
                    dve.wait_ge(sc_done, STEPS * (b - 1))
                for c in range(DC):
                    if "bk" in Bc:
                        last = nc.vector.tensor_scalar(kT[:, p, c, :], bank[2][:, c * S:c * S + S],
                                                       Bc["bk"][:, c:c + 1], None, ALU.add)
                    else:
                        last = nc.vector.tensor_copy(kT[:, p, c, :], bank[2][:, c * S:c * S + S])
                last.then_inc(k_ev, 1)
                dve.wait_ge(v_ps, b + 1)
                if reuse:
                    dve.wait_ge(pv_done, STEPS * (b - 1))
                for t in range(QT):
                    if "bv" in Br:
                        last = nc.vector.tensor_tensor(v[:, p, t, :], bank[3][:, t * D:t * D + D], Br["bv"][:], ALU.add)
                    else:
                        last = nc.vector.tensor_copy(v[:, p, t, :], bank[3][:, t * D:t * D + D])
                last.then_inc(v_ev, 1)

            def turn_and_read(b, p, reuse):
                cos = cosT[:].unsqueeze(1).to_broadcast([P, DC, S])
                sin = sinT[:].unsqueeze(1).to_broadcast([P, DC, S])

                def at(k):
                    return bank[k][:].rearrange("p (c n) -> p c n", c=DC)

                dve.wait_ge(kt_set, b)
                nc.vector.tensor_tensor(krot[:, 0, :, :], at(2), cos, ALU.mult).then_inc(k_ev, 1)
                dve.wait_ge(v_ps, b + 1)
                if reuse:
                    dve.wait_ge(pv_done, STEPS * (b - 1))
                nc.vector.tensor_copy(v[:, p, :, :].rearrange("p t n -> p (t n)"), bank[3][:]).then_inc(v_ev, 1)
                dve.wait_ge(q_ps, b + 1)
                dve.wait_ge(rot_step, b)
                nc.vector.tensor_tensor(rot[:, 0, :, :], at(1), cos, ALU.mult).then_inc(q_ev, 1)
                dve.wait_ge(qs_ps, b + 1)
                nc.vector.tensor_tensor(rot[:, 1, :, :], at(0), sin, ALU.mult).then_inc(qs_ev, 1)
                dve.wait_ge(qs_ev, b + 1)
                dve.wait_ge(q_ev, b + 1)
                nc.vector.tensor_tensor(qf[:, p, :, :], rot[:, 0, :, :], rot[:, 1, :, :], ALU.add).then_inc(rot_step, 1)
                dve.wait_ge(ks_ps, b + 1)
                nc.vector.tensor_tensor(krot[:, 1, :, :], at(2), sin, ALU.mult).then_inc(ks_ev, 1)
                dve.wait_ge(ks_ev, b + 1)
                dve.wait_ge(k_ev, b + 1)
                if reuse:
                    dve.wait_ge(sc_done, STEPS * (b - 1))
                nc.vector.tensor_tensor(kT[:, p, :, :], krot[:, 0, :, :], krot[:, 1, :, :], ALU.add).then_inc(kt_set, 1)

            def mark_largest(b, p, n):
                qt, h0 = n // PER_QT, n % PER_QT * 2
                if n >= 2:
                    dve.wait_ge(sum_done, STEPS * b + n - 1)
                dve.wait_ge(capped, STEPS * b + n + 1)
                nc.vector.tensor_copy(bound[:], ident[:, 0:1]).then_inc(pick_step, 1)
                for r in range(TOPK // 8):
                    for e in range(2):
                        if r:
                            dve.wait_ge(pick_step, 4 * r + e)
                        nc.vector.max(top8[:, n % 2, e, 8 * r:8 * r + 8],
                                      sc_sb[:, n % 2, e, :] if r == 0 else left[:, n % 2, e, :]).then_inc(pick_step, 1)
                    for e in range(2):
                        dve.wait_ge(pick_step, 4 * r + 2 + e)
                        ins = nc.vector.match_replace(out=left[:, n % 2, e, :], in_to_replace=top8[:, n % 2, e, 8 * r:8 * r + 8],
                                                      in_values=sc_sb[:, n % 2, e, :] if r == 0 else left[:, n % 2, e, :],
                                                      imm_value=GONE)
                        if r < TOPK // 8 - 1:
                            ins.then_inc(pick_step, 1)
                        if r == 0 and e == 0:
                            dve.wait_ge(pick_step, 3)
                            nc.vector.tensor_scalar(nmax[:, qt, h0:h0 + 2], top8[:, n % 2, :, 0], -1.0, None, ALU.mult)\
                                .then_inc(max_done, 1)
                ins.then_inc(marked, 1)
                dve.sem_clear(pick_step)

            def row_max(b, n):
                qt, h0 = n // PER_QT, n % PER_QT * 2
                dve.wait_ge(sc_done, STEPS * b + n + 1)
                nc.vector.tensor_reduce(nmax[:, qt, h0:h0 + 2], bank[n % 4][:].rearrange("p (e k) -> p e k", e=2),
                                        AX.X, ALU.max, negate=True).then_inc(max_done, 1)

            def read_transposes(b, n):
                dve.wait_ge(tr_done, STEPS * b + n + 1)
                if n >= 2:
                    dve.wait_ge(pv_done, STEPS * b + n - 1)
                nc.vector.tensor_copy(probT[:, n % 2, :, :, :].rearrange("p k e q -> p (k e q)"),
                                      psT[n % 2][:].rearrange("p k e q -> p (k e q)")).then_inc(pT_done, 1)

            def registers_dve(b, p, n):
                if n == 0:
                    dve.wait_ge(q_set, b + 1)
                    for c in range(DC):
                        ins = nc.vector.tensor_tensor(rg_q[:, c, :, :], qf[:, p, c, 0:REG].unsqueeze(1).to_broadcast([P, H, REG]),
                                                      rg_sel[:, c, :].unsqueeze(2).to_broadcast([P, H, REG]), ALU.mult)
                    ins.then_inc(rg_set, 1)
                if n == 1:
                    dve.wait_ge(rg_sc, b + 1)
                    nc.vector.tensor_reduce(rg_nmax[:], psX[0:RG, 0:S], AX.X, ALU.max, negate=True).then_inc(rg_max, 1)
                if n == 3:
                    dve.wait_ge(rg_exp, b + 1)
                    nc.vector.reciprocal(rg_inv[:], rg_sum[:]).then_inc(rg_step, 1)
                    dve.wait_ge(rg_step, 2 * b + 1)
                    nc.vector.tensor_scalar(rg_p[:], rg_e[:], rg_inv[:, 0:1], None, ALU.mult).then_inc(rg_prob, 1)
                if n == 4:
                    dve.wait_ge(rg_tr, b + 1)
                    nc.vector.tensor_copy(rg_pT[:].rearrange("p k m -> p (k m)"), psX[:, D:D + QT * RG]).then_inc(rg_read, 1)
                if n == 6:
                    dve.wait_ge(rg_pv, b + 1)
                    nc.vector.tensor_tensor(rg_o[:], psX[0:RG, 0:D], rg_own[:], ALU.mult).then_inc(rg_cut, 1)

            def registers_mean(b):
                dve.wait_ge(on_half, b + 1)
                dve.wait_ge(rg_sum_ps, b + 1)
                rows = on[0:REG, 0, :, :].rearrange("p h d -> p (h d)")
                nc.vector.tensor_tensor(rg_x[:], psX[0:REG, D:2 * D], rows, ALU.add).then_inc(rg_step, 1)
                dve.wait_ge(rg_step, 2 * b + 2)
                nc.vector.tensor_scalar(rows, rg_x[:], 0.5, None, ALU.mult).then_inc(on_done, 1)

            def normalise_out(b, p, qt):
                dve.wait_ge(exp_done if topk is None else sum_done, STEPS * b + (qt + 1) * PER_QT)
                nc.vector.reciprocal(rinv[:, qt, :], rsum[:, p, qt, :]).then_inc(inv_done, 1)
                dve.wait_ge(inv_done, QT * b + qt + 1)
                dve.wait_ge(pv_done, STEPS * b + (qt + 1) * PER_QT)
                nc.vector.tensor_tensor(on[:, qt, :, :], psO[:, 0:D].rearrange("p (h d) -> p h d", h=H),
                                        rinv[:, qt, :].unsqueeze(2).to_broadcast([P, H, DK]), ALU.mult)\
                    .then_inc(on_done if groups is None or qt else on_half, 1)
                if groups is not None and qt == 0:
                    registers_mean(b)

            def read_out_transposes(b, qt):
                dve.wait_ge(ot_done, QT * b + qt + 1)
                nc.vector.tensor_copy(oT[:].rearrange("p c n -> p (c n)"), psX[:, 0:D]).then_inc(oT_done, 1)

            def add_out(b, qt):
                dve.wait_ge(out_ps, QT * b + qt + 1)
                xt = x[:, b * QT + qt, :]
                if "bo" in Br:
                    nc.vector.tensor_tensor(obias[:], psX[:, D:2 * D], Br["bo"][:], ALU.add).then_inc(out_b, 1)
                    dve.wait_ge(out_b, QT * b + qt + 1)
                    nc.vector.tensor_tensor(xt, obias[:], xt, ALU.add).then_inc(x_done, 1)
                else:
                    nc.vector.tensor_tensor(xt, psX[:, D:2 * D], xt, ALU.add).then_inc(x_done, 1)

            def attend(b, p):
                for n in range(STEPS + 3):
                    if n < STEPS and topk is None:
                        row_max(b, n)
                    elif n < STEPS:
                        mark_largest(b, p, n)
                    if groups is not None:
                        registers_dve(b, p, n)
                    if 2 <= n < STEPS + 2 and topk is None:
                        read_transposes(b, n - 2)
                    if n == PER_QT + 2:
                        normalise_out(b, p, 0)
                    if n == 12:
                        read_out_transposes(b, 0)
                    if n == 14:
                        add_out(b, 0)
                normalise_out(b, p, 1)

            def finish(b):
                read_out_transposes(b, 1)
                add_out(b, 1)

            dve.wait_ge(w_in, 16 * n_w)
            if groups is not None:
                nc.vector.tensor_copy(rg_two[:], rg_one[:]).then_inc(rg_mix, 1)
            normalise(0, 0, False)
            normalise(1, 1, False)
            read_mask(0, 0, 0)
            read_mask(1, 1, 0)
            read_projections(0, 0, False)
            read_projections(1, 1, False)
            with dve.Fori(0, B // 2 - 1) as i:
                for k in range(2):
                    normalise(i * 2 + k + 2, k, True)
                    attend(i * 2 + k, k)
                    read_mask(i * 2 + k + 2, k, i + 1)
                    read_projections(i * 2 + k + 2, k, True)
                    finish(i * 2 + k)
            attend(B - 2, 0)
            finish(B - 2)
            attend(B - 1, 1)
            finish(B - 1)

F = 1024
FC = F // P
E = 8
ROW_B1 = DC * F
ROW_1 = ROW_B1 + FC
ROW_B2 = FC * D
ROW_2 = ROW_B2 + D
SKIP = float(1 << 20)


def moe_blocks(k):
    n = NT * k + E - 1
    return n + n % 2


class Counted:

    def __init__(self, sem):
        self.sem, self.base = sem, 0


def moe(nc, dma, name, k_top, x, ident, rstd, mean, c, wr, br, table, slots_x, slots_y):
    NB, KT = moe_blocks(k_top), k_top * NT
    slots_x, slots_y = slots_x[0:NB * P, :], slots_y[0:NB * P, :]
    with Scope(nc, name) as o:
        slot = o.sb("slot", [P, KT], U32)
        gate = o.sb("gate", [P, k_top, NT])
        widx = o.sb("widx", [P, NB], U32)

        with Scope(nc, f"{name}_route") as s:
            wr_sb, br_sb = s.sb("wr", [P, DC, E]), s.sb("br", [P, E])
            zero = s.sb("zero", [P, 2 * D])
            xn = s.sb("xn", [P, NT, D])
            xT = s.sb("xT", [P, 2, DC, P])
            lg = s.sb("lg", [P, NT, E])
            ex = s.sb("ex", [P, NT, E])
            top = s.sb("top", [P, NT, 8])
            topi = s.sb("topi", [P, NT, 8], U32)
            idf = s.sb("idf", [P, k_top, NT])
            hot = s.sb("hot", [P, k_top, NT, E])
            tot = s.sb("tot", [P, KT, E])
            incl = s.sb("incl", [P, E, KT])
            pos = s.sb("pos", [P, E, KT])
            nb_i, nb_s = s.sb("nb_i", [P, E], I32), s.sb("nb_s", [P, E], I32)
            nb, nb_end, first = s.sb("nb", [P, E]), s.sb("nb_end", [P, E]), s.sb("first", [P, E])
            slot_f = s.sb("slot_f", [P, KT])
            ge = s.sb("ge", [P, NB, E])
            eid, same, widx_f = s.sb("eid", [P, NB]), s.sb("same", [P, NB]), s.sb("widx_f", [P, NB])
            ones = s.sb("ones", [P, KT])
            xn2 = s.sb("xn2", [P, 2, D])
            lg2 = s.sb("lg2", [P, NT, E])
            gsum = s.sb("gsum", [P, NT])
            psT = [s.ps(f"psT{i}", [P, 512]) for i in range(2)]
            psL = s.ps("psL", [P, 512])
            psR = s.ps("psR", [P, 512])
            w_in, zero_set, zeroed, x_norm, t_done, t_read, l_done = (
                s.sem(n) for n in ("w_in", "zero_set", "zeroed", "x_norm", "t_done", "t_read", "l_done"))
            step, hot_done, ranked, exp_in, exp_out = (
                s.sem(n) for n in ("step", "hot_done", "ranked", "exp_in", "exp_out"))
            scattered = dma["scattered"]
            slot_done = s.sem("slot_done")
            block = s.block()

            @block.sync
            def _(sp):
                sp.dma_start(wr_sb[:], wr.rearrange("(c p) e -> p c e", p=P)).then_inc(w_in, 16)
                sp.dma_start(br_sb[:], br).then_inc(w_in, 16)
                sp.wait_ge(zero_set, 1)
                for j in range(NB // 2):
                    sp.dma_start(slots_x[j * 2 * P:(j + 1) * 2 * P, :].rearrange("(p r) d -> p (r d)", r=2), zero[:])\
                        .then_inc(zeroed, 16)

            @block.tensor
            def _(pe):
                pe.wait_ge(w_in, 32)

                def tile_logits(t, k, again):
                    pe.wait_ge(x_norm, t + 1)
                    if again:
                        pe.wait_ge(t_read, t - 1)
                    for c_ in range(DC):
                        mm = nc.tensor.transpose(psT[k][:, c_ * P:c_ * P + P], xn2[:, k, c_ * P:c_ * P + P], ident[:])
                    mm.then_inc(t_done, 1)
                    pe.wait_ge(t_read, t + 1)
                    for c_ in range(DC):
                        mm = nc.tensor.matmul(psL[:, bass.ds(t * E, E)], xT[:, k, c_, :], wr_sb[:, c_, :],
                                              start=(c_ == 0), stop=(c_ == DC - 1))
                    mm.then_inc(l_done, 1)

                tile_logits(0, 0, False)
                tile_logits(1, 1, False)
                with pe.Fori(1, NT // 2) as i:
                    for k in range(2):
                        tile_logits(i * 2 + k, k, True)
                pe.wait_ge(hot_done, 1)
                hot_rows = hot[:].rearrange("p k t e -> p (k t e)")
                nc.tensor.matmul(psR[:, 0:KT * E], c["before"][:], hot_rows, start=True, stop=True)
                nc.tensor.matmul(psR[:, 256:256 + KT * E], c["ones"][:], hot_rows, start=True, stop=True)\
                    .then_inc(ranked, 1)

            @block.scalar
            def _(act):
                act.wait_ge(exp_in, 1)
                if k_top == 1:
                    nc.scalar.activation(ex[:], lg2[:], ACT.Exp).then_inc(exp_out, 1)
                else:
                    nc.scalar.activation(ex[:, :, 0], lg2[:, :, 0], ACT.Exp).then_inc(exp_out, 1)

            @block.gpsimd
            def _(pool):
                pool.wait_ge(slot_done, 1)
                pool.wait_ge(zeroed, 16 * (NB // 2))
                for k in range(k_top):
                    for t in range(NT):
                        pool.indirect_dma_start(
                            out=slots_x, out_offset=bass.IndirectOffsetOnAxis(ap=slot[:, k * NT + t:k * NT + t + 1], axis=0),
                            in_=xn[:, t, :], in_offset=None).then_inc(scattered.sem, 16)
                pool.wait_ge(scattered.sem, scattered.base + 16 * KT)

            @block.vector
            def _(dve):
                n_steps = [0]

                def then(ins):
                    n_steps[0] += 1
                    ins.then_inc(step, 1)
                    dve.wait_ge(step, n_steps[0])

                nc.vector.memset(zero[:], 0.0).then_inc(zero_set, 1)

                def tile(t, k, again):
                    if again:
                        dve.wait_ge(t_done, t - 1)
                    nc.vector.tensor_scalar(xn2[:, k, :], x[:, t, :], mean[:, bass.ds(t, 1)], rstd[:, bass.ds(t, 1)],
                                            ALU.subtract, ALU.mult).then_inc(x_norm, 1)
                    dve.wait_ge(t_done, t + 1)
                    if again:
                        dve.wait_ge(l_done, t - 1)
                    nc.vector.tensor_copy(xT[:, k, :, :].rearrange("p c n -> p (c n)"), psT[k][:, 0:D]).then_inc(t_read, 1)
                    nc.vector.tensor_copy(xn[:, t, :], xn2[:, k, :])

                tile(0, 0, False)
                tile(1, 1, False)
                with dve.Fori(1, NT // 2) as i:
                    for k in range(2):
                        tile(i * 2 + k, k, True)
                dve.wait_ge(l_done, NT)
                then(nc.vector.tensor_tensor(lg[:], psL[:, 0:NT * E].rearrange("p (t e) -> p t e", e=E),
                                             br_sb[:].unsqueeze(1).to_broadcast([P, NT, E]), ALU.add))
                for t in range(NT):
                    ins = nc.vector.max(top[:, t, :], lg[:, t, :])
                then(ins)
                for t in range(NT):
                    ins = nc.vector.max_index(topi[:, t, :], top[:, t, :], lg[:, t, :])
                then(ins)
                if k_top == 1:
                    nc.vector.tensor_tensor(lg2[:], lg[:], top[:, :, 0:1].to_broadcast([P, NT, E]),
                                            ALU.subtract).then_inc(exp_in, 1)
                else:
                    nc.vector.tensor_tensor(lg2[:, :, 0], top[:, :, 1], top[:, :, 0], ALU.subtract).then_inc(exp_in, 1)
                for k in range(k_top):
                    ins = nc.vector.tensor_copy(idf[:, k, :], topi[:, :, k])
                then(ins)
                for k in range(k_top):
                    ins = nc.vector.tensor_tensor(hot[:, k, :, :], c["iota"][:, 0:E].unsqueeze(1).to_broadcast([P, NT, E]),
                                                  idf[:, k, :].unsqueeze(2).to_broadcast([P, NT, E]), ALU.is_equal)
                ins.then_inc(hot_done, 1)
                then(nc.vector.memset(ones[:], 1.0))
                dve.wait_ge(exp_out, 1)
                if k_top == 1:
                    then(nc.vector.tensor_reduce(gsum[:], ex[:], AX.X, ALU.add))
                    then(nc.vector.reciprocal(gate[:, 0, :], gsum[:]))
                else:
                    then(nc.vector.tensor_scalar(gsum[:], ex[:, :, 0], 1.0, None, ALU.add))
                    then(nc.vector.reciprocal(gate[:, 0, :], gsum[:]))
                    then(nc.vector.tensor_tensor(gate[:, 1, :], gate[:, 0, :], ex[:, :, 0], ALU.mult))
                dve.wait_ge(ranked, 1)
                then(nc.vector.tensor_copy(tot[:].rearrange("p n e -> p (n e)"), psR[:, 256:256 + KT * E]))
                for e in range(E):
                    ins = nc.vector.tensor_tensor_scan(incl[:, e, :], ones[:], tot[:, :, e], 0.0, ALU.mult, ALU.add)
                then(ins)
                then(nc.vector.tensor_scalar(nb_i[:], incl[:, :, KT - 1], float(P - 1), None, ALU.add))
                then(nc.vector.tensor_single_scalar(nb_s[:], nb_i[:], 7, ALU.arith_shift_right))
                then(nc.vector.tensor_copy(nb[:], nb_s[:]))
                then(nc.vector.tensor_tensor_scan(nb_end[:], ones[:, 0:E], nb[:], 0.0, ALU.mult, ALU.add))
                then(nc.vector.tensor_tensor(first[:], nb_end[:], nb[:], ALU.subtract))
                then(nc.vector.tensor_scalar(first[:], first[:], float(P), None, ALU.mult))
                then(nc.vector.tensor_tensor(pos[:], incl[:], tot[:].rearrange("p n e -> p e n"), ALU.subtract))
                then(nc.vector.tensor_tensor(pos[:], psR[:, 0:KT * E].rearrange("p (n e) -> p e n", e=E), pos[:], ALU.add))
                then(nc.vector.tensor_tensor(pos[:], pos[:], first[:].unsqueeze(2).to_broadcast([P, E, KT]), ALU.add))
                then(nc.vector.tensor_tensor(pos[:], pos[:], hot[:].rearrange("p k t e -> p e (k t)"), ALU.mult))
                then(nc.vector.tensor_reduce(slot_f[:], pos[:].rearrange("p e n -> p n e"), AX.X, ALU.add))
                nc.vector.tensor_copy(slot[:], slot_f[:]).then_inc(slot_done, 1)
                then(nc.vector.tensor_tensor(ge[:], c["iota"][:, 0:NB].unsqueeze(2).to_broadcast([P, NB, E]),
                                             nb_end[:].unsqueeze(1).to_broadcast([P, NB, E]), ALU.is_ge))
                then(nc.vector.tensor_reduce(eid[:], ge[:], AX.X, ALU.add))
                then(nc.vector.tensor_scalar(eid[:], eid[:], float(E - 1), None, ALU.min))
                then(nc.vector.memset(same[:], 0.0))
                then(nc.vector.tensor_tensor(same[:, 2:NB], eid[:, 2:NB], eid[:, 0:NB - 2], ALU.is_equal))
                then(nc.vector.tensor_scalar(widx_f[:], eid[:], float(P), c["lane"][:, 0:1], ALU.mult, ALU.add))
                then(nc.vector.scalar_tensor_tensor(out=widx_f[:], in0=same[:], scalar=SKIP, in1=widx_f[:],
                                                    op0=ALU.mult, op1=ALU.add))
                nc.vector.tensor_copy(widx[:], widx_f[:])

        dma["scattered"].base += 16 * KT

        with Scope(nc, f"{name}_ffn") as s:
            wt1, wt2 = s.sb("wt1", [P, 2, ROW_1]), s.sb("wt2", [P, 2, ROW_2])
            idx, none = s.sb("idx", [P, 2, 2], U32), s.sb("none", [P, 1], U32)
            xs = s.sb("xs", [P, 2, D])
            xsT = s.sb("xsT", [P, 2, DC, P])
            hT = s.sb("hT", [P, 2, FC, P])
            y = s.sb("y", [P, 2, D])
            psT = s.ps("psT", [P, 512])
            psH = [s.ps(f"psH{i}", [P, 4, P]) for i in range(4)]
            psY = [s.ps(f"psY{i}", [P, 512]) for i in range(2)]
            idx_set, t_done, t_read, h_done, g_done, y_ps, y_done = (
                s.sem(n) for n in ("idx_set", "t_done", "t_read", "h_done", "g_done", "y_ps", "y_done"))
            x_in, y_out = ([s.sem(f"{n}{p}") for p in range(2)] for n in ("x_in", "y_out"))
            w1_in, w2_in = dma["fetched_w1"], dma["fetched_w2"]
            block = s.block()
            w1 = [[[wt1[:, p, c_ * F + f * P:c_ * F + f * P + P] for f in range(FC)] for c_ in range(DC)] for p in range(2)]
            w2 = [[wt2[:, p, f * D:f * D + D] for f in range(FC)] for p in range(2)]

            @block.gpsimd
            def _(pool):
                last_row = pool.to_reg(E * P - 1)

                def fetch(j, p, pair, again):
                    if again:
                        pool.wait_ge(w2_in[p].sem, w2_in[p].base + 16 * pair)
                        pool.wait_ge(w1_in[p].sem, w1_in[p].base + 16 * pair)
                        pool.wait_ge(g_done, FC * (j - 1))
                    nc.gpsimd.tensor_copy(idx[:, p, 0:1], widx[:, bass.ds(j, 1)]).then_inc(idx_set, 1)
                    pool.wait_ge(idx_set, 1)
                    pool.indirect_dma_start(out=wt1[:, p, :], out_offset=None, in_=table[0],
                                            in_offset=bass.IndirectOffsetOnAxis(ap=idx[:, p, 0:1], axis=0),
                                            bounds_check=last_row, oob_is_err=False).then_inc(w1_in[p].sem, 16)
                    if again:
                        pool.wait_ge(y_done, j - 1)
                    nc.gpsimd.tensor_tensor(idx[:, p, 1:2], idx[:, p, 0:1], none[:], ALU.add).then_inc(idx_set, 1)
                    pool.wait_ge(idx_set, 2)
                    pool.sem_clear(idx_set)
                    pool.indirect_dma_start(out=wt2[:, p, :], out_offset=None, in_=table[1],
                                            in_offset=bass.IndirectOffsetOnAxis(ap=idx[:, p, 1:2], axis=0),
                                            bounds_check=last_row, oob_is_err=False).then_inc(w2_in[p].sem, 16)

                nc.gpsimd.memset(none[:], 0).then_inc(idx_set, 1)
                pool.wait_ge(idx_set, 1)
                pool.sem_clear(idx_set)
                fetch(0, 0, 0, False)
                fetch(1, 1, 0, False)
                with pool.Fori(1, NB // 2) as i:
                    for k in range(2):
                        fetch(i * 2 + k, k, i, True)

            @block.sync
            def _(sp):
                def load(j, p, again):
                    if again:
                        sp.wait_ge(t_done, j - 1)
                    sp.dma_start(xs[:, p, :], slots_x[bass.ds(j * P, P), :]).then_inc(x_in[p], 16)

                def store(j, p):
                    sp.wait_ge(y_done, j + 1)
                    sp.dma_start(slots_y[bass.ds(j * P, P), :], y[:, p, :]).then_inc(y_out[p], 16)

                load(0, 0, False)
                load(1, 1, False)
                with sp.Fori(0, NB // 2 - 1) as i:
                    for k in range(2):
                        load(i * 2 + k + 2, k, True)
                        store(i * 2 + k, k)
                store(NB - 2, 0)
                store(NB - 1, 1)
                for k in range(2):
                    sp.wait_ge(y_out[k], 16 * (NB // 2))

            @block.tensor
            def _(pe):
                def up(j, p, pair, again):
                    pe.wait_ge(x_in[p], 16 * (pair + 1))
                    pe.wait_ge(t_read, j)
                    for c_ in range(DC):
                        mm = nc.tensor.transpose(psT[:, c_ * P:c_ * P + P], xs[:, p, c_ * P:c_ * P + P], ident[:])
                    mm.then_inc(t_done, 1)
                    pe.wait_ge(t_read, j + 1)
                    pe.wait_ge(w1_in[p].sem, w1_in[p].base + 16 * (pair + 1))
                    if again:
                        pe.wait_ge(g_done, FC * (j - 1))
                    for f in range(FC):
                        for c_ in range(DC):
                            mm = nc.tensor.matmul(psH[2 * p + f // 4][:, f % 4, :], w1[p][c_][f], xsT[:, p, c_, :],
                                                  start=(c_ == 0), stop=(c_ == DC - 1))
                        if f % 4 == 3:
                            mm.then_inc(h_done, 1)

                def down(j, p, pair, again):
                    pe.wait_ge(w2_in[p].sem, w2_in[p].base + 16 * (pair + 1))
                    if again:
                        pe.wait_ge(y_done, j - 1)
                    for f in range(FC):
                        pe.wait_ge(g_done, FC * j + f + 1)
                        mm = nc.tensor.matmul(psY[p][:, 0:D], hT[:, p, f, :], w2[p][f], start=(f == 0), stop=(f == FC - 1))
                    mm.then_inc(y_ps, 1)

                up(0, 0, 0, False)
                up(1, 1, 0, False)
                down(0, 0, 0, False)
                up(2, 0, 1, True)
                down(1, 1, 0, False)
                with pe.Fori(1, NB // 2 - 1) as i:
                    up(i * 2 + 1, 1, i, True)
                    down(i * 2, 0, i, True)
                    up(i * 2 + 2, 0, i + 1, True)
                    down(i * 2 + 1, 1, i, True)
                up(NB - 1, 1, NB // 2 - 1, True)
                down(NB - 2, 0, NB // 2 - 1, True)
                down(NB - 1, 1, NB // 2 - 1, True)

            @block.scalar
            def _(act):
                def gelu(j, p, again):
                    if again:
                        act.wait_ge(y_ps, j - 1)
                    for f in range(FC):
                        if f % 4 == 0:
                            act.wait_ge(h_done, 2 * j + f // 4 + 1)
                        nc.scalar.activation(hT[:, p, f, :], psH[2 * p + f // 4][:, f % 4, :], ACT.Gelu,
                                             bias=wt1[:, p, ROW_B1 + f:ROW_B1 + f + 1]).then_inc(g_done, 1)

                gelu(0, 0, False)
                gelu(1, 1, False)
                with act.Fori(1, NB // 2) as i:
                    for k in range(2):
                        gelu(i * 2 + k, k, True)

            @block.vector
            def _(dve):
                def read_t(j, p, again):
                    dve.wait_ge(t_done, j + 1)
                    if again:
                        dve.wait_ge(h_done, 2 * (j - 1))
                    nc.vector.tensor_copy(xsT[:, p, :, :].rearrange("p c n -> p (c n)"), psT[:, 0:D]).then_inc(t_read, 1)

                def add_b2(j, p, pair, again):
                    dve.wait_ge(y_ps, j + 1)
                    if again:
                        dve.wait_ge(y_out[p], 16 * pair)
                    nc.vector.tensor_tensor(y[:, p, :], psY[p][:, 0:D], wt2[:, p, ROW_B2:ROW_B2 + D], ALU.add)\
                        .then_inc(y_done, 1)

                read_t(0, 0, False)
                read_t(1, 1, False)
                add_b2(0, 0, 0, False)
                read_t(2, 0, True)
                add_b2(1, 1, 0, False)
                with dve.Fori(1, NB // 2 - 1) as i:
                    read_t(i * 2 + 1, 1, True)
                    add_b2(i * 2, 0, i, True)
                    read_t(i * 2 + 2, 0, True)
                    add_b2(i * 2 + 1, 1, i, True)
                read_t(NB - 1, 1, True)
                add_b2(NB - 2, 0, NB // 2 - 1, True)
                add_b2(NB - 1, 1, NB // 2 - 1, True)

        for p in range(2):
            dma["fetched_w1"][p].base += 16 * (NB // 2)
            dma["fetched_w2"][p].base += 16 * (NB // 2)

        with Scope(nc, f"{name}_back") as s:
            yb = s.sb("yb", [P, KT, D])
            back = dma["back"]
            added = s.sem("added")
            block = s.block()

            @block.gpsimd
            def _(pool):
                for t in range(NT):
                    for k in range(k_top):
                        n = k * NT + t
                        pool.indirect_dma_start(out=yb[:, n, :], out_offset=None, in_=slots_y,
                                                in_offset=bass.IndirectOffsetOnAxis(ap=slot[:, n:n + 1], axis=0))\
                            .then_inc(back[t].sem, 16)

            @block.vector
            def _(dve):
                for k in range(k_top):
                    for t in range(NT):
                        if k == 0:
                            dve.wait_ge(back[t].sem, back[t].base + 16 * k_top)
                        else:
                            dve.wait_ge(added, t + 1)
                        nc.vector.scalar_tensor_tensor(out=x[:, t, :], in0=yb[:, k * NT + t, :], scalar=gate[:, k, t:t + 1],
                                                       in1=x[:, t, :], op0=ALU.mult, op1=ALU.add).then_inc(added, 1)
        for t in range(NT):
            dma["back"][t].base += 16 * k_top


CH = 16
PAIRS = S // (2 * CH)
W1C = S + 1


def alignment(nc, x, ident, rstd, mean, consts, ctx, ctxT, dist, cost, table):
    with Scope(nc, "dtw") as o:
        ctx_sb = o.sb("ctx", [P, NT, D])
        ctx_in = o.sem("ctx_in")

        with Scope(nc, "dist") as s:
            aa = s.sb("aa", [P, NT])
            xn = s.sb("xn", [P, 2, QT, D])
            xm2, xsq = s.sb("xm2", [P, 2, DC, S]), s.sb("xsq", [P, 2, DC, S])
            aT = s.sb("aT", [P, 2, DC, S])
            d2, dd = s.sb("d2", [P, 2, QT, S]), s.sb("dd", [P, 2, QT, S])
            junk = s.sb("junk", [P, 2, D])
            psT = [s.ps(f"psT{i}", [P, 512]) for i in range(2)]
            psD = [s.ps(f"psD{i}", [P, 512]) for i in range(2)]
            a_in, d_out = ([s.sem(f"{n}{p}") for p in range(2)] for n in ("a_in", "d_out"))
            x_norm, t_done, m2_done, sq_done, d_ps, d2_done, dd_done, aa_done = (
                s.sem(n) for n in ("x_norm", "t_done", "m2_done", "sq_done", "d_ps", "d2_done", "dd_done", "aa_done"))
            block = s.block()

            @block.sync
            def _(sp):
                sp.dma_start(ctx_sb[:], ctx.rearrange("b (t p) d -> p (b t) d", p=P)).then_inc(ctx_in, 16)

                def load(b, p, again):
                    if again:
                        sp.wait_ge(d_ps, b - 1)
                    sp.dma_start(aT[:, p, :, :], ctxT[:, :, bass.ds(b * S, S)].rearrange("c p n -> p c n"))\
                        .then_inc(a_in[p], 16)

                def store(b, p):
                    sp.wait_ge(dd_done, b + 1)
                    sp.dma_start(dist[bass.ds(b, 1), :, :].rearrange("b (t p) j -> p (b t) j", p=P), dd[:, p, :, :])\
                        .then_inc(d_out[p], 16)

                load(0, 0, False)
                load(1, 1, False)
                with sp.Fori(0, B // 2 - 1) as i:
                    for k in range(2):
                        load(i * 2 + k + 2, k, True)
                        store(i * 2 + k, k)
                store(B - 2, 0)
                store(B - 1, 1)
                for k in range(2):
                    sp.wait_ge(d_out[k], 16 * (B // 2))
                sp.wait_ge(ctx_in, 16)

            @block.tensor
            def _(pe):
                def batch(b, p, pair, again):
                    pe.wait_ge(x_norm, b + 1)
                    if again:
                        pe.wait_ge(sq_done, b - 1)
                    for c in range(DC):
                        for t in range(QT):
                            mm = nc.tensor.transpose(psT[p][:, c * S + t * P:c * S + t * P + P],
                                                     xn[:, p, t, c * P:c * P + P], ident[:])
                    mm.then_inc(t_done, 1)
                    pe.wait_ge(a_in[p], 16 * (pair + 1))
                    pe.wait_ge(m2_done, b + 1)
                    pe.wait_ge(sq_done, b + 1)
                    if again:
                        pe.wait_ge(d2_done, b - 1)
                    for t in range(QT):
                        out = psD[p][:, t * S:t * S + S]
                        for c in range(DC):
                            nc.tensor.matmul(out, aT[:, p, c, t * P:t * P + P], xm2[:, p, c, :], start=(c == 0), stop=False)
                        for c in range(DC):
                            mm = nc.tensor.matmul(out, consts["ones"][:], xsq[:, p, c, :], start=False, stop=(c == DC - 1))
                    mm.then_inc(d_ps, 1)

                batch(0, 0, 0, False)
                batch(1, 1, 0, False)
                with pe.Fori(1, B // 2) as i:
                    for k in range(2):
                        batch(i * 2 + k, k, i, True)

            @block.scalar
            def _(act):
                act.wait_ge(ctx_in, 16)
                for t in range(NT):
                    if t >= 2:
                        act.wait_ge(aa_done, t - 1)
                    nc.scalar.activation(junk[:, t % 2, :], ctx_sb[:, t, :], ACT.Square,
                                         accum_out=aa[:, t:t + 1]).then_inc(aa_done, 1)

                def batch(b, p, pair):
                    act.wait_ge(t_done, b + 1)
                    act.wait_ge(m2_done, b + 1)
                    nc.scalar.activation(xsq[:, p, :, :].rearrange("p c n -> p (c n)"), psT[p][:], ACT.Square)\
                        .then_inc(sq_done, 1)
                    act.wait_ge(d2_done, b + 1)
                    act.wait_ge(d_out[p], 16 * pair)
                    nc.scalar.activation(dd[:, p, :, :], d2[:, p, :, :], ACT.Sqrt).then_inc(dd_done, 1)

                batch(0, 0, 0)
                batch(1, 1, 0)
                with act.Fori(1, B // 2) as i:
                    for k in range(2):
                        batch(i * 2 + k, k, i)

            @block.vector
            def _(dve):
                def normalise(b, p):
                    for t in range(QT):
                        ins = nc.vector.tensor_scalar(xn[:, p, t, :], x[:, b * QT + t, :], mean[:, bass.ds(b * QT + t, 1)],
                                                      rstd[:, bass.ds(b * QT + t, 1)], ALU.subtract, ALU.mult)
                    ins.then_inc(x_norm, 1)

                def batch(b, p, again):
                    dve.wait_ge(t_done, b + 1)
                    if again:
                        dve.wait_ge(d_ps, b - 1)
                    nc.vector.tensor_scalar(xm2[:, p, :, :].rearrange("p c n -> p (c n)"), psT[p][:], -2.0, None,
                                            ALU.mult).then_inc(m2_done, 1)
                    dve.wait_ge(d_ps, b + 1)
                    if again:
                        dve.wait_ge(dd_done, b - 1)
                    for t in range(QT):
                        ins = nc.vector.tensor_scalar(d2[:, p, t, :], psD[p][:, t * S:t * S + S],
                                                      aa[:, bass.ds(b * QT + t, 1)], 0.0, ALU.add, ALU.max)
                    ins.then_inc(d2_done, 1)

                dve.wait_ge(aa_done, NT)
                normalise(0, 0)
                normalise(1, 1)
                batch(0, 0, False)
                batch(1, 1, False)
                with dve.Fori(1, B // 2) as i:
                    for k in range(2):
                        normalise(i * 2 + k, k)
                        batch(i * 2 + k, k, True)

        with Scope(nc, "cost") as s:
            drow = s.sb("drow", [B, 2, CH, S])
            r = s.sb("r", [B, 2 * CH + 1, W1C])
            near = s.sb("near", [B, 2, S])
            edge = s.sb("edge", [B, W1C])
            d_in, r_out = ([s.sem(f"{n}{p}") for p in range(2)] for n in ("d_in", "r_out"))
            step, edge_out, edge_set = s.sem("step"), s.sem("edge_out"), s.sem("edge_set")
            per_round = 2 * 2 * CH + 1
            block = s.block()

            @block.sync
            def _(sp):
                sp.wait_ge(edge_set, 1)
                sp.dma_start(cost[:, 0, :], edge[:]).then_inc(edge_out, 16)

                def load(i, k):
                    sp.dma_start(drow[:, k, :, :], dist[:, bass.ds((i * 2 + k) * CH, CH), :]).then_inc(d_in[k], 16)

                def store(i, k):
                    sp.wait_ge(step, per_round * i + 2 * CH * (k + 1))
                    sp.dma_start(cost[:, bass.ds((i * 2 + k) * CH + 1, CH), :], r[:, 1 + k * CH:1 + (k + 1) * CH, :])\
                        .then_inc(r_out[k], 16)

                load(0, 0)
                load(0, 1)
                with sp.Fori(0, PAIRS - 1) as i:
                    for k in range(2):
                        store(i, k)
                        sp.wait_ge(r_out[k], 16 * (i + 1))
                        load(i + 1, k)
                store(PAIRS - 1, 0)
                store(PAIRS - 1, 1)
                for k in range(2):
                    sp.wait_ge(r_out[k], 16 * PAIRS)
                sp.wait_ge(edge_out, 16)

            @block.vector
            def _(dve):
                nc.vector.memset(edge[:], BIG).then_inc(edge_set, 1)
                nc.vector.memset(r[:], BIG).then_inc(edge_set, 1)
                dve.wait_ge(edge_set, 2)
                nc.vector.memset(r[:, 0, 0:1], 0.0).then_inc(edge_set, 1)
                dve.wait_ge(edge_set, 3)
                with dve.Fori(0, PAIRS) as i:
                    for n in range(2 * CH):
                        k = n // CH
                        if n % CH == 0:
                            dve.wait_ge(d_in[k], 16 * (i + 1))
                        nc.vector.tensor_tensor(near[:, n % 2, :], r[:, n, 1:W1C], r[:, n, 0:S], ALU.min)\
                            .then_inc(step, 1)
                        dve.wait_ge(step, per_round * i + 2 * n + 1)
                        nc.vector.tensor_tensor_scan(r[:, n + 1, 1:W1C], near[:, n % 2, :], drow[:, k, n % CH, :], BIG,
                                                     ALU.min, ALU.add).then_inc(step, 1)
                        dve.wait_ge(step, per_round * i + 2 * n + 2)
                    nc.vector.tensor_copy(r[:, 0, :], r[:, 2 * CH, :]).then_inc(step, 1)
                    dve.wait_ge(step, per_round * (i + 1))

        with Scope(nc, "path") as o2:
            start = o2.sb("start", [P, QT, B, S])
            ends = o2.sb("ends", [B, S])
            NB8 = B * S

            with Scope(nc, "back") as s:
                here, up = s.sb("here", [P, B, W1C]), s.sb("up", [P, B, W1C])
                best, left = s.sb("best", [P, B, S]), s.sb("left", [P, B, S])
                stay, where = s.sb("stay", [P, B, S]), s.sb("where", [P, B, S])
                tab = s.sb("tab", [P, QT, B, S], BF16)
                r_in, t_out, step = s.sem("r_in"), s.sem("t_out"), s.sem("step")
                block = s.block()

                @block.sync
                def _(sp):
                    for q in range(QT):
                        if q:
                            sp.wait_ge(step, 9 * q)
                        sp.dma_start(here[:], cost[:, 1 + q * P:1 + q * P + P, :].rearrange("b p j -> p b j")).then_inc(r_in, 16)
                        sp.dma_start(up[:], cost[:, q * P:q * P + P, :].rearrange("b p j -> p b j")).then_inc(r_in, 16)
                    sp.wait_ge(step, 9 * QT)
                    for q in range(QT):
                        sp.dma_start(table[:, q * P:q * P + P, :].rearrange("b p j -> p b j"), tab[:, q, :, :]).then_inc(t_out, 16)
                    sp.wait_ge(t_out, 16 * QT)

                @block.vector
                def _(dve):
                    n = [0]

                    def then(ins):
                        n[0] += 1
                        ins.then_inc(step, 1)
                        dve.wait_ge(step, n[0])

                    def flat(t):
                        return t.rearrange("p b j -> p (b j)")

                    iota = consts["iota"][:].unsqueeze(1).to_broadcast([P, B, S])
                    for q in range(QT):
                        dve.wait_ge(r_in, 32 * (q + 1))
                        diag, above, before = up[:, :, 0:S], up[:, :, 1:W1C], here[:, :, 0:S]
                        then(nc.vector.tensor_tensor(best[:], diag, above, ALU.min))
                        then(nc.vector.tensor_tensor(left[:], best[:], before, ALU.is_gt))
                        then(nc.vector.tensor_scalar(flat(stay[:]), flat(left[:]), -1.0, 1.0, ALU.mult, ALU.add))
                        then(nc.vector.tensor_tensor(where[:], stay[:], iota, ALU.mult))
                        then(nc.vector.tensor_tensor_scan(flat(start[:, q, :, :]), flat(left[:]), flat(where[:]), 0.0,
                                                          ALU.mult, ALU.add))
                        then(nc.vector.tensor_tensor(best[:], diag, above, ALU.is_le))
                        then(nc.vector.tensor_tensor(best[:], best[:], stay[:], ALU.mult))
                        then(nc.vector.tensor_tensor(where[:], where[:], best[:], ALU.subtract))
                        then(nc.vector.tensor_tensor_scan(flat(tab[:, q, :, :]), flat(left[:]), flat(where[:]), 0.0,
                                                          ALU.mult, ALU.add))

            with Scope(nc, "walk") as s:
                trow = s.sb("trow", [B, 2, CH, S], BF16)
                pick = s.sb("pick", [B, 2, S])
                t_in = [s.sem(f"t_in{p}") for p in range(2)]
                step = s.sem("step")
                n_chunks = S // CH
                block = s.block()

                @block.sync
                def _(sp):
                    for n in range(n_chunks):
                        if n >= 2:
                            sp.wait_ge(step, 1 + CH * (n - 1))
                        c0 = (n_chunks - 1 - n) * CH
                        sp.dma_start(trow[:, n % 2, :, :], table[:, c0:c0 + CH, :]).then_inc(t_in[n % 2], 16)

                @block.vector
                def _(dve):
                    nc.vector.memset(ends[:, S - 1:S], float(S - 1)).then_inc(step, 1)
                    for n in range(n_chunks):
                        dve.wait_ge(t_in[n % 2], 16 * (n // 2 + 1))
                        for m in range(CH):
                            i = S - 1 - n * CH - m
                            if i == 0:
                                continue
                            dve.wait_ge(step, S - i)
                            nc.vector.scalar_tensor_tensor(out=pick[:, i % 2, :], in0=consts["iota"][0:B, :],
                                                           scalar=ends[:, i:i + 1], in1=trow[:, n % 2, CH - 1 - m, :],
                                                           op0=ALU.is_equal, op1=ALU.mult,
                                                           accum_out=ends[:, i - 1:i]).then_inc(step, 1)

            with Scope(nc, "lay") as s:
                last, first = s.sb("last", [P, QT, B]), s.sb("first", [P, QT, B])
                pick = s.sb("pick", [P, 2, S])
                after, on = s.sb("after", [P, 2, QT, S]), s.sb("on", [P, 2, QT, S])
                psE = s.ps("psE", [P, QT, B])
                psA = [s.ps(f"psA{i}", [P, QT, D]) for i in range(2)]
                e_done, e_read, found, cut, laid, spread, added = (
                    s.sem(n) for n in ("e_done", "e_read", "found", "cut", "laid", "spread", "added"))
                block = s.block()

                @block.tensor
                def _(pe):
                    for q in range(QT):
                        mm = nc.tensor.transpose(psE[:, q, :], ends[:, q * P:q * P + P], ident[0:B, 0:B])
                    mm.then_inc(e_done, 1)
                    for b in range(B):
                        pe.wait_ge(laid, b + 1)
                        if b >= 2:
                            pe.wait_ge(added, b - 1)
                        for t in range(QT):
                            for q in range(QT):
                                mm = nc.tensor.matmul(psA[b % 2][:, t, :], on[:, b % 2, q, t * P:t * P + P],
                                                      ctx_sb[:, b * QT + q, :], start=(q == 0), stop=(q == QT - 1))
                        mm.then_inc(spread, 1)

                @block.vector
                def _(dve):
                    dve.wait_ge(e_done, 1)
                    nc.vector.tensor_copy(last[:], psE[:]).then_inc(e_read, 1)
                    dve.wait_ge(e_read, 1)
                    iota = consts["iota"]
                    for q in range(QT):
                        for b in range(B):
                            n = q * B + b
                            if n >= 2:
                                dve.wait_ge(found, n - 1)
                            nc.vector.scalar_tensor_tensor(out=pick[:, n % 2, :], in0=iota[:], scalar=last[:, q, b:b + 1],
                                                           in1=start[:, q, b, :], op0=ALU.is_equal, op1=ALU.mult,
                                                           accum_out=first[:, q, b:b + 1]).then_inc(found, 1)
                    dve.wait_ge(found, QT * B)

                    def add(b):
                        dve.wait_ge(spread, b + 1)
                        nc.vector.tensor_tensor(x[:, b * QT:b * QT + QT, :], psA[b % 2][:], x[:, b * QT:b * QT + QT, :],
                                                ALU.add).then_inc(added, 1)

                    for b in range(B):
                        for q in range(QT):
                            if b >= 2:
                                dve.wait_ge(laid, b - 1)
                            nc.vector.tensor_scalar(after[:, b % 2, q, :], iota[:], first[:, q, b:b + 1], None,
                                                    ALU.is_ge).then_inc(cut, 1)
                        dve.wait_ge(cut, QT * (b + 1))
                        if b >= 2:
                            dve.wait_ge(spread, b - 1)
                        for q in range(QT):
                            ins = nc.vector.scalar_tensor_tensor(out=on[:, b % 2, q, :], in0=iota[:], scalar=last[:, q, b:b + 1],
                                                                 in1=after[:, b % 2, q, :], op0=ALU.is_le, op1=ALU.mult)
                        ins.then_inc(laid, 1)
                        if b >= 1:
                            add(b - 1)
                    add(B - 1)


HID = 768
HC = HID // P
QSCALE = 1.0 / 127.0


def gated_ffn(nc, name, x, ident, rstd, mean, w_gate, w_up, w_down):
    with Scope(nc, name) as s:
        raw = {n: s.sb(f"raw_{n}", sh, I32) for n, sh in (("g", [P, DC, HID]), ("u", [P, DC, HID]), ("d", [P, HC, D]))}
        W = {n: s.sb(f"w_{n}", list(t.shape)) for n, t in raw.items()}
        xn, xnT = s.sb("xn", [P, 2, QT, D]), s.sb("xnT", [P, 2, DC, S])
        act_g = s.sb("act_g", [P, 2, 2 * S])
        hT = s.sb("hT", [P, 2, HC, S])
        psT, psY = s.ps("psT", [P, 512]), s.ps("psY", [P, QT, D])
        psG, psU = [s.ps(f"psG{i}", [P, 512]) for i in range(2)], [s.ps(f"psU{i}", [P, 512]) for i in range(2)]
        w_in = [s.sem(f"w_in{n}") for n in "gud"]
        w_set, x_norm, t_done, t_read, gu_done, silu_done, h_done, y_ps, x_done = (
            s.sem(n) for n in ("w_set", "x_norm", "t_done", "t_read", "gu_done", "silu_done", "h_done", "y_ps", "x_done"))
        G = HC // 2
        def par(b, p, q):
            return (p * G + q) % 2

        block = s.block()

        @block.sync
        def _(sp):
            for q, (n, src) in enumerate((("g", w_gate), ("u", w_up), ("d", w_down))):
                sp.dma_start(raw[n][:], src.rearrange("(c p) n -> p c n", p=P)).then_inc(w_in[q], 16)

        @block.tensor
        def _(pe):
            def up(b, p, again):
                pe.wait_ge(x_norm, b + 1)
                pe.wait_ge(t_read, b)
                for c in range(DC):
                    for t in range(QT):
                        mm = nc.tensor.transpose(psT[:, c * S + t * P:c * S + t * P + P], xn[:, p, t, c * P:c * P + P], ident[:])
                mm.then_inc(t_done, 1)
                pe.wait_ge(t_read, b + 1)
                for q in range(G):
                    if again or q >= 2:
                        pe.wait_ge(h_done, G * b + q - 1)
                    for ps, w in ((psG, W["g"]), (psU, W["u"])):
                        for f in range(2):
                            for c in range(DC):
                                o = (2 * q + f) * P
                                mm = nc.tensor.matmul(ps[par(b, p, q)][:, f * S:f * S + S], w[:, c, o:o + P], xnT[:, p, c, :],
                                                      start=(c == 0), stop=(c == DC - 1))
                    mm.then_inc(gu_done, 1)

            def down(b, p):
                pe.wait_ge(h_done, G * (b + 1))
                pe.wait_ge(x_done, b)
                for t in range(QT):
                    for f in range(HC):
                        mm = nc.tensor.matmul(psY[:, t, :], hT[:, p, f, t * P:t * P + P], W["d"][:, f, :],
                                              start=(f == 0), stop=(f == HC - 1))
                mm.then_inc(y_ps, 1)

            pe.wait_ge(w_set, 3)
            up(0, 0, False)
            up(1, 1, True)
            down(0, 0)
            up(2, 0, True)
            down(1, 1)
            with pe.Fori(1, B // 2 - 1) as i:
                up(i * 2 + 1, 1, True)
                down(i * 2, 0)
                up(i * 2 + 2, 0, True)
                down(i * 2 + 1, 1)
            up(B - 1, 1, True)
            down(B - 2, 0)
            down(B - 1, 1)

        @block.scalar
        def _(act):
            def silu(b, p, again):
                for q in range(G):
                    k = par(b, p, q)
                    act.wait_ge(gu_done, G * b + q + 1)
                    if again or q >= 2:
                        act.wait_ge(h_done, G * b + q - 1)
                    nc.scalar.activation(act_g[:, k, :], psG[k][:], ACT.Silu).then_inc(silu_done, 1)

            silu(0, 0, False)
            silu(1, 1, True)
            with act.Fori(1, B // 2) as i:
                for k in range(2):
                    silu(i * 2 + k, k, True)

        @block.vector
        def _(dve):
            def normalise(b, p, again):
                if again:
                    dve.wait_ge(t_done, b - 1)
                for t in range(QT):
                    ins = nc.vector.tensor_scalar(xn[:, p, t, :], x[:, b * QT + t, :], mean[:, bass.ds(b * QT + t, 1)],
                                                  rstd[:, bass.ds(b * QT + t, 1)], ALU.subtract, ALU.mult)
                ins.then_inc(x_norm, 1)

            def hidden(b, p, again):
                dve.wait_ge(t_done, b + 1)
                if again:
                    dve.wait_ge(gu_done, G * (b - 1))
                nc.vector.tensor_copy(xnT[:, p, :, :].rearrange("p c n -> p (c n)"), psT[:]).then_inc(t_read, 1)
                if again:
                    dve.wait_ge(y_ps, b - 1)
                for q in range(G):
                    k = par(b, p, q)
                    dve.wait_ge(silu_done, G * b + q + 1)
                    nc.vector.tensor_tensor(hT[:, p, 2 * q:2 * q + 2, :].rearrange("p f n -> p (f n)"), psU[k][:],
                                            act_g[:, k, :], ALU.mult).then_inc(h_done, 1)

            def add(b):
                dve.wait_ge(y_ps, b + 1)
                nc.vector.tensor_tensor(x[:, bass.ds(b * QT, QT), :], psY[:], x[:, bass.ds(b * QT, QT), :], ALU.add)\
                    .then_inc(x_done, 1)

            normalise(0, 0, False)
            normalise(1, 1, False)
            for q, n in enumerate("gud"):
                dve.wait_ge(w_in[q], 16)
                k_ = W[n].shape[1] * W[n].shape[2]
                nc.vector.tensor_scalar(W[n][:].rearrange("p c n -> p (c n)"), raw[n][:].rearrange("p c n -> p (c n)"),
                                        QSCALE, None, ALU.mult).then_inc(w_set, 1)
            hidden(0, 0, False)
            hidden(1, 1, False)
            normalise(2, 0, True)
            add(0)
            hidden(2, 0, True)
            normalise(3, 1, True)
            add(1)
            with dve.Fori(1, B // 2 - 1) as i:
                hidden(i * 2 + 1, 1, True)
                normalise(i * 2 + 2, 0, True)
                add(i * 2)
                hidden(i * 2 + 2, 0, True)
                normalise(i * 2 + 3, 1, True)
                add(i * 2 + 1)
            hidden(B - 1, 1, True)
            add(B - 2)
            add(B - 1)


def find_groups(nc, name, x, ident, rstd, mean, wq, qg, regs, flags):
    with Scope(nc, name) as s:
        wq_sb, g_sb, reg = s.sb("wq", [P, DC, D]), s.sb("g", [P, H, DK]), s.sb("reg", [P, NT])
        xn, xT = s.sb("xn", [P, 2, D]), s.sb("xT", [P, 2, DC, P])
        q = s.sb("q", [P, NT, D])
        big = s.sb("big", [P, NT * H, DK])
        n2, dot = s.sb("n2", [P, NT * H]), s.sb("dot", [P, NT * H])
        g2, gn, gr, gq = s.sb("g2", [P, H, DK]), s.sb("gn", [P, H]), s.sb("gr", [P, H]), s.sb("gq", [P, H, DK])
        gs, root = s.sb("gs", [P, H]), s.sb("root", [P, NT * H])
        sim, t1 = s.sb("sim", [P, NT]), s.sb("t1", [P, NT])
        ends, ends_all = s.sb("ends", [P, 2]), s.sb("ends_all", [P, 2])
        span, inv = s.sb("span", [P, 1]), s.sb("inv", [P, 1])
        col = s.sb("col", [P, 4, NT])
        rows = s.sb("rows", [4 * NT, P], BF16)
        psT, psQ = [s.ps(f"psT{i}", [P, 512]) for i in range(2)], [s.ps(f"psQ{i}", [P, 512]) for i in range(2)]
        psF = s.ps("psF", [P, P])
        (w_in, x_norm, t_done, t_read, q_ps, q_read, step, g_in, g_out, n_in, n_out, e_in, e_out, c_done, f_done, r_done,
         stored) = (s.sem(n) for n in ("w_in", "x_norm", "t_done", "t_read", "q_ps", "q_read", "step", "g_in", "g_out",
                                       "n_in", "n_out", "e_in", "e_out", "c_done", "f_done", "r_done", "stored"))
        block = s.block()

        @block.sync
        def _(sp):
            sp.dma_start(wq_sb[:], wq.rearrange("(c p) n -> p c n", p=P)).then_inc(w_in, 16)
            sp.dma_start(g_sb[:], qg.rearrange("p (h d) -> p h d", h=H)).then_inc(w_in, 16)
            sp.dma_start(reg[:], regs).then_inc(w_in, 16)
            sp.wait_ge(r_done, 1)
            sp.dma_start(flags.rearrange("f (t p) -> (f t) p", p=P), rows[:]).then_inc(stored, 16)
            sp.wait_ge(stored, 16)

        @block.tensor
        def _(pe):
            pe.wait_ge(w_in, 48)

            def tile(t, k, again):
                pe.wait_ge(x_norm, t + 1)
                if again:
                    pe.wait_ge(t_read, t - 1)
                for c in range(DC):
                    mm = nc.tensor.transpose(psT[k][:, c * P:c * P + P], xn[:, k, c * P:c * P + P], ident[:])
                mm.then_inc(t_done, 1)
                pe.wait_ge(t_read, t + 1)
                if again:
                    pe.wait_ge(q_read, t - 1)
                for c in range(DC):
                    mm = nc.tensor.matmul(psQ[k][:, 0:D], xT[:, k, c, :], wq_sb[:, c, :], start=(c == 0), stop=(c == DC - 1))
                mm.then_inc(q_ps, 1)

            tile(0, 0, False)
            tile(1, 1, False)
            with pe.Fori(1, NT // 2) as i:
                for k in range(2):
                    tile(i * 2 + k, k, True)
            pe.wait_ge(c_done, 1)
            nc.tensor.transpose(psF[0:4 * NT, :], col[:].rearrange("p f t -> p (f t)"), ident[:]).then_inc(f_done, 1)

        @block.scalar
        def _(act):
            act.wait_ge(g_in, 1)
            nc.scalar.activation(gs[:], gn[:], ACT.Sqrt).then_inc(g_out, 1)
            with act.Fori(0, NT // 2) as i:
                for k in range(2):
                    act.wait_ge(q_ps, i * 2 + k + 1)
                    nc.scalar.activation(q[:, i * 2 + k, :], psQ[k][:, 0:D], ACT.Copy).then_inc(q_read, 1)
            act.wait_ge(n_in, 1)
            nc.scalar.activation(root[:], n2[:], ACT.Sqrt).then_inc(n_out, 1)

        @block.gpsimd
        def _(pool):
            pool.wait_ge(e_in, 1)
            nc.gpsimd.partition_all_reduce(ends_all[:], ends[:], P, bass.bass_isa.ReduceOp.max).then_inc(e_out, 1)

        @block.vector
        def _(dve):
            n = [0]

            def then(ins):
                n[0] += 1
                ins.then_inc(step, 1)
                dve.wait_ge(step, n[0])

            dve.wait_ge(w_in, 48)
            then(nc.vector.tensor_tensor(g2[:], g_sb[:], g_sb[:], ALU.mult))
            nc.vector.tensor_reduce(gn[:], g2[:], AX.X, ALU.add).then_inc(g_in, 1)
            dve.wait_ge(g_out, 1)
            then(nc.vector.reciprocal(gr[:], gs[:]))
            then(nc.vector.tensor_tensor(gq[:], g_sb[:], gr[:].unsqueeze(2).to_broadcast([P, H, DK]), ALU.mult))

            def tile(t, k, again):
                if again:
                    dve.wait_ge(t_done, t - 1)
                nc.vector.tensor_scalar(xn[:, k, :], x[:, t, :], mean[:, bass.ds(t, 1)], rstd[:, bass.ds(t, 1)],
                                        ALU.subtract, ALU.mult).then_inc(x_norm, 1)
                dve.wait_ge(t_done, t + 1)
                if again:
                    dve.wait_ge(q_ps, t - 1)
                nc.vector.tensor_copy(xT[:, k, :, :].rearrange("p c n -> p (c n)"), psT[k][:, 0:D]).then_inc(t_read, 1)

            tile(0, 0, False)
            tile(1, 1, False)
            with dve.Fori(1, NT // 2) as i:
                for k in range(2):
                    tile(i * 2 + k, k, True)
            dve.wait_ge(q_read, NT)
            q4 = q[:].rearrange("p t (h d) -> p t h d", h=H)
            q3 = q[:].rearrange("p t (h d) -> p (t h) d", h=H)
            then(nc.vector.tensor_tensor(big[:], q3, q3, ALU.mult))
            nc.vector.tensor_reduce(n2[:], big[:], AX.X, ALU.add).then_inc(n_in, 1)
            dve.wait_ge(n_in, 1)
            big4 = big[:].rearrange("p (t m) d -> p t (m d)", t=NT)
            then(nc.vector.tensor_tensor(big4, q[:], gq[:].rearrange("p h d -> p (h d)").unsqueeze(1).to_broadcast([P, NT, D]),
                                         ALU.mult))
            then(nc.vector.tensor_reduce(dot[:], big[:], AX.X, ALU.add))
            dve.wait_ge(n_out, 1)
            then(nc.vector.reciprocal(root[:], root[:]))
            then(nc.vector.tensor_tensor(dot[:], dot[:], root[:], ALU.mult))
            then(nc.vector.tensor_reduce(sim[:], dot[:].rearrange("p (t h) -> p t h", t=NT), AX.X, ALU.add))
            then(nc.vector.tensor_scalar(sim[:], sim[:], 1.0 / H, None, ALU.mult))
            then(nc.vector.scalar_tensor_tensor(out=t1[:], in0=reg[:], scalar=-BIG, in1=sim[:], op0=ALU.mult, op1=ALU.add))
            then(nc.vector.tensor_reduce(ends[:, 0:1], t1[:], AX.X, ALU.max))
            then(nc.vector.scalar_tensor_tensor(out=t1[:], in0=reg[:], scalar=BIG, in1=sim[:], op0=ALU.mult, op1=ALU.add))
            then(nc.vector.tensor_reduce(ends[:, 1:2], t1[:], AX.X, ALU.min))
            nc.vector.tensor_scalar(ends[:, 1:2], ends[:, 1:2], -1.0, None, ALU.mult).then_inc(e_in, 1)
            dve.wait_ge(e_out, 1)
            then(nc.vector.tensor_tensor(span[:], ends_all[:, 0:1], ends_all[:, 1:2], ALU.add))
            then(nc.vector.reciprocal(inv[:], span[:]))
            then(nc.vector.tensor_scalar(t1[:], sim[:], ends_all[:, 1:2], inv[:, 0:1], ALU.add, ALU.mult))
            then(nc.vector.tensor_scalar(t1[:], t1[:], 0.9, None, ALU.is_gt))
            then(nc.vector.tensor_tensor(col[:, 0, :], t1[:], reg[:], ALU.max))
            then(nc.vector.tensor_scalar(col[:, 1, :], col[:, 0, :], -1.0, 1.0, ALU.mult, ALU.add))
            then(nc.vector.tensor_scalar(col[:, 2, :], col[:, 1, :], -BIG, None, ALU.mult))
            then(nc.vector.tensor_tensor(t1[:], col[:, 0, :], reg[:], ALU.subtract))
            nc.vector.tensor_scalar(col[:, 3, :], t1[:], -BIG, None, ALU.mult).then_inc(c_done, 1)
            dve.wait_ge(f_done, 1)
            nc.vector.tensor_copy(rows[:], psF[0:4 * NT, :]).then_inc(r_done, 1)



def program(nc, t, out):
    with Scope(nc, "all") as s:
        x = s.sb("x", [P, NT, D])
        ident = s.sb("ident", [P, P])
        rstd, mean = s.sb("rstd", [P, NT]), s.sb("mean", [P, NT])
        parts_at = nc.dram_tensor("parts_at", (2, 2, 3, D, S), BF16, kind="Internal").ap()
        consts = {"before": s.sb("before", [P, P]), "ones": s.sb("ones", [P, P]), "iota": s.sb("iota", [P, S]),
                  "lane": s.sb("lane", [P, 1])}
        NB = moe_blocks(2)
        slots_x = nc.dram_tensor("slots_x", (NB * P, D), F32, kind="Internal").ap()
        slots_y = nc.dram_tensor("slots_y", (NB * P, D), F32, kind="Internal").ap()
        dma = {"scattered": Counted(s.sem("scattered")), "fetched_w1": [Counted(s.sem(f"fetched_w1{p}")) for p in range(2)],
               "fetched_w2": [Counted(s.sem(f"fetched_w2{p}")) for p in range(2)],
               "back": [Counted(s.sem(f"back{t_}")) for t_ in range(NT)]}
        with Scope(nc, "start") as s0:
            loaded = s0.sem("loaded")
            block = s0.block()

            @block.sync
            def _(sp):
                sp.dma_start(x[:], t["x"].rearrange("b (t p) d -> p (b t) d", p=P)).then_inc(loaded, 16)
                sp.dma_start(ident[:], t["c_ident"]).then_inc(loaded, 16)
                for n, a in consts.items():
                    sp.dma_start(a[:], t[f"c_{n}"]).then_inc(loaded, 16)
                sp.wait_ge(loaded, 32 + 16 * len(consts))

        def weights(pre, names):
            return {k: t[f"{pre}{n}"] for k, n in names.items()}

        layernorm_stats(nc, x, rstd, mean, "l0a")
        attention(nc, "l0a", x, ident, rstd, mean, DK ** -0.5,
                  weights("L0_", {k: k for k in ("wq", "wk", "wv", "wo", "bq", "bk", "bv", "bo")}), parts_at,
                  ctxT=t["ctxT"])

        layernorm_stats(nc, x, rstd, mean, "l0f")
        moe(nc, dma, "l0f", 1, x, ident, rstd, mean, consts, t["L0_wr"], t["L0_br"], (t["L0_table1"], t["L0_table2"]), slots_x, slots_y)

        layernorm_stats(nc, x, rstd, mean, "l1a")
        dist = nc.dram_tensor("dist", (B, S, S), F32, kind="Internal").ap()
        cost = nc.dram_tensor("cost", (B, S + 1, S + 1), F32, kind="Internal").ap()
        table = nc.dram_tensor("table", (B, S, S), BF16, kind="Internal").ap()
        alignment(nc, x, ident, rstd, mean, consts, t["ctx"], t["ctxT"], dist, cost, table)

        layernorm_stats(nc, x, rstd, mean, "l1f")
        gated_ffn(nc, "l1f", x, ident, rstd, mean, t["L1_gate"], t["L1_up"], t["L1_down"])
        layernorm_stats(nc, x, rstd, mean, "l2a")
        attention(nc, "l2a", x, ident, rstd, mean, 1.0,
                  weights("L2_", {k: k for k in ("wq", "wk", "wv", "wo", "wq_swap", "wk_swap")}), parts_at, ctxT=t["ctxT"],
                  rope=(t["c_cos"], t["c_sin"]))
        layernorm_stats(nc, x, rstd, mean, "l2f")
        moe(nc, dma, "l2f", 2, x, ident, rstd, mean, consts, t["L2_wr"], t["L2_br"], (t["L2_table1"], t["L2_table2"]), slots_x, slots_y)
        layernorm_stats(nc, x, rstd, mean, "l3a")
        attention(nc, "l3a", x, ident, rstd, mean, DK ** -0.5,
                  weights("L3_", {k: k for k in ("wq", "wk", "wv", "wo", "bq", "bk", "bv", "bo")}), parts_at, ctxT=t["ctxT"],
                  topk=t["mask"])
        layernorm_stats(nc, x, rstd, mean, "l3f")
        flags = nc.dram_tensor("flags", (4, TOK), BF16, kind="Internal").ap()
        find_groups(nc, "l3g", x, ident, rstd, mean, t["L3f_wq"], t["L3f_guide"], t["c_reg"], flags)
        w = weights("L3f_", {k: k for k in ("wq", "wk", "wv", "wo", "bo")})
        w.update({k: t[f"c_rg_{k}"] for k in ("sel", "own", "fold", "one")})
        attention(nc, "l3f", x, ident, rstd, mean, DK ** -0.5, w, parts_at, groups=flags)

        with Scope(nc, "end") as s1:
            stored = s1.sem("stored")
            block = s1.block()

            @block.sync
            def _(sp):
                sp.dma_start(out.rearrange("b (t p) d -> p (b t) d", p=P), x[:]).then_inc(stored, 16)
                sp.wait_ge(stored, 16)


def kernel(**inputs):
    import concourse.bacc as bacc
    from concourse.bass_utils import run_bass_kernel_spmd

    def c(a):
        return np.ascontiguousarray(a)

    def column(a):
        return c(np.asarray(a).reshape(DC, P).T)

    def rows(a):
        return c(np.broadcast_to(np.asarray(a).reshape(1, -1), (P, np.asarray(a).size)))

    g = {k: np.asarray(v) for k, v in inputs.items()}
    arrays = {
        "x": c(g["x"]),
        "c_ident": np.eye(P, dtype=np.float32),
        "ctx": c(g["ctx_1024"]),
        "c_before": np.triu(np.ones((P, P), np.float32), 1),
        "c_ones": np.ones((P, P), np.float32),
        "c_iota": c(np.broadcast_to(np.arange(S, dtype=np.float32), (P, S))),
        "c_lane": np.arange(P, dtype=np.float32).reshape(P, 1),
        "ctxT": c(g["ctx_1024"].reshape(TOK, DC, P).transpose(1, 2, 0)),
    }
    for n in ("wq", "wk", "wv", "wo"):
        arrays[f"L0_{n}"] = c(g[f"L0_xattn_{n}"].T)
    for n in ("bq", "bk"):
        arrays[f"L0_{n}"] = column(g[f"L0_xattn_{n}"])
    for n in ("bv", "bo"):
        arrays[f"L0_{n}"] = rows(g[f"L0_xattn_{n}"])

    arrays["L1_gate"], arrays["L1_up"], arrays["L1_down"] = (c(g[f"L1_ffn_w_{n}"].T) for n in ("gate", "up", "down"))
    kv = g["L2_xattn_Wkv"].reshape(H, 2, DK, D)
    wk, wv = kv[:, 0].reshape(D, D), kv[:, 1].reshape(D, D)
    swap = np.arange(D) ^ 1
    arrays["L2_wq"], arrays["L2_wk"], arrays["L2_wv"] = c(g["L2_xattn_Wq"].T), c(wk.T), c(wv.T)
    arrays["L2_wq_swap"], arrays["L2_wk_swap"] = c(g["L2_xattn_Wq"][swap].T), c(wk[swap].T)
    arrays["L2_wo"] = c(g["L2_xattn_Wo"].T)
    theta = np.power(np.float32(10000.0), np.float32(2.0) * np.arange(DK // 2, dtype=np.float32) / np.float32(DK))
    ang = (np.arange(S, dtype=np.float32)[:, None] / theta.astype(np.float32)).astype(np.float32)
    sign = np.where(np.arange(P) % 2 == 0, np.float32(-1), np.float32(1))[:, None]
    arrays["c_cos"] = c(np.tile(np.repeat(np.cos(ang), 2, axis=1).T, (P // DK, 1)))
    arrays["c_sin"] = c(np.tile(np.repeat(np.sin(ang), 2, axis=1).T, (P // DK, 1)) * sign)
    for n in ("q", "k", "v", "o"):
        arrays[f"L3_w{n}"] = c(g[f"L3_xattn_W{n}"].T)
        arrays[f"L3_b{n}"] = (column if n in "qk" else rows)(g[f"L3_xattn_b{n}"])
    arrays["mask"] = c(g["mask_BxSxS2_if1"].reshape(B * QT, P, S))
    for n, a in enumerate("qkv"):
        arrays[f"L3f_w{a}"] = c(g["L3_ffn_W_qkv"][:, n * D:(n + 1) * D])
    arrays["L3f_wo"], arrays["L3f_bo"] = c(g["L3_ffn_W_proj"]), rows(g["L3_ffn_b_proj"])
    arrays["L3f_guide"] = rows(g["L3_ffn_g_info"][0, 0])
    reg = np.zeros((P, NT), np.float32)
    reg[:REG, ::QT] = 1
    arrays["c_reg"] = reg
    head = np.arange(H)
    m = np.arange(RG)
    arrays["c_rg_sel"] = c((np.arange(P)[:, None, None] // DK + np.arange(DC)[None, :, None] * (P // DK)
                            == head[None, None, :]).astype(np.float32))
    arrays["c_rg_own"] = c((m[:, None] // REG == np.arange(D)[None, :] // DK).astype(np.float32))
    arrays["c_rg_fold"] = c((m[:, None] % REG == np.arange(REG)[None, :]).astype(np.float32))
    arrays["c_rg_one"] = c(np.stack([np.zeros(RG), np.ones(RG)]).astype(np.float32))
    for k, wr, br in (("L0", "Wr", "br"), ("L2", "Wg", "bg")):
        w1, b1, w2, b2 = (g[f"{k}_ffn_{n}"] for n in ("W1", "b1", "W2", "b2"))
        arrays[f"{k}_wr"], arrays[f"{k}_br"] = c(g[f"{k}_ffn_{wr}"]), rows(g[f"{k}_ffn_{br}"])
        arrays[f"{k}_table1"] = c(np.concatenate([
            w1.reshape(E, DC, P, F).transpose(0, 2, 1, 3).reshape(E * P, DC * F),
            b1.reshape(E, FC, P).transpose(0, 2, 1).reshape(E * P, FC)], axis=1))
        arrays[f"{k}_table2"] = c(np.concatenate([
            w2.reshape(E, FC, P, D).transpose(0, 2, 1, 3).reshape(E * P, FC * D),
            np.broadcast_to(b2.reshape(E, 1, D), (E, P, D)).reshape(E * P, D)], axis=1))

    nc = bacc.Bacc("TRN2", target_bir_lowering=False, num_devices=1)
    aps = {n: nc.dram_tensor(f"in_{n}", a.shape, mybir.dt.from_np(a.dtype), kind="ExternalInput").ap()
           for n, a in arrays.items()}
    out = nc.dram_tensor("out_x", (B, S, D), F32, kind="ExternalOutput").ap()
    program(nc, aps, out)
    r = run_bass_kernel_spmd(nc, [{f"in_{n}": a for n, a in arrays.items()}], core_ids=[0])
    return r.results[0]["out_x"]
```

```python
from contextlib import ExitStack

import numpy as np

import concourse.bass as bass
from concourse import mybir

F32 = mybir.dt.float32
BF16 = mybir.dt.bfloat16
I32 = mybir.dt.int32
U32 = mybir.dt.uint32
ALU = mybir.AluOpType
ACT = mybir.ActivationFunctionType
AX = mybir.AxisListType

P = 128
B, S, D = 8, 256, 256
TOK = B * S
NT = TOK // P
DC = D // P
H, DK = 16, 16
QT = S // P
EPS = 1e-5
STEPS = H
PER_QT = STEPS // QT
BIG = 1.0e30
NEG = -1.0e9
TOPK = 32
REG = 5
PAIRS_OF_PARTS = [(a, b) for a in range(3) for b in range(3) if a + b < 4]
RG = H * REG
GONE = -3.0e38


class Scope:

    def __init__(self, nc, name):
        self.nc, self.name, self.ctx, self.sems, self.blocks = nc, name, ExitStack(), [], ExitStack()

    def __enter__(self):
        self.ctx.__enter__()
        return self

    def __exit__(self, *what):
        self.blocks.__exit__(*what)
        if what[0] is None:
            numbers = sorted(x.num for x in self.sems) if self.name != "all" else []
            while numbers:
                n = 1
                while n < len(numbers) and numbers[n] == numbers[0] + n:
                    n += 1
                self.nc.all_engine_barrier(sems_to_clear=range(numbers[0], numbers[0] + n))
                numbers = numbers[n:]
        return self.ctx.__exit__(*what)

    def sb(self, name, shape, dt=F32):
        return self.ctx.enter_context(self.nc.sbuf_tensor(f"{self.name}_{name}", shape, dt))

    def ps(self, name, shape, dt=F32):
        return self.ctx.enter_context(self.nc.psum_tensor(f"{self.name}_{name}", shape, dt))

    def sem(self, name):
        self.sems.append(self.ctx.enter_context(self.nc.semaphore(f"{self.name}_{name}")))
        return self.sems[-1]

    def block(self):
        return self.blocks.enter_context(self.nc.Block())


def layernorm_stats(nc, x, rstd, mean, name):
    with Scope(nc, f"{name}_ln") as s:
        st = s.sb("st", [P, NT, 6])
        mv = s.sb("mv", [P, NT, 2])
        std = s.sb("std", [P, NT])
        epst = s.sb("eps", [P, 1])
        eps_set, stats, moments, rooted, done = (s.sem(n) for n in ("eps_set", "stats", "moments", "rooted", "done"))
        block = s.block()

        @block.vector
        def _(dve):
            nc.vector.memset(epst[:], EPS).then_inc(eps_set, 1)
            for t in range(NT):
                nc.vector.bn_stats(st[:, t, :], x[:, t, :]).then_inc(stats, 1)
            dve.wait_ge(stats, NT)
            for t in range(NT):
                nc.vector.bn_aggr(mv[:, t, :], st[:, t, :]).then_inc(moments, 1)
            dve.wait_ge(moments, NT)
            nc.vector.tensor_copy(mean[:], mv[:, :, 0])
            dve.wait_ge(rooted, 1)
            nc.vector.reciprocal(rstd[:], std[:]).then_inc(done, 1)

        @block.scalar
        def _(act):
            act.wait_ge(eps_set, 1)
            act.wait_ge(moments, NT)
            nc.scalar.activation(std[:], mv[:, :, 1], ACT.Sqrt, bias=epst[:, 0:1]).then_inc(rooted, 1)


def attention(nc, name, x, ident, rstd, mean, scale, w, parts_at, ctxT=None, rope=None, topk=None, groups=None):
    with Scope(nc, name) as s:
        names = ["wq", "wk", "wv", "wo"] + (["wq_swap", "wk_swap"] if rope is not None else [])
        W = {n: s.sb(n, [P, DC, D]) for n in names}
        Bc = {n: s.sb(n, [P, DC]) for n in ("bq", "bk") if w.get(n) is not None}
        Br = {n: s.sb(n, [P, D]) for n in ("bv", "bo") if w.get(n) is not None}
        xn = s.sb("xn", [P, 2, QT, D])
        xnT = s.sb("xnT", [P, 2, DC, S])
        kvT = s.sb("kvT", [P, 2, DC, S]) if ctxT is not None else xnT
        qf = s.sb("qf", [P, 2, DC, S])
        part = s.sb("part", [P, 2, 3, DC, S], BF16)
        rest_of = s.sb("rest_of", [P, 2, DC, S])
        stack = s.sb("stack", [P, 2, 2, H, S], BF16)
        kT = s.sb("kT", [P, 2, DC, S])
        vp = s.sb("vp", [P, 2, QT, DC, P // DK * (P + DK)])
        v = s.sb("v", [P, 2, QT, D]) if groups is not None else None
        prob = s.sb("prob", [P, 4, 2, S])
        probT = s.sb("probT", [P, 2, 2, 2, P])
        nmax = s.sb("nmax", [P, QT, H])
        rsum = s.sb("rsum", [P, 2, QT, H])
        inv = s.sb("inv", [P, H])
        rinv = s.sb("rinv", [P, H, DK])
        rT = s.sb("rT", [P, DC, P])
        oT = s.sb("oT", [P, DC, P])
        if rope is not None:
            cosT, sinT = s.sb("cosT", [P, S]), s.sb("sinT", [P, S])
            rot = s.sb("rot", [P, 2, DC, S])
            krot = s.sb("krot", [P, 2, DC, S])
        if topk is not None:
            mraw = s.sb("mraw", [P, 2, QT, S], I32)
            mlow = s.sb("mlow", [P, 2, QT, S])
            mone = s.sb("mone", [P, 2, QT, S])
            raw_sc = s.sb("raw_sc", [P, 2, 2, S])
            kept = s.sb("kept", [P, 2, S])
            carrier = s.sb("carrier", [P, 1])
            sc_sb = s.sb("sc_sb", [P, 4, 2, S])
            left = s.sb("left", [P, 2, 2, S])
            top8 = s.sb("top8", [P, 2, 2, TOPK])
            expd = s.sb("expd", [P, 2, 2, S])
            rest = s.sb("rest", [P, 2, 2, S])
            top_exp = s.sb("top_exp", [P, 2, TOPK])
        if groups is not None:
            mq, mk = s.sb("mq", [P, 2, S], BF16), s.sb("mk", [P, 2, S], BF16)
            rg_sel, rg_own, rg_fold, rg_one = (s.sb(n, sh) for n, sh in (
                ("rg_sel", [P, DC, H]), ("rg_own", [RG, D]), ("rg_fold", [RG, REG]), ("rg_one", [2, RG])))
            rg_two = s.sb("rg_two", [2, RG], BF16)
            rg_q = s.sb("rg_q", [P, DC, H, REG])
            rg_nmax, rg_sum, rg_inv = (s.sb(n, [RG, 1]) for n in ("rg_nmax", "rg_sum", "rg_inv"))
            rg_e, rg_p = s.sb("rg_e", [RG, S]), s.sb("rg_p", [RG, S])
            rg_pT, rg_o = s.sb("rg_pT", [P, QT, RG]), s.sb("rg_o", [RG, D])
            rg_x = s.sb("rg_x", [P, DC, REG])
            m_zero = s.sem("m_zero")
            (rg_step, rg_set, rg_sc, rg_max, rg_exp, rg_prob, rg_tr, rg_read, rg_pv, rg_cut, rg_sum_ps, rg_mix) = (
                s.sem(n) for n in ("rg_step", "rg_set", "rg_sc", "rg_max", "rg_exp", "rg_prob", "rg_tr", "rg_read",
                                   "rg_pv", "rg_cut", "rg_sum_ps", "rg_mix"))

        bqs = s.sb("bqs", [P, DC]) if "bq" in Bc else None
        obias = s.sb("obias", [P, D]) if "bo" in Br else None
        bank = [s.ps(f"bank{g}", [P, 512]) for g in range(4)]
        psT = [s.ps(f"psT{i}", [P, 2, 2, P]) for i in range(2)]
        psO = s.ps("psO", [P, 512])
        psX = s.ps("psX", [P, 512])

        q_set = s.sem("q_set")
        cast_0, rest_set, cast_1, split = (s.sem(n) for n in ("cast_0", "rest_set", "cast_1", "split"))
        parts_out, stack_in = s.sem("parts_out"), [s.sem(f"stack_in{p}") for p in range(2)]
        n_in = 2 * len(PAIRS_OF_PARTS)
        w_in, x_norm = s.sem("w_in"), s.sem("x_norm")
        kv_in = [s.sem(f"kv_in{p}") for p in range(2)]
        m_in = [s.sem(f"m_in{p}") for p in range(2)]
        m_cap, raw_set, kept_set = s.sem("m_cap"), s.sem("raw_set"), s.sem("kept_set")
        xT_ps, q_ps, k_ps, v_ps = (s.sem(n) for n in ("xT_ps", "q_ps", "k_ps", "v_ps"))
        xT_ev, q_ev, k_ev, v_ev = (s.sem(n) for n in ("xT_ev", "q_ev", "k_ev", "v_ev"))
        kt_set = s.sem("kt_set")
        qs_ps, ks_ps, qs_ev, ks_ev, rot_step = (s.sem(n) for n in ("qs_ps", "ks_ps", "qs_ev", "ks_ev", "rot_step"))
        sc_done, max_done, exp_done, tr_done, pT_done, pv_done = (
            s.sem(n) for n in ("sc_done", "max_done", "exp_done", "tr_done", "pT_done", "pv_done"))
        bqs_set, on_half = s.sem("bqs_set"), s.sem("on_half")
        picked, pick_step = s.sem("picked"), s.sem("pick_step")
        capped, marked, rest_done, sum_done = s.sem("capped"), s.sem("marked"), s.sem("rest_done"), s.sem("sum_done")
        prob_done = exp_done if topk is None else picked
        inv_done, rT_ps, rT_done, oT_done, out_ps, out_b, x_done, vp_zero, inv_set = (
            s.sem(n) for n in ("inv_done", "rT_ps", "rT_done", "oT_done", "out_ps", "out_b", "x_done", "vp_zero", "inv_set"))
        n_w = len(W) + len(Bc) + len(Br) + (2 if rope is not None else 0) + (4 if groups is not None else 0)
        made = ["k", "xT", "q", "v"] if rope is None else ["k", "xT", "q", "k_swap", "q_swap", "v"]
        if ctxT is None:
            made = ["xT", "k", "q", "v"]
        made_at, first_at, second_at = ([0, 1, 3, 5], (4, 5), (6, 7))
        if rope is not None:
            made_at, first_at, second_at = ([0, 1, 2, 3, 4, 6], (5, 6), (7, 8))
        if topk is not None:
            made_at, first_at, second_at = ([0, 1, 2, 4], (3, 4), (5, 6))
        if groups is not None:
            made_at, first_at, second_at = ([0, 2, 3, 5], (4, 5), (6, 7))
        read_of = {"xT": xT_ev, "k": k_ev, "v": v_ev, "q": q_set if rope is None else q_ev, "k_swap": ks_ev, "q_swap": qs_ev}
        bank_free = raw_set if topk is not None else exp_done
        block = s.block()

        @block.sync
        def _(sp):
            for n, t in W.items():
                sp.dma_start(t[:], w[n].rearrange("(c p) n -> p c n", p=P)).then_inc(w_in, 16)
            for n, t in list(Bc.items()) + list(Br.items()):
                sp.dma_start(t[:], w[n]).then_inc(w_in, 16)
            if groups is not None:
                for n, t in (("sel", rg_sel), ("own", rg_own), ("fold", rg_fold), ("one", rg_one)):
                    sp.dma_start(t[:], w[n]).then_inc(w_in, 16)
            if rope is not None:
                sp.dma_start(cosT[:], rope[0]).then_inc(w_in, 16)
                sp.dma_start(sinT[:], rope[1]).then_inc(w_in, 16)

            def load(b, p, reuse):
                if ctxT is not None:
                    if reuse:
                        sp.wait_ge(v_ps, b - 1)
                    sp.dma_start(kvT[:, p, :, :], ctxT[:, :, bass.ds(b * S, S)].rearrange("c p n -> p c n"))\
                        .then_inc(kv_in[p], 16)
                if topk is not None:
                    if reuse:
                        sp.wait_ge(m_cap, b - 1)
                    sp.dma_start(mraw[:, p, :, :], topk[bass.ds(b * QT, QT), :, :].rearrange("q p n -> p q n"))\
                        .then_inc(m_in[p], 16)

                if groups is not None:
                    if reuse:
                        sp.wait_ge(sc_done, STEPS * (b - 1))
                        sp.wait_ge(rg_sc, b - 1)
                    else:
                        sp.wait_ge(m_zero, 2)
                    for dst, row in ((mq, 0), (mk, 2)):
                        sp.dma_start(dst[0:2, p, :], groups[row:row + 2, bass.ds(b * S, S)]).then_inc(m_in[p], 16)

            def spread(b, p):
                sp.wait_ge(split, 2 * (b + 1))
                for t in range(2):
                    sp.dma_start(parts_at[p, t].rearrange("m (c r) n -> r m c n", r=P), part[:, t, :, :, :])\
                        .then_inc(parts_out, 16)
                sp.wait_ge(parts_out, 32 * (b + 1))
                for row, of in enumerate(PAIRS_OF_PARTS):
                    for t in range(2):
                        sp.dma_start(stack[DK * row:DK * row + DK, p, t, :, :],
                                     parts_at[p, t, of[1 - t]].rearrange("(h d) n -> d h n", d=DK)).then_inc(stack_in[p], 16)

            load(0, 0, False)
            load(1, 1, False)
            spread(0, 0)
            with sp.Fori(0, B // 2 - 1) as i:
                for k in range(2):
                    if groups is None:
                        load(i * 2 + 2 + k, k, True)
                        spread(i * 2 + 1 + k, 1 - k)
                    else:
                        spread(i * 2 + 1 + k, 1 - k)
                        load(i * 2 + 2 + k, k, True)
            spread(B - 1, 1)

        @block.tensor
        def _(pe):
            def product(out, lhs, rhs):
                for c in range(DC):
                    mm = nc.tensor.matmul(out, lhs[c], rhs[c], start=(c == 0), stop=(c == DC - 1))
                return mm

            def project(b, p, pair, what, first=False):
                k = made.index(what)
                out = bank[2 + k % 2]
                if k >= 2 or not first:
                    pe.wait_ge(read_of[made[k - 2]], b + 1 if k >= 2 else b)
                if what == "xT":
                    pe.wait_ge(x_norm, b + 1)
                    for c in range(DC):
                        for t in range(QT):
                            mm = nc.tensor.transpose(out[:, c * S + t * P:c * S + t * P + P],
                                                     xn[:, p, t, c * P:c * P + P], ident[:])
                    mm.then_inc(xT_ps, 1)
                    return
                if what in ("q", "q_swap") or ctxT is None:
                    pe.wait_ge(xT_ev, b + 1)
                else:
                    pe.wait_ge(kv_in[p], (pair + 1) * 16)
                src = xnT if what in ("q", "q_swap") else kvT
                for o in range(DC):
                    if what == "v":
                        mm = product(out[:, o * D:o * D + D], [kvT[:, p, c, o * P:o * P + P] for c in range(DC)],
                                     [W["wv"][:, c, :] for c in range(DC)])
                    else:
                        mm = product(out[:, o * S:o * S + S], [W["w" + what][:, c, o * P:o * P + P] for c in range(DC)],
                                     [src[:, p, c, :] for c in range(DC)])
                mm.then_inc({"k": k_ps, "q": q_ps, "v": v_ps, "k_swap": ks_ps, "q_swap": qs_ps}[what], 1)

            def score(b, p, pair, n, prev):
                qt, h0, g = n // PER_QT, n % PER_QT * 2, n % 2
                if n == 0:
                    pe.wait_ge(stack_in[p], 16 * n_in * (pair + 1))
                if n == 0 and groups is not None:
                    pe.wait_ge(m_in[p], 16 * 2 * (pair + 1))
                if n >= 2 or prev:
                    pe.wait_ge(bank_free, STEPS * b + n - 1)
                for e in range(2):
                    mm = nc.tensor.matmul(bank[g][:, e * S:e * S + S], stack[:, p, 1, h0 + e, qt * P:qt * P + P],
                                          stack[:, p, 0, h0 + e, :], start=True, stop=(groups is None))
                    if groups is not None:
                        mm = nc.tensor.matmul(bank[g][:, e * S:e * S + S], mq[:, p, qt * P:qt * P + P], mk[:, p, :],
                                              start=False, stop=True)
                mm.then_inc(sc_done, 1)

            def transposes(b, p, n):
                pe.wait_ge(prob_done, STEPS * b + n + 1)
                if n >= 2:
                    pe.wait_ge(pT_done, STEPS * b + n - 1)
                for kc in range(2):
                    for e in range(2):
                        mm = nc.tensor.transpose(psT[n % 2][:, kc, e, :], prob[:, n % 4, e, kc * P:kc * P + P],
                                                 ident[:])
                mm.then_inc(tr_done, 1)

            def values(b, p, n, prev=True):
                qt, h0, c = n // PER_QT, n % PER_QT * 2, n % PER_QT // 4
                pe.wait_ge(pT_done, STEPS * b + n + 1)
                if n % PER_QT == 0 and (n or prev):
                    pe.wait_ge(oT_done, QT * b + n // PER_QT)
                for e in range(2):
                    for kc in range(2):
                        mm = nc.tensor.matmul(psO[:, c * P:c * P + P], vp[:, p, kc, c, (h0 + e) % 8 * P:(h0 + e) % 8 * P + P], probT[:, n % 2, kc, e, :],
                                              start=(n % 4 == 0 and e == 0 and kc == 0),
                                              stop=(n % 4 == 3 and e == 1 and kc == 1))
                mm.then_inc(pv_done, 1)

            def registers_pe(b, p, n, prev):
                if n == 5:
                    if prev:
                        pe.wait_ge(x_done, QT * b)
                    pe.wait_ge(rg_set, b + 1)
                    for c in range(DC):
                        nc.tensor.matmul(psX[0:RG, 0:S], rg_q[:, c, :, :].rearrange("p h r -> p (h r)"), kT[:, p, c, :],
                                         start=(c == 0), stop=False)
                    nc.tensor.matmul(psX[0:RG, 0:S], rg_two[:], mk[0:2, p, :], start=False, stop=True).then_inc(rg_sc, 1)
                if n == 7:
                    pe.wait_ge(rg_prob, b + 1)
                    for kc in range(QT):
                        mm = nc.tensor.transpose(psX[:, D + kc * RG:D + kc * RG + RG], rg_p[:, kc * P:kc * P + P],
                                                 ident[0:RG, 0:RG])
                    mm.then_inc(rg_tr, 1)
                if n == 8:
                    pe.wait_ge(rg_read, b + 1)
                    for kc in range(QT):
                        mm = nc.tensor.matmul(psX[0:RG, 0:D], rg_pT[:, kc, :], v[:, p, kc, :], start=(kc == 0), stop=(kc == 1))
                    mm.then_inc(rg_pv, 1)
                if n == 9:
                    pe.wait_ge(rg_cut, b + 1)
                    for c in range(DC):
                        mm = nc.tensor.matmul(psX[:, D + c * REG:D + c * REG + REG], rg_o[:, c * P:c * P + P], rg_fold[:],
                                              start=True, stop=True)
                    mm.then_inc(rg_sum_ps, 1)

            def spread_sums(b, qt, prev=True):
                pe.wait_ge(inv_done, QT * b + qt + 1)
                if qt or prev:
                    pe.wait_ge(x_done, QT * b + qt)
                if groups is not None and qt == 0:
                    pe.wait_ge(rg_cut, b + 1)
                for c in range(DC):
                    mm = nc.tensor.matmul(psX[:, c * P:c * P + P],
                                          rinv[:, c * 8:c * 8 + 8, :].rearrange("p h d -> p (h d)"), ident[:],
                                          start=True, stop=True)
                mm.then_inc(rT_ps, 1)

            def out_project(b, qt):
                pe.wait_ge(oT_done, QT * b + qt + 1)
                product(psX[:, D:2 * D], [oT[:, c, :] for c in range(DC)],
                        [W["wo"][:, c, :] for c in range(DC)]).then_inc(out_ps, 1)

            def attend(b, p, pair, prev, following):
                if topk is not None and not prev:
                    score(b, p, pair, 0, prev)
                for n in range(STEPS):
                    if topk is None:
                        score(b, p, pair, n, prev)
                    elif n + 1 < STEPS:
                        score(b, p, pair, n + 1, prev)
                    elif following:
                        score(b + 1, 1 - p, pair + p, 0, True)
                    if n >= 2:
                        transposes(b, p, n - 2)
                    elif prev:
                        transposes(b - 1, 1 - p, STEPS + n - 2)
                    if n >= 3:
                        values(b, p, n - 3, prev)
                    elif prev:
                        values(b - 1, 1 - p, STEPS + n - 3)
                    if prev and n == 1:
                        spread_sums(b - 1, 1)
                    if prev and n == 3:
                        out_project(b - 1, 1)
                    if groups is not None:
                        registers_pe(b, p, n, prev)
                    if n == PER_QT + 1:
                        spread_sums(b, 0, prev)
                    if n == PER_QT + 4:
                        out_project(b, 0)
                    if following and n in made_at:
                        project(b + 1, 1 - p, pair + p, made[made_at.index(n)])

            pe.wait_ge(w_in, 16 * n_w)
            pe.wait_ge(vp_zero, 2)
            if groups is not None:
                pe.wait_ge(rg_mix, 1)
            for what in made:
                project(0, 0, 0, what, True)
            attend(0, 0, 0, False, True)
            with pe.Fori(0, B // 2 - 1) as i:
                for k in range(2):
                    attend(i * 2 + 1 + k, 1 - k, i + k, True, True)
            attend(B - 1, 1, B // 2 - 1, True, False)
            transposes(B - 1, 1, STEPS - 2)
            values(B - 1, 1, STEPS - 3)
            transposes(B - 1, 1, STEPS - 1)
            values(B - 1, 1, STEPS - 2)
            spread_sums(B - 1, 1)
            values(B - 1, 1, STEPS - 1)
            out_project(B - 1, 1)

        @block.gpsimd
        def _(pool):
            def whole(p, t):
                return (kT, qf)[t][:, p, :, :]

            def keep_rest(b, p, t):
                pool.wait_ge(cast_0, 2 * b + t + 1)
                nc.gpsimd.tensor_tensor(rest_of[:, t, :, :], whole(p, t), part[:, t, 0, :, :], ALU.subtract)\
                    .then_inc(rest_set, 1)

            def last_part(b, t):
                pool.wait_ge(cast_1, 2 * b + t + 1)
                nc.gpsimd.tensor_tensor(part[:, t, 2, :, :], rest_of[:, t, :, :], part[:, t, 1, :, :],
                                        ALU.subtract).then_inc(split, 1)

            def split_parts(b, p, step):
                if step in first_at:
                    keep_rest(b, p, first_at.index(step))
                if step in second_at:
                    last_part(b, second_at.index(step))

            def cap_scores(b, p, n, prev):
                qt = n // PER_QT
                if n == 0:
                    pool.wait_ge(m_cap, b + 1)
                if n or prev:
                    pool.wait_ge(capped, STEPS * b + n)
                pool.wait_ge(raw_set, STEPS * b + n + 1)
                nc.gpsimd.tensor_tensor(kept[:], raw_sc[:, n % 2, :, :],
                                        mone[:, p, qt, :].unsqueeze(1).to_broadcast([P, 2, S]), ALU.mult)\
                    .then_inc(kept_set, 1)
                pool.wait_ge(kept_set, STEPS * b + n + 1)
                if n >= 4 or prev:
                    pool.wait_ge(exp_done, STEPS * b + n - 3)
                    pool.wait_ge(marked, STEPS * b + n - 3)
                nc.gpsimd.tensor_tensor(sc_sb[:, n % 4, :, :], kept[:],
                                        mlow[:, p, qt, :].unsqueeze(1).to_broadcast([P, 2, S]), ALU.add)\
                    .then_inc(capped, 1)

            def pick(b, n, prev=True):
                pool.wait_ge(rest_done, STEPS * b + n + 1)
                if n >= 4 or prev:
                    pool.wait_ge(tr_done, STEPS * b + n - 3)
                nc.gpsimd.tensor_tensor(prob[:, n % 4, :, :], expd[:, n % 2, :, :], rest[:, n % 2, :, :],
                                        ALU.subtract).then_inc(picked, 1)

            def attend(b, p, prev, following):
                for n in range(STEPS):
                    if topk is not None:
                        cap_scores(b, p, n, prev)
                    if following:
                        split_parts(b + 1, 1 - p, n)
                    if topk is not None and n >= 2:
                        pick(b, n - 2, prev)
                    elif topk is not None and prev:
                        pick(b - 1, STEPS + n - 2)

            if groups is not None:
                for m in (mq, mk):
                    nc.gpsimd.memset(m[:], 0.0).then_inc(m_zero, 1)
            for q in range(2):
                nc.gpsimd.memset(vp[:, q, :, :, :].rearrange("p k c m -> p (k c m)"), 0.0).then_inc(vp_zero, 1)
            for n in range(STEPS):
                split_parts(0, 0, n)
            attend(0, 0, False, True)
            with pool.Fori(0, B // 2 - 1) as i:
                for k in range(2):
                    attend(i * 2 + 1 + k, 1 - k, True, True)
            if topk is not None:
                attend(B - 1, 1, True, False)
                pick(B - 1, STEPS - 2)
                pick(B - 1, STEPS - 1)

        @block.scalar
        def _(act):
            def read_q(b, p):
                if rope is not None:
                    return
                act.wait_ge(q_ps, b + 1)
                at_q = bank[2 + made.index("q") % 2]
                for c in range(DC):
                    if "bq" in Bc:
                        last = nc.scalar.activation(qf[:, p, c, :], at_q[:, c * S:c * S + S], ACT.Identity,
                                                    bias=bqs[:, c:c + 1], scale=scale)
                    else:
                        last = nc.scalar.activation(qf[:, p, c, :], at_q[:, c * S:c * S + S], ACT.Copy, scale=scale)
                last.then_inc(q_set, 1)

            def split_parts(b, p, step):
                for t, at in enumerate(first_at):
                    if step == at:
                        act.wait_ge((k_ev if rope is None else kt_set, q_set if rope is None else rot_step)[t], b + 1)
                        act.wait_ge(parts_out, 32 * b)
                        nc.scalar.activation(part[:, t, 0, :, :], (kT, qf)[t][:, p, :, :], ACT.Copy).then_inc(cast_0, 1)
                for t, at in enumerate(second_at):
                    if step == at:
                        act.wait_ge(rest_set, 2 * b + t + 1)
                        nc.scalar.activation(part[:, t, 1, :, :], rest_of[:, t, :, :], ACT.Copy).then_inc(cast_1, 1)

            def copy_transposes(b, n, prev=True):
                act.wait_ge(tr_done, STEPS * b + n + 1)
                if n >= 2 or prev:
                    act.wait_ge(pv_done, STEPS * b + n - 1)
                nc.scalar.activation(probT[:, n % 2, :, :, :].rearrange("p k e q -> p (k e q)"),
                                     psT[n % 2][:].rearrange("p k e q -> p (k e q)"), ACT.Copy).then_inc(pT_done, 1)

            def read_sums(b, qt, prev=True):
                act.wait_ge(rT_ps, QT * b + qt + 1)
                if qt or prev:
                    act.wait_ge(oT_done, QT * b + qt)
                nc.scalar.activation(rT[:].rearrange("p c n -> p (c n)"), psX[:, 0:D], ACT.Copy).then_inc(rT_done, 1)

            def copy_scores(b, n, prev=True):
                act.wait_ge(sc_done, STEPS * b + n + 1)
                if n >= 2 or prev:
                    act.wait_ge(kept_set, STEPS * b + n - 1)
                nc.scalar.activation(raw_sc[:, n % 2, :, :].rearrange("p e k -> p (e k)"), bank[n % 2][:], ACT.Copy)\
                    .then_inc(raw_set, 1)

            def attend(b, p, prev, following):
                if topk is not None and not prev:
                    copy_scores(b, 0, prev)
                for n in range(STEPS):
                    qt, h0 = n // PER_QT, n % PER_QT * 2
                    if following and n == made_at[2] + 2:
                        read_q(b + 1, 1 - p)
                    if prev and n == 2:
                        read_sums(b - 1, 1)
                    if n == PER_QT + 2:
                        read_sums(b, 0, prev)
                    if following:
                        split_parts(b + 1, 1 - p, n)
                    if topk is not None and n + 1 < STEPS:
                        copy_scores(b, n + 1, prev)
                    elif topk is not None and following:
                        copy_scores(b + 1, 0)
                    act.wait_ge(max_done, STEPS * b + n + 1)
                    if topk is not None:
                        if n >= 2 or prev:
                            act.wait_ge(picked, STEPS * b + n - 1)
                        for e in range(2):
                            h = h0 + e
                            last = nc.scalar.activation(expd[:, n % 2, e, :], sc_sb[:, n % 4, e, :], ACT.Exp,
                                                        bias=nmax[:, qt, h:h + 1])
                        last.then_inc(exp_done, 1)
                        if n >= 2:
                            copy_transposes(b, n - 2, prev)
                        elif prev:
                            copy_transposes(b - 1, STEPS + n - 2)
                        act.wait_ge(marked, STEPS * b + n + 1)
                        for e in range(2):
                            h = h0 + e
                            last = nc.scalar.activation(rest[:, n % 2, e, :], left[:, n % 2, e, :], ACT.Exp,
                                                        bias=nmax[:, qt, h:h + 1])
                        last.then_inc(rest_done, 1)
                        if n or prev:
                            act.wait_ge(sum_done, STEPS * b + n)
                        for e in range(2):
                            h = h0 + e
                            last = nc.scalar.activation(top_exp[:, e, :], top8[:, n % 2, e, :], ACT.Exp,
                                                        bias=nmax[:, qt, h:h + 1], accum_out=rsum[:, p, qt, h:h + 1])
                        last.then_inc(sum_done, 1)
                        continue
                    if n >= 4 or prev:
                        act.wait_ge(tr_done, STEPS * b + n - 3)
                    for e in range(2):
                        h = h0 + e
                        last = nc.scalar.activation(prob[:, n % 4, e, :], bank[n % 2][:, e * S:e * S + S], ACT.Exp,
                                                    bias=nmax[:, qt, h:h + 1], accum_out=rsum[:, p, qt, h:h + 1])
                    last.then_inc(exp_done, 1)
                    if groups is not None and n == 5:
                        act.wait_ge(rg_max, b + 1)
                        nc.scalar.activation(rg_e[:], psX[0:RG, 0:S], ACT.Exp, bias=rg_nmax[:, 0:1],
                                             accum_out=rg_sum[:, 0:1]).then_inc(rg_exp, 1)

            if "bq" in Bc:
                act.wait_ge(w_in, 16 * n_w)
                nc.scalar.activation(bqs[:], Bc["bq"][:], ACT.Copy, scale=scale).then_inc(bqs_set, 1)
                act.wait_ge(bqs_set, 1)
            read_q(0, 0)
            for n in range(STEPS):
                split_parts(0, 0, n)
            attend(0, 0, False, True)
            with act.Fori(0, B // 2 - 1) as i:
                for k in range(2):
                    attend(i * 2 + 1 + k, 1 - k, True, True)
            attend(B - 1, 1, True, False)
            if topk is not None:
                copy_transposes(B - 1, STEPS - 2)
                copy_transposes(B - 1, STEPS - 1)
            read_sums(B - 1, 1)

        @block.vector
        def _(dve):
            def read_mask(b, p, pair):
                if topk is None:
                    return
                dve.wait_ge(m_in[p], 16 * (pair + 1))
                raw, one, low = (a[:, p, :, :].rearrange("p q n -> p (q n)") for a in (mraw, mone, mlow))
                nc.vector.tensor_scalar(low, raw, 0.0, NEG, ALU.is_equal, ALU.mult)
                nc.vector.tensor_scalar(one, raw, 0.0, 1.0, ALU.not_equal, ALU.mult).then_inc(m_cap, 1)

            def normalise(b, p, reuse):
                if reuse:
                    dve.wait_ge(xT_ps, b - 1)
                for t in range(QT):
                    last = nc.vector.tensor_scalar(xn[:, p, t, :], x[:, b * QT + t, :], mean[:, bass.ds(b * QT + t, 1)],
                                                   rstd[:, bass.ds(b * QT + t, 1)], ALU.subtract, ALU.mult)
                last.then_inc(x_norm, 1)

            def heads_of(p, t):
                return vp[:, p, t, :, :].rearrange("p c (h m) -> p c h m", m=P + DK)[:, :, :, 0:DK]

            def read_product(b, p, what, reuse):
                at = bank[2 + made.index(what) % 2]
                turns = at[:].rearrange("p (c n) -> p c n", c=DC)
                if what == "xT":
                    dve.wait_ge(xT_ps, b + 1)
                    if reuse:
                        dve.wait_ge(q_ps if rope is None else qs_ps, b - 1)
                        if ctxT is None:
                            dve.wait_ge(v_ps, b - 1)
                    nc.vector.tensor_copy(xnT[:, p, :, :].rearrange("p c n -> p (c n)"), at[:]).then_inc(xT_ev, 1)
                if what == "v":
                    dve.wait_ge(v_ps, b + 1)
                    if reuse:
                        dve.wait_ge(pv_done, STEPS * (b - 1))
                    for t in range(QT):
                        src = at[:, t * D:t * D + D].rearrange("p (c h d) -> p c h d", c=DC, d=DK)
                        dst = heads_of(p, t)
                        if "bv" in Br:
                            last = nc.vector.tensor_tensor(dst, src, Br["bv"][:].rearrange("p (c h d) -> p c h d", c=DC, d=DK),
                                                           ALU.add)
                        else:
                            last = nc.vector.tensor_copy(dst, src)
                    if groups is not None:
                        last = nc.vector.tensor_copy(v[:, p, :, :].rearrange("p t n -> p (t n)"), at[:])
                    last.then_inc(v_ev, 1)
                if what == "k" and rope is None:
                    dve.wait_ge(k_ps, b + 1)
                    if reuse:
                        dve.wait_ge(split, 2 * (b - 1))
                        if groups is not None:
                            dve.wait_ge(rg_sc, b - 1)
                    for c in range(DC):
                        if "bk" in Bc:
                            last = nc.vector.tensor_scalar(kT[:, p, c, :], at[:, c * S:c * S + S], Bc["bk"][:, c:c + 1],
                                                           None, ALU.add)
                        else:
                            last = nc.vector.tensor_copy(kT[:, p, c, :], at[:, c * S:c * S + S])
                    last.then_inc(k_ev, 1)
                if rope is None:
                    return
                cos = cosT[:].unsqueeze(1).to_broadcast([P, DC, S])
                sin = sinT[:].unsqueeze(1).to_broadcast([P, DC, S])
                if what == "k":
                    dve.wait_ge(k_ps, b + 1)
                    dve.wait_ge(kt_set, b)
                    nc.vector.tensor_tensor(krot[:, 0, :, :], turns, cos, ALU.mult).then_inc(k_ev, 1)
                if what == "q":
                    dve.wait_ge(q_ps, b + 1)
                    dve.wait_ge(rot_step, b)
                    nc.vector.tensor_tensor(rot[:, 0, :, :], turns, cos, ALU.mult).then_inc(q_ev, 1)
                if what == "k_swap":
                    dve.wait_ge(ks_ps, b + 1)
                    nc.vector.tensor_tensor(krot[:, 1, :, :], turns, sin, ALU.mult).then_inc(ks_ev, 1)
                    dve.wait_ge(ks_ev, b + 1)
                    dve.wait_ge(k_ev, b + 1)
                    if reuse:
                        dve.wait_ge(split, 2 * (b - 1))
                    nc.vector.tensor_tensor(kT[:, p, :, :], krot[:, 0, :, :], krot[:, 1, :, :], ALU.add).then_inc(kt_set, 1)
                if what == "q_swap":
                    dve.wait_ge(qs_ps, b + 1)
                    nc.vector.tensor_tensor(rot[:, 1, :, :], turns, sin, ALU.mult).then_inc(qs_ev, 1)
                    dve.wait_ge(qs_ev, b + 1)
                    dve.wait_ge(q_ev, b + 1)
                    nc.vector.tensor_tensor(qf[:, p, :, :], rot[:, 0, :, :], rot[:, 1, :, :], ALU.add).then_inc(rot_step, 1)

            def mark_largest(b, p, n, prev):
                qt, h0 = n // PER_QT, n % PER_QT * 2
                if n >= 2 or prev:
                    dve.wait_ge(sum_done, STEPS * b + n - 1)
                dve.wait_ge(capped, STEPS * b + n + 1)
                nc.vector.tensor_copy(carrier[:], ident[:, 0:1]).then_inc(pick_step, 1)
                for r in range(TOPK // 8):
                    for e in range(2):
                        if r:
                            dve.wait_ge(pick_step, 4 * r + e)
                        nc.vector.max(top8[:, n % 2, e, 8 * r:8 * r + 8],
                                      sc_sb[:, n % 4, e, :] if r == 0 else left[:, n % 2, e, :]).then_inc(pick_step, 1)
                    for e in range(2):
                        dve.wait_ge(pick_step, 4 * r + 2 + e)
                        ins = nc.vector.match_replace(out=left[:, n % 2, e, :], in_to_replace=top8[:, n % 2, e, 8 * r:8 * r + 8],
                                                      in_values=sc_sb[:, n % 4, e, :] if r == 0 else left[:, n % 2, e, :],
                                                      imm_value=GONE)
                        if r < TOPK // 8 - 1:
                            ins.then_inc(pick_step, 1)
                        if r == 0 and e == 0:
                            dve.wait_ge(pick_step, 3)
                            nc.vector.tensor_scalar(nmax[:, qt, h0:h0 + 2], top8[:, n % 2, :, 0], -1.0, None, ALU.mult)\
                                .then_inc(max_done, 1)
                ins.then_inc(marked, 1)
                dve.sem_clear(pick_step)

            def row_max(b, n):
                qt, h0 = n // PER_QT, n % PER_QT * 2
                dve.wait_ge(sc_done, STEPS * b + n + 1)
                nc.vector.tensor_reduce(nmax[:, qt, h0:h0 + 2], bank[n % 2][:].rearrange("p (e k) -> p e k", e=2),
                                        AX.X, ALU.max, negate=True).then_inc(max_done, 1)

            def read_transposes(b, n, prev=True):
                dve.wait_ge(tr_done, STEPS * b + n + 1)
                if n >= 2 or prev:
                    dve.wait_ge(pv_done, STEPS * b + n - 1)
                nc.vector.tensor_copy(probT[:, n % 2, :, :, :].rearrange("p k e q -> p (k e q)"),
                                      psT[n % 2][:].rearrange("p k e q -> p (k e q)")).then_inc(pT_done, 1)

            def registers_dve(b, p, n):
                if n == 0:
                    dve.wait_ge(q_set, b + 1)
                    for c in range(DC):
                        ins = nc.vector.tensor_tensor(rg_q[:, c, :, :], qf[:, p, c, 0:REG].unsqueeze(1).to_broadcast([P, H, REG]),
                                                      rg_sel[:, c, :].unsqueeze(2).to_broadcast([P, H, REG]), ALU.mult)
                    ins.then_inc(rg_set, 1)
                if n == 5:
                    dve.wait_ge(rg_sc, b + 1)
                    nc.vector.tensor_reduce(rg_nmax[:], psX[0:RG, 0:S], AX.X, ALU.max, negate=True).then_inc(rg_max, 1)
                if n == 6:
                    dve.wait_ge(rg_exp, b + 1)
                    nc.vector.reciprocal(rg_inv[:], rg_sum[:]).then_inc(rg_step, 1)
                    dve.wait_ge(rg_step, 2 * b + 1)
                    nc.vector.tensor_scalar(rg_p[:], rg_e[:], rg_inv[:, 0:1], None, ALU.mult).then_inc(rg_prob, 1)
                if n == 7:
                    dve.wait_ge(rg_tr, b + 1)
                    nc.vector.tensor_copy(rg_pT[:].rearrange("p k m -> p (k m)"), psX[:, D:D + QT * RG]).then_inc(rg_read, 1)
                if n == 8:
                    dve.wait_ge(rg_pv, b + 1)
                    nc.vector.tensor_tensor(rg_o[:], psX[0:RG, 0:D], rg_own[:], ALU.mult).then_inc(rg_cut, 1)

            def registers_mean(b):
                dve.wait_ge(on_half, b + 1)
                dve.wait_ge(rg_sum_ps, b + 1)
                columns = oT[:, :, 0:REG]
                nc.vector.tensor_tensor(rg_x[:], psX[:, D:D + DC * REG].rearrange("p (c r) -> p c r", c=DC), columns,
                                        ALU.add).then_inc(rg_step, 1)
                dve.wait_ge(rg_step, 2 * b + 2)
                nc.vector.tensor_scalar(columns, rg_x[:], 0.5, None, ALU.mult).then_inc(oT_done, 1)

            def invert_sums(b, p, qt):
                dve.wait_ge(exp_done if topk is None else sum_done, STEPS * b + (qt + 1) * PER_QT)
                nc.vector.reciprocal(inv[:], rsum[:, p, qt, :]).then_inc(inv_set, 1)
                dve.wait_ge(inv_set, QT * b + qt + 1)
                nc.vector.tensor_copy(rinv[:], inv[:].unsqueeze(2).to_broadcast([P, H, DK])).then_inc(inv_done, 1)

            def normalise_out(b, qt):
                dve.wait_ge(rT_done, QT * b + qt + 1)
                dve.wait_ge(pv_done, STEPS * b + (qt + 1) * PER_QT)
                nc.vector.tensor_tensor(oT[:].rearrange("p c n -> p (c n)"), psO[:, 0:D], rT[:].rearrange("p c n -> p (c n)"),
                                        ALU.mult).then_inc(oT_done if groups is None or qt else on_half, 1)
                if groups is not None and qt == 0:
                    registers_mean(b)

            def add_out(b, qt):
                dve.wait_ge(out_ps, QT * b + qt + 1)
                xt = x[:, b * QT + qt, :]
                if "bo" in Br:
                    nc.vector.tensor_tensor(obias[:], psX[:, D:2 * D], Br["bo"][:], ALU.add).then_inc(out_b, 1)
                    dve.wait_ge(out_b, QT * b + qt + 1)
                    nc.vector.tensor_tensor(xt, obias[:], xt, ALU.add).then_inc(x_done, 1)
                else:
                    nc.vector.tensor_tensor(xt, psX[:, D:2 * D], xt, ALU.add).then_inc(x_done, 1)

            def attend(b, p, pair, prev, following):
                if following:
                    normalise(b + 1, 1 - p, prev)
                for n in range(STEPS):
                    if topk is None:
                        row_max(b, n)
                    else:
                        mark_largest(b, p, n, prev)
                    if prev and n == 0:
                        invert_sums(b - 1, 1 - p, 1)
                    if prev and n == 2:
                        normalise_out(b - 1, 1)
                    if n == PER_QT:
                        invert_sums(b, p, 0)
                    if n == PER_QT + 2:
                        normalise_out(b, 0)
                    if topk is None and n >= 2:
                        read_transposes(b, n - 2, prev)
                    elif topk is None and prev:
                        read_transposes(b - 1, STEPS + n - 2)
                    if prev and n == 4:
                        add_out(b - 1, 1)
                    if groups is not None:
                        registers_dve(b, p, n)
                    if n == PER_QT + 5:
                        add_out(b, 0)
                    if following and n == 1:
                        read_mask(b + 1, 1 - p, pair + p)
                    if following and n - 1 in made_at:
                        read_product(b + 1, 1 - p, made[made_at.index(n - 1)], prev)

            dve.wait_ge(w_in, 16 * n_w)
            dve.wait_ge(vp_zero, 2)
            if groups is not None:
                nc.vector.tensor_copy(rg_two[:], rg_one[:]).then_inc(rg_mix, 1)
            normalise(0, 0, False)
            read_mask(0, 0, 0)
            for what in made:
                read_product(0, 0, what, False)
            attend(0, 0, 0, False, True)
            with dve.Fori(0, B // 2 - 1) as i:
                for k in range(2):
                    attend(i * 2 + 1 + k, 1 - k, i + k, True, True)
            attend(B - 1, 1, B // 2 - 1, True, False)
            invert_sums(B - 1, 1, 1)
            if topk is None:
                read_transposes(B - 1, STEPS - 2)
                read_transposes(B - 1, STEPS - 1)
            normalise_out(B - 1, 1)
            add_out(B - 1, 1)

F = 1024
FC = F // P
E = 8
ROW_B1 = DC * F
ROW_1 = ROW_B1 + FC
ROW_B2 = FC * D
ROW_2 = ROW_B2 + D
SKIP = float(1 << 20)


def moe_blocks(k):
    n = NT * k + E - 1
    return n + n % 2


class Counted:

    def __init__(self, sem):
        self.sem, self.base = sem, 0


def moe(nc, dma, name, k_top, x, ident, rstd, mean, c, wr, br, table, slots_x, slots_y):
    NB, KT = moe_blocks(k_top), k_top * NT
    slots_x, slots_y = slots_x[0:NB * P, :], slots_y[0:NB * P, :]
    with Scope(nc, name) as o:
        slot = o.sb("slot", [P, KT], U32)
        gate = o.sb("gate", [P, k_top, NT])
        widx = o.sb("widx", [P, NB], U32)

        with Scope(nc, f"{name}_route") as s:
            wr_sb, br_sb = s.sb("wr", [P, DC, E]), s.sb("br", [P, E])
            zero = s.sb("zero", [P, 2 * D])
            xn = s.sb("xn", [P, NT, D])
            xT = s.sb("xT", [P, 2, DC, P])
            lg = s.sb("lg", [P, NT, E])
            ex = s.sb("ex", [P, NT, E])
            top = s.sb("top", [P, NT, 8])
            topi = s.sb("topi", [P, NT, 8], U32)
            idf = s.sb("idf", [P, k_top, NT])
            hot = s.sb("hot", [P, k_top, NT, E])
            tot = s.sb("tot", [P, KT, E])
            incl = s.sb("incl", [P, E, KT])
            pos = s.sb("pos", [P, E, KT])
            nb_i, nb_s = s.sb("nb_i", [P, E], I32), s.sb("nb_s", [P, E], I32)
            nb, nb_end, first = s.sb("nb", [P, E]), s.sb("nb_end", [P, E]), s.sb("first", [P, E])
            slot_f = s.sb("slot_f", [P, KT])
            ge = s.sb("ge", [P, NB, E])
            eid, same, widx_f = s.sb("eid", [P, NB]), s.sb("same", [P, NB]), s.sb("widx_f", [P, NB])
            ones = s.sb("ones", [P, KT])
            lg2 = s.sb("lg2", [P, NT, E])
            gsum = s.sb("gsum", [P, NT])
            psT = [s.ps(f"psT{i}", [P, 512]) for i in range(2)]
            psL = s.ps("psL", [P, 512])
            psR = s.ps("psR", [P, 512])
            w_in, zero_set, zeroed, x_norm, t_done, t_read, l_done = (
                s.sem(n) for n in ("w_in", "zero_set", "zeroed", "x_norm", "t_done", "t_read", "l_done"))
            step, hot_done, ranked, exp_in, exp_out = (
                s.sem(n) for n in ("step", "hot_done", "ranked", "exp_in", "exp_out"))
            scattered = dma["scattered"]
            slot_done = s.sem("slot_done")
            block = s.block()

            @block.sync
            def _(sp):
                sp.dma_start(wr_sb[:], wr.rearrange("(c p) e -> p c e", p=P)).then_inc(w_in, 16)
                sp.dma_start(br_sb[:], br).then_inc(w_in, 16)
                sp.wait_ge(zero_set, 1)
                for j in range(NB // 2):
                    sp.dma_start(slots_x[j * 2 * P:(j + 1) * 2 * P, :].rearrange("(p r) d -> p (r d)", r=2), zero[:])\
                        .then_inc(zeroed, 16)

            @block.tensor
            def _(pe):
                pe.wait_ge(w_in, 32)

                for t in range(NT + 1):
                    if t < NT:
                        pe.wait_ge(x_norm, t + 1)
                        if t >= 2:
                            pe.wait_ge(t_read, t - 1)
                        for c_ in range(DC):
                            mm = nc.tensor.transpose(psT[t % 2][:, c_ * P:c_ * P + P], xn[:, t, c_ * P:c_ * P + P], ident[:])
                        mm.then_inc(t_done, 1)
                    if t >= 1:
                        u = t - 1
                        pe.wait_ge(t_read, u + 1)
                        for c_ in range(DC):
                            mm = nc.tensor.matmul(psL[:, u * E:u * E + E], xT[:, u % 2, c_, :], wr_sb[:, c_, :],
                                                  start=(c_ == 0), stop=(c_ == DC - 1))
                        mm.then_inc(l_done, 1)
                pe.wait_ge(hot_done, 1)
                hot_rows = hot[:].rearrange("p k t e -> p (k t e)")
                nc.tensor.matmul(psR[:, 0:KT * E], c["before"][:], hot_rows, start=True, stop=True)
                nc.tensor.matmul(psR[:, 256:256 + KT * E], c["ones"][:], hot_rows, start=True, stop=True)\
                    .then_inc(ranked, 1)

            @block.scalar
            def _(act):
                def read_t(t, k, again):
                    act.wait_ge(t_done, t + 1)
                    if again:
                        act.wait_ge(l_done, t - 1)
                    nc.scalar.activation(xT[:, k, :, :].rearrange("p c n -> p (c n)"), psT[k][:, 0:D], ACT.Copy)\
                        .then_inc(t_read, 1)

                read_t(0, 0, False)
                read_t(1, 1, False)
                with act.Fori(1, NT // 2) as i:
                    for k in range(2):
                        read_t(i * 2 + k, k, True)
                act.wait_ge(exp_in, 1)
                if k_top == 1:
                    nc.scalar.activation(ex[:], lg2[:], ACT.Exp).then_inc(exp_out, 1)
                else:
                    nc.scalar.activation(ex[:, :, 0], lg2[:, :, 0], ACT.Exp).then_inc(exp_out, 1)

            @block.gpsimd
            def _(pool):
                pool.wait_ge(slot_done, 1)
                pool.wait_ge(x_norm, NT)
                pool.wait_ge(zeroed, 16 * (NB // 2))
                for k in range(k_top):
                    for t in range(NT):
                        pool.indirect_dma_start(
                            out=slots_x, out_offset=bass.IndirectOffsetOnAxis(ap=slot[:, k * NT + t:k * NT + t + 1], axis=0),
                            in_=xn[:, t, :], in_offset=None).then_inc(scattered.sem, 16)
                pool.wait_ge(scattered.sem, scattered.base + 16 * KT)

            @block.vector
            def _(dve):
                n_steps = [0]

                def then(ins):
                    n_steps[0] += 1
                    ins.then_inc(step, 1)
                    dve.wait_ge(step, n_steps[0])

                nc.vector.memset(zero[:], 0.0).then_inc(zero_set, 1)

                for t in range(NT):
                    nc.vector.tensor_scalar(xn[:, t, :], x[:, t, :], mean[:, t:t + 1], rstd[:, t:t + 1],
                                            ALU.subtract, ALU.mult).then_inc(x_norm, 1)
                dve.wait_ge(l_done, NT)
                then(nc.vector.tensor_tensor(lg[:], psL[:, 0:NT * E].rearrange("p (t e) -> p t e", e=E),
                                             br_sb[:].unsqueeze(1).to_broadcast([P, NT, E]), ALU.add))
                for t in range(NT):
                    ins = nc.vector.max(top[:, t, :], lg[:, t, :])
                then(ins)
                for t in range(NT):
                    ins = nc.vector.max_index(topi[:, t, :], top[:, t, :], lg[:, t, :])
                then(ins)
                if k_top == 1:
                    nc.vector.tensor_tensor(lg2[:], lg[:], top[:, :, 0:1].to_broadcast([P, NT, E]),
                                            ALU.subtract).then_inc(exp_in, 1)
                else:
                    nc.vector.tensor_tensor(lg2[:, :, 0], top[:, :, 1], top[:, :, 0], ALU.subtract).then_inc(exp_in, 1)
                for k in range(k_top):
                    ins = nc.vector.tensor_copy(idf[:, k, :], topi[:, :, k])
                then(ins)
                for k in range(k_top):
                    ins = nc.vector.tensor_tensor(hot[:, k, :, :], c["iota"][:, 0:E].unsqueeze(1).to_broadcast([P, NT, E]),
                                                  idf[:, k, :].unsqueeze(2).to_broadcast([P, NT, E]), ALU.is_equal)
                ins.then_inc(hot_done, 1)
                then(nc.vector.memset(ones[:], 1.0))
                dve.wait_ge(exp_out, 1)
                if k_top == 1:
                    then(nc.vector.tensor_reduce(gsum[:], ex[:], AX.X, ALU.add))
                    then(nc.vector.reciprocal(gate[:, 0, :], gsum[:]))
                else:
                    then(nc.vector.tensor_scalar(gsum[:], ex[:, :, 0], 1.0, None, ALU.add))
                    then(nc.vector.reciprocal(gate[:, 0, :], gsum[:]))
                    then(nc.vector.tensor_tensor(gate[:, 1, :], gate[:, 0, :], ex[:, :, 0], ALU.mult))
                dve.wait_ge(ranked, 1)
                then(nc.vector.tensor_copy(tot[:].rearrange("p n e -> p (n e)"), psR[:, 256:256 + KT * E]))
                for e in range(E):
                    ins = nc.vector.tensor_tensor_scan(incl[:, e, :], ones[:], tot[:, :, e], 0.0, ALU.mult, ALU.add)
                then(ins)
                then(nc.vector.tensor_scalar(nb_i[:], incl[:, :, KT - 1], float(P - 1), None, ALU.add))
                then(nc.vector.tensor_single_scalar(nb_s[:], nb_i[:], 7, ALU.arith_shift_right))
                then(nc.vector.tensor_copy(nb[:], nb_s[:]))
                then(nc.vector.tensor_tensor_scan(nb_end[:], ones[:, 0:E], nb[:], 0.0, ALU.mult, ALU.add))
                then(nc.vector.tensor_tensor(first[:], nb_end[:], nb[:], ALU.subtract))
                then(nc.vector.tensor_scalar(first[:], first[:], float(P), None, ALU.mult))
                then(nc.vector.tensor_tensor(pos[:], incl[:], tot[:].rearrange("p n e -> p e n"), ALU.subtract))
                then(nc.vector.tensor_tensor(pos[:], psR[:, 0:KT * E].rearrange("p (n e) -> p e n", e=E), pos[:], ALU.add))
                then(nc.vector.tensor_tensor(pos[:], pos[:], first[:].unsqueeze(2).to_broadcast([P, E, KT]), ALU.add))
                then(nc.vector.tensor_tensor(pos[:], pos[:], hot[:].rearrange("p k t e -> p e (k t)"), ALU.mult))
                then(nc.vector.tensor_reduce(slot_f[:], pos[:].rearrange("p e n -> p n e"), AX.X, ALU.add))
                nc.vector.tensor_copy(slot[:], slot_f[:]).then_inc(slot_done, 1)
                then(nc.vector.tensor_tensor(ge[:], c["iota"][:, 0:NB].unsqueeze(2).to_broadcast([P, NB, E]),
                                             nb_end[:].unsqueeze(1).to_broadcast([P, NB, E]), ALU.is_ge))
                then(nc.vector.tensor_reduce(eid[:], ge[:], AX.X, ALU.add))
                then(nc.vector.tensor_scalar(eid[:], eid[:], float(E - 1), None, ALU.min))
                then(nc.vector.memset(same[:], 0.0))
                then(nc.vector.tensor_tensor(same[:, 2:NB], eid[:, 2:NB], eid[:, 0:NB - 2], ALU.is_equal))
                then(nc.vector.tensor_scalar(widx_f[:], eid[:], float(P), c["lane"][:, 0:1], ALU.mult, ALU.add))
                then(nc.vector.scalar_tensor_tensor(out=widx_f[:], in0=same[:], scalar=SKIP, in1=widx_f[:],
                                                    op0=ALU.mult, op1=ALU.add))
                nc.vector.tensor_copy(widx[:], widx_f[:])

        dma["scattered"].base += 16 * KT

        with Scope(nc, f"{name}_ffn") as s:
            wt1, wt2 = s.sb("wt1", [P, 2, ROW_1]), s.sb("wt2", [P, 2, ROW_2])
            idx, none = s.sb("idx", [P, 2, 2], U32), s.sb("none", [P, 1], U32)
            xs = s.sb("xs", [P, 2, D])
            xsT = s.sb("xsT", [P, 2, DC, P])
            hT = s.sb("hT", [P, 2, FC, P])
            y = s.sb("y", [P, 2, D])
            psT = s.ps("psT", [P, 512])
            psH = [s.ps(f"psH{i}", [P, 4, P]) for i in range(4)]
            psY = [s.ps(f"psY{i}", [P, 512]) for i in range(2)]
            idx_set, t_done, t_read, h_done, g_done, y_ps, y_done = (
                s.sem(n) for n in ("idx_set", "t_done", "t_read", "h_done", "g_done", "y_ps", "y_done"))
            x_in, y_out = ([s.sem(f"{n}{p}") for p in range(2)] for n in ("x_in", "y_out"))
            w1_in, w2_in = dma["fetched_w1"], dma["fetched_w2"]
            block = s.block()
            w1 = [[[wt1[:, p, c_ * F + f * P:c_ * F + f * P + P] for f in range(FC)] for c_ in range(DC)] for p in range(2)]
            w2 = [[wt2[:, p, f * D:f * D + D] for f in range(FC)] for p in range(2)]

            @block.gpsimd
            def _(pool):
                last_row = pool.to_reg(E * P - 1)

                def fetch(j, p, pair, again):
                    if again:
                        pool.wait_ge(w2_in[p].sem, w2_in[p].base + 16 * pair)
                        pool.wait_ge(w1_in[p].sem, w1_in[p].base + 16 * pair)
                        pool.wait_ge(g_done, FC * (j - 1))
                    nc.gpsimd.tensor_copy(idx[:, p, 0:1], widx[:, bass.ds(j, 1)]).then_inc(idx_set, 1)
                    pool.wait_ge(idx_set, 1)
                    pool.indirect_dma_start(out=wt1[:, p, :], out_offset=None, in_=table[0],
                                            in_offset=bass.IndirectOffsetOnAxis(ap=idx[:, p, 0:1], axis=0),
                                            bounds_check=last_row, oob_is_err=False).then_inc(w1_in[p].sem, 16)
                    if again:
                        pool.wait_ge(y_done, j - 1)
                    nc.gpsimd.tensor_tensor(idx[:, p, 1:2], idx[:, p, 0:1], none[:], ALU.add).then_inc(idx_set, 1)
                    pool.wait_ge(idx_set, 2)
                    pool.sem_clear(idx_set)
                    pool.indirect_dma_start(out=wt2[:, p, :], out_offset=None, in_=table[1],
                                            in_offset=bass.IndirectOffsetOnAxis(ap=idx[:, p, 1:2], axis=0),
                                            bounds_check=last_row, oob_is_err=False).then_inc(w2_in[p].sem, 16)

                nc.gpsimd.memset(none[:], 0).then_inc(idx_set, 1)
                pool.wait_ge(idx_set, 1)
                pool.sem_clear(idx_set)
                fetch(0, 0, 0, False)
                fetch(1, 1, 0, False)
                with pool.Fori(1, NB // 2) as i:
                    for k in range(2):
                        fetch(i * 2 + k, k, i, True)

            @block.sync
            def _(sp):
                def load(j, p, again):
                    if again:
                        sp.wait_ge(t_done, j - 1)
                    sp.dma_start(xs[:, p, :], slots_x[bass.ds(j * P, P), :]).then_inc(x_in[p], 16)

                def store(j, p):
                    sp.wait_ge(y_done, j + 1)
                    sp.dma_start(slots_y[bass.ds(j * P, P), :], y[:, p, :]).then_inc(y_out[p], 16)

                load(0, 0, False)
                load(1, 1, False)
                with sp.Fori(0, NB // 2 - 1) as i:
                    for k in range(2):
                        load(i * 2 + k + 2, k, True)
                        store(i * 2 + k, k)
                store(NB - 2, 0)
                store(NB - 1, 1)
                for k in range(2):
                    sp.wait_ge(y_out[k], 16 * (NB // 2))

            @block.tensor
            def _(pe):
                def up(j, p, pair, again):
                    pe.wait_ge(x_in[p], 16 * (pair + 1))
                    pe.wait_ge(t_read, j)
                    for c_ in range(DC):
                        mm = nc.tensor.transpose(psT[:, c_ * P:c_ * P + P], xs[:, p, c_ * P:c_ * P + P], ident[:])
                    mm.then_inc(t_done, 1)
                    pe.wait_ge(t_read, j + 1)
                    pe.wait_ge(w1_in[p].sem, w1_in[p].base + 16 * (pair + 1))
                    if again:
                        pe.wait_ge(g_done, FC * (j - 1))
                    for f in range(FC):
                        for c_ in range(DC):
                            mm = nc.tensor.matmul(psH[2 * p + f // 4][:, f % 4, :], w1[p][c_][f], xsT[:, p, c_, :],
                                                  start=(c_ == 0), stop=(c_ == DC - 1))
                        if f % 4 == 3:
                            mm.then_inc(h_done, 1)

                def down(j, p, pair, again):
                    pe.wait_ge(w2_in[p].sem, w2_in[p].base + 16 * (pair + 1))
                    if again:
                        pe.wait_ge(y_done, j - 1)
                    for f in range(FC):
                        pe.wait_ge(g_done, FC * j + f + 1)
                        mm = nc.tensor.matmul(psY[p][:, 0:D], hT[:, p, f, :], w2[p][f], start=(f == 0), stop=(f == FC - 1))
                    mm.then_inc(y_ps, 1)

                up(0, 0, 0, False)
                up(1, 1, 0, False)
                down(0, 0, 0, False)
                up(2, 0, 1, True)
                down(1, 1, 0, False)
                with pe.Fori(1, NB // 2 - 1) as i:
                    up(i * 2 + 1, 1, i, True)
                    down(i * 2, 0, i, True)
                    up(i * 2 + 2, 0, i + 1, True)
                    down(i * 2 + 1, 1, i, True)
                up(NB - 1, 1, NB // 2 - 1, True)
                down(NB - 2, 0, NB // 2 - 1, True)
                down(NB - 1, 1, NB // 2 - 1, True)

            @block.scalar
            def _(act):
                def gelu(j, p, again):
                    if again:
                        act.wait_ge(y_ps, j - 1)
                    for f in range(FC):
                        if f % 4 == 0:
                            act.wait_ge(h_done, 2 * j + f // 4 + 1)
                        nc.scalar.activation(hT[:, p, f, :], psH[2 * p + f // 4][:, f % 4, :], ACT.Gelu,
                                             bias=wt1[:, p, ROW_B1 + f:ROW_B1 + f + 1]).then_inc(g_done, 1)

                gelu(0, 0, False)
                gelu(1, 1, False)
                with act.Fori(1, NB // 2) as i:
                    for k in range(2):
                        gelu(i * 2 + k, k, True)

            @block.vector
            def _(dve):
                def read_t(j, p, again):
                    dve.wait_ge(t_done, j + 1)
                    if again:
                        dve.wait_ge(h_done, 2 * (j - 1))
                    nc.vector.tensor_copy(xsT[:, p, :, :].rearrange("p c n -> p (c n)"), psT[:, 0:D]).then_inc(t_read, 1)

                def add_b2(j, p, pair, again):
                    dve.wait_ge(y_ps, j + 1)
                    if again:
                        dve.wait_ge(y_out[p], 16 * pair)
                    nc.vector.tensor_tensor(y[:, p, :], psY[p][:, 0:D], wt2[:, p, ROW_B2:ROW_B2 + D], ALU.add)\
                        .then_inc(y_done, 1)

                read_t(0, 0, False)
                read_t(1, 1, False)
                add_b2(0, 0, 0, False)
                read_t(2, 0, True)
                add_b2(1, 1, 0, False)
                with dve.Fori(1, NB // 2 - 1) as i:
                    read_t(i * 2 + 1, 1, True)
                    add_b2(i * 2, 0, i, True)
                    read_t(i * 2 + 2, 0, True)
                    add_b2(i * 2 + 1, 1, i, True)
                read_t(NB - 1, 1, True)
                add_b2(NB - 2, 0, NB // 2 - 1, True)
                add_b2(NB - 1, 1, NB // 2 - 1, True)

        for p in range(2):
            dma["fetched_w1"][p].base += 16 * (NB // 2)
            dma["fetched_w2"][p].base += 16 * (NB // 2)

        with Scope(nc, f"{name}_back") as s:
            yb = s.sb("yb", [P, KT, D])
            back = dma["back"]
            added = s.sem("added")
            block = s.block()

            @block.gpsimd
            def _(pool):
                for t in range(NT):
                    for k in range(k_top):
                        n = k * NT + t
                        pool.indirect_dma_start(out=yb[:, n, :], out_offset=None, in_=slots_y,
                                                in_offset=bass.IndirectOffsetOnAxis(ap=slot[:, n:n + 1], axis=0))\
                            .then_inc(back[t].sem, 16)

            @block.vector
            def _(dve):
                for k in range(k_top):
                    for t in range(NT):
                        if k == 0:
                            dve.wait_ge(back[t].sem, back[t].base + 16 * k_top)
                        else:
                            dve.wait_ge(added, t + 1)
                        nc.vector.scalar_tensor_tensor(out=x[:, t, :], in0=yb[:, k * NT + t, :], scalar=gate[:, k, t:t + 1],
                                                       in1=x[:, t, :], op0=ALU.mult, op1=ALU.add).then_inc(added, 1)
        for t in range(NT):
            dma["back"][t].base += 16 * k_top


CH = 16
PAIRS = S // (2 * CH)
W1C = S + 1


def alignment(nc, x, ident, rstd, mean, consts, ctx, ctxT, dist, cost, table):
    with Scope(nc, "dtw") as o:
        ctx_sb = o.sb("ctx", [P, NT, D])
        ctx_in = o.sem("ctx_in")

        with Scope(nc, "dist") as s:
            aa = s.sb("aa", [P, NT])
            xn = s.sb("xn", [P, 2, QT, D])
            xm2, xsq = s.sb("xm2", [P, 2, DC, S]), s.sb("xsq", [P, 2, DC, S])
            aT = s.sb("aT", [P, 2, DC, S])
            d2, dd = s.sb("d2", [P, 2, QT, S]), s.sb("dd", [P, 2, QT, S])
            junk = s.sb("junk", [P, 2, D])
            psT = [s.ps(f"psT{i}", [P, 512]) for i in range(2)]
            psD = [s.ps(f"psD{i}", [P, 512]) for i in range(2)]
            a_in, d_out = ([s.sem(f"{n}{p}") for p in range(2)] for n in ("a_in", "d_out"))
            x_norm, t_done, m2_done, sq_done, d_ps, d2_done, dd_done, aa_done = (
                s.sem(n) for n in ("x_norm", "t_done", "m2_done", "sq_done", "d_ps", "d2_done", "dd_done", "aa_done"))
            block = s.block()

            @block.sync
            def _(sp):
                sp.dma_start(ctx_sb[:], ctx.rearrange("b (t p) d -> p (b t) d", p=P)).then_inc(ctx_in, 16)

                def load(b, p, again):
                    if again:
                        sp.wait_ge(d_ps, b - 1)
                    sp.dma_start(aT[:, p, :, :], ctxT[:, :, bass.ds(b * S, S)].rearrange("c p n -> p c n"))\
                        .then_inc(a_in[p], 16)

                def store(b, p):
                    sp.wait_ge(dd_done, b + 1)
                    sp.dma_start(dist[bass.ds(b, 1), :, :].rearrange("b (t p) j -> p (b t) j", p=P), dd[:, p, :, :])\
                        .then_inc(d_out[p], 16)

                load(0, 0, False)
                load(1, 1, False)
                with sp.Fori(0, B // 2 - 1) as i:
                    for k in range(2):
                        load(i * 2 + k + 2, k, True)
                        store(i * 2 + k, k)
                store(B - 2, 0)
                store(B - 1, 1)
                for k in range(2):
                    sp.wait_ge(d_out[k], 16 * (B // 2))
                sp.wait_ge(ctx_in, 16)

            @block.tensor
            def _(pe):
                def batch(b, p, pair, again):
                    pe.wait_ge(x_norm, b + 1)
                    if again:
                        pe.wait_ge(sq_done, b - 1)
                    for c in range(DC):
                        for t in range(QT):
                            mm = nc.tensor.transpose(psT[p][:, c * S + t * P:c * S + t * P + P],
                                                     xn[:, p, t, c * P:c * P + P], ident[:])
                    mm.then_inc(t_done, 1)
                    pe.wait_ge(a_in[p], 16 * (pair + 1))
                    pe.wait_ge(m2_done, b + 1)
                    pe.wait_ge(sq_done, b + 1)
                    if again:
                        pe.wait_ge(d2_done, b - 1)
                    for t in range(QT):
                        out = psD[p][:, t * S:t * S + S]
                        for c in range(DC):
                            nc.tensor.matmul(out, aT[:, p, c, t * P:t * P + P], xm2[:, p, c, :], start=(c == 0), stop=False)
                        for c in range(DC):
                            mm = nc.tensor.matmul(out, consts["ones"][:], xsq[:, p, c, :], start=False, stop=(c == DC - 1))
                    mm.then_inc(d_ps, 1)

                batch(0, 0, 0, False)
                batch(1, 1, 0, False)
                with pe.Fori(1, B // 2) as i:
                    for k in range(2):
                        batch(i * 2 + k, k, i, True)

            @block.scalar
            def _(act):
                act.wait_ge(ctx_in, 16)
                for t in range(NT):
                    if t >= 2:
                        act.wait_ge(aa_done, t - 1)
                    nc.scalar.activation(junk[:, t % 2, :], ctx_sb[:, t, :], ACT.Square,
                                         accum_out=aa[:, t:t + 1]).then_inc(aa_done, 1)

                def batch(b, p, pair):
                    act.wait_ge(t_done, b + 1)
                    act.wait_ge(m2_done, b + 1)
                    nc.scalar.activation(xsq[:, p, :, :].rearrange("p c n -> p (c n)"), psT[p][:], ACT.Square)\
                        .then_inc(sq_done, 1)
                    act.wait_ge(d2_done, b + 1)
                    act.wait_ge(d_out[p], 16 * pair)
                    nc.scalar.activation(dd[:, p, :, :], d2[:, p, :, :], ACT.Sqrt).then_inc(dd_done, 1)

                batch(0, 0, 0)
                batch(1, 1, 0)
                with act.Fori(1, B // 2) as i:
                    for k in range(2):
                        batch(i * 2 + k, k, i)

            @block.vector
            def _(dve):
                def normalise(b, p):
                    for t in range(QT):
                        ins = nc.vector.tensor_scalar(xn[:, p, t, :], x[:, b * QT + t, :], mean[:, bass.ds(b * QT + t, 1)],
                                                      rstd[:, bass.ds(b * QT + t, 1)], ALU.subtract, ALU.mult)
                    ins.then_inc(x_norm, 1)

                def batch(b, p, again):
                    dve.wait_ge(t_done, b + 1)
                    if again:
                        dve.wait_ge(d_ps, b - 1)
                    nc.vector.tensor_scalar(xm2[:, p, :, :].rearrange("p c n -> p (c n)"), psT[p][:], -2.0, None,
                                            ALU.mult).then_inc(m2_done, 1)
                    dve.wait_ge(d_ps, b + 1)
                    if again:
                        dve.wait_ge(dd_done, b - 1)
                    for t in range(QT):
                        ins = nc.vector.tensor_scalar(d2[:, p, t, :], psD[p][:, t * S:t * S + S],
                                                      aa[:, bass.ds(b * QT + t, 1)], 0.0, ALU.add, ALU.max)
                    ins.then_inc(d2_done, 1)

                dve.wait_ge(aa_done, NT)
                normalise(0, 0)
                normalise(1, 1)
                batch(0, 0, False)
                batch(1, 1, False)
                with dve.Fori(1, B // 2) as i:
                    for k in range(2):
                        normalise(i * 2 + k, k)
                        batch(i * 2 + k, k, True)

        with Scope(nc, "cost") as s:
            drow = s.sb("drow", [B, 2, CH, S])
            r = s.sb("r", [B, 2 * CH + 1, W1C])
            near = s.sb("near", [B, 2, S])
            edge = s.sb("edge", [B, W1C])
            d_in, r_out = ([s.sem(f"{n}{p}") for p in range(2)] for n in ("d_in", "r_out"))
            step, edge_out, edge_set = s.sem("step"), s.sem("edge_out"), s.sem("edge_set")
            per_round = 2 * 2 * CH + 1
            block = s.block()

            @block.sync
            def _(sp):
                sp.wait_ge(edge_set, 1)
                sp.dma_start(cost[:, 0, :], edge[:]).then_inc(edge_out, 16)

                def load(i, k):
                    sp.dma_start(drow[:, k, :, :], dist[:, bass.ds((i * 2 + k) * CH, CH), :]).then_inc(d_in[k], 16)

                def store(i, k):
                    sp.wait_ge(step, per_round * i + 2 * CH * (k + 1))
                    sp.dma_start(cost[:, bass.ds((i * 2 + k) * CH + 1, CH), :], r[:, 1 + k * CH:1 + (k + 1) * CH, :])\
                        .then_inc(r_out[k], 16)

                load(0, 0)
                load(0, 1)
                with sp.Fori(0, PAIRS - 1) as i:
                    for k in range(2):
                        store(i, k)
                        sp.wait_ge(r_out[k], 16 * (i + 1))
                        load(i + 1, k)
                store(PAIRS - 1, 0)
                store(PAIRS - 1, 1)
                for k in range(2):
                    sp.wait_ge(r_out[k], 16 * PAIRS)
                sp.wait_ge(edge_out, 16)

            @block.vector
            def _(dve):
                nc.vector.memset(edge[:], BIG).then_inc(edge_set, 1)
                nc.vector.memset(r[:], BIG).then_inc(edge_set, 1)
                dve.wait_ge(edge_set, 2)
                nc.vector.memset(r[:, 0, 0:1], 0.0).then_inc(edge_set, 1)
                dve.wait_ge(edge_set, 3)
                with dve.Fori(0, PAIRS) as i:
                    for n in range(2 * CH):
                        k = n // CH
                        if n % CH == 0:
                            dve.wait_ge(d_in[k], 16 * (i + 1))
                        nc.vector.tensor_tensor(near[:, n % 2, :], r[:, n, 1:W1C], r[:, n, 0:S], ALU.min)\
                            .then_inc(step, 1)
                        dve.wait_ge(step, per_round * i + 2 * n + 1)
                        nc.vector.tensor_tensor_scan(r[:, n + 1, 1:W1C], near[:, n % 2, :], drow[:, k, n % CH, :], BIG,
                                                     ALU.min, ALU.add).then_inc(step, 1)
                        dve.wait_ge(step, per_round * i + 2 * n + 2)
                    nc.vector.tensor_copy(r[:, 0, :], r[:, 2 * CH, :]).then_inc(step, 1)
                    dve.wait_ge(step, per_round * (i + 1))

        with Scope(nc, "path") as o2:
            start = o2.sb("start", [P, QT, B, S])
            ends = o2.sb("ends", [B, S])
            NB8 = B * S

            with Scope(nc, "back") as s:
                here, up = s.sb("here", [P, B, W1C]), s.sb("up", [P, B, W1C])
                best, left = s.sb("best", [P, B, S]), s.sb("left", [P, B, S])
                stay, where = s.sb("stay", [P, B, S]), s.sb("where", [P, B, S])
                tab = s.sb("tab", [P, QT, B, S], BF16)
                r_in, t_out, step = s.sem("r_in"), s.sem("t_out"), s.sem("step")
                block = s.block()

                @block.sync
                def _(sp):
                    for q in range(QT):
                        if q:
                            sp.wait_ge(step, 9 * q)
                        sp.dma_start(here[:], cost[:, 1 + q * P:1 + q * P + P, :].rearrange("b p j -> p b j")).then_inc(r_in, 16)
                        sp.dma_start(up[:], cost[:, q * P:q * P + P, :].rearrange("b p j -> p b j")).then_inc(r_in, 16)
                    sp.wait_ge(step, 9 * QT)
                    for q in range(QT):
                        sp.dma_start(table[:, q * P:q * P + P, :].rearrange("b p j -> p b j"), tab[:, q, :, :]).then_inc(t_out, 16)
                    sp.wait_ge(t_out, 16 * QT)

                @block.vector
                def _(dve):
                    n = [0]

                    def then(ins):
                        n[0] += 1
                        ins.then_inc(step, 1)
                        dve.wait_ge(step, n[0])

                    def flat(t):
                        return t.rearrange("p b j -> p (b j)")

                    iota = consts["iota"][:].unsqueeze(1).to_broadcast([P, B, S])
                    for q in range(QT):
                        dve.wait_ge(r_in, 32 * (q + 1))
                        diag, above, before = up[:, :, 0:S], up[:, :, 1:W1C], here[:, :, 0:S]
                        then(nc.vector.tensor_tensor(best[:], diag, above, ALU.min))
                        then(nc.vector.tensor_tensor(left[:], best[:], before, ALU.is_gt))
                        then(nc.vector.tensor_scalar(flat(stay[:]), flat(left[:]), -1.0, 1.0, ALU.mult, ALU.add))
                        then(nc.vector.tensor_tensor(where[:], stay[:], iota, ALU.mult))
                        then(nc.vector.tensor_tensor_scan(flat(start[:, q, :, :]), flat(left[:]), flat(where[:]), 0.0,
                                                          ALU.mult, ALU.add))
                        then(nc.vector.tensor_tensor(best[:], diag, above, ALU.is_le))
                        then(nc.vector.tensor_tensor(best[:], best[:], stay[:], ALU.mult))
                        then(nc.vector.tensor_tensor(where[:], where[:], best[:], ALU.subtract))
                        then(nc.vector.tensor_tensor_scan(flat(tab[:, q, :, :]), flat(left[:]), flat(where[:]), 0.0,
                                                          ALU.mult, ALU.add))

            with Scope(nc, "walk") as s:
                trow = s.sb("trow", [B, 2, CH, S], BF16)
                pick = s.sb("pick", [B, 2, S])
                t_in = [s.sem(f"t_in{p}") for p in range(2)]
                step = s.sem("step")
                n_chunks = S // CH
                block = s.block()

                @block.sync
                def _(sp):
                    for n in range(n_chunks):
                        if n >= 2:
                            sp.wait_ge(step, 1 + CH * (n - 1))
                        c0 = (n_chunks - 1 - n) * CH
                        sp.dma_start(trow[:, n % 2, :, :], table[:, c0:c0 + CH, :]).then_inc(t_in[n % 2], 16)

                @block.vector
                def _(dve):
                    nc.vector.memset(ends[:, S - 1:S], float(S - 1)).then_inc(step, 1)
                    for n in range(n_chunks):
                        dve.wait_ge(t_in[n % 2], 16 * (n // 2 + 1))
                        for m in range(CH):
                            i = S - 1 - n * CH - m
                            if i == 0:
                                continue
                            dve.wait_ge(step, S - i)
                            nc.vector.scalar_tensor_tensor(out=pick[:, i % 2, :], in0=consts["iota"][0:B, :],
                                                           scalar=ends[:, i:i + 1], in1=trow[:, n % 2, CH - 1 - m, :],
                                                           op0=ALU.is_equal, op1=ALU.mult,
                                                           accum_out=ends[:, i - 1:i]).then_inc(step, 1)

            with Scope(nc, "lay") as s:
                last, first = s.sb("last", [P, QT, B]), s.sb("first", [P, QT, B])
                pick = s.sb("pick", [P, 2, S])
                after, on = s.sb("after", [P, 2, QT, S]), s.sb("on", [P, 2, QT, S])
                psE = s.ps("psE", [P, QT, B])
                psA = [s.ps(f"psA{i}", [P, QT, D]) for i in range(2)]
                e_done, e_read, found, cut, laid, spread, added = (
                    s.sem(n) for n in ("e_done", "e_read", "found", "cut", "laid", "spread", "added"))
                block = s.block()

                @block.tensor
                def _(pe):
                    for q in range(QT):
                        mm = nc.tensor.transpose(psE[:, q, :], ends[:, q * P:q * P + P], ident[0:B, 0:B])
                    mm.then_inc(e_done, 1)
                    for b in range(B):
                        pe.wait_ge(laid, b + 1)
                        if b >= 2:
                            pe.wait_ge(added, b - 1)
                        for t in range(QT):
                            for q in range(QT):
                                mm = nc.tensor.matmul(psA[b % 2][:, t, :], on[:, b % 2, q, t * P:t * P + P],
                                                      ctx_sb[:, b * QT + q, :], start=(q == 0), stop=(q == QT - 1))
                        mm.then_inc(spread, 1)

                @block.vector
                def _(dve):
                    dve.wait_ge(e_done, 1)
                    nc.vector.tensor_copy(last[:], psE[:]).then_inc(e_read, 1)
                    dve.wait_ge(e_read, 1)
                    iota = consts["iota"]
                    for q in range(QT):
                        for b in range(B):
                            n = q * B + b
                            if n >= 2:
                                dve.wait_ge(found, n - 1)
                            nc.vector.scalar_tensor_tensor(out=pick[:, n % 2, :], in0=iota[:], scalar=last[:, q, b:b + 1],
                                                           in1=start[:, q, b, :], op0=ALU.is_equal, op1=ALU.mult,
                                                           accum_out=first[:, q, b:b + 1]).then_inc(found, 1)
                    dve.wait_ge(found, QT * B)

                    def add(b):
                        dve.wait_ge(spread, b + 1)
                        nc.vector.tensor_tensor(x[:, b * QT:b * QT + QT, :], psA[b % 2][:], x[:, b * QT:b * QT + QT, :],
                                                ALU.add).then_inc(added, 1)

                    for b in range(B):
                        for q in range(QT):
                            if b >= 2:
                                dve.wait_ge(laid, b - 1)
                            nc.vector.tensor_scalar(after[:, b % 2, q, :], iota[:], first[:, q, b:b + 1], None,
                                                    ALU.is_ge).then_inc(cut, 1)
                        dve.wait_ge(cut, QT * (b + 1))
                        if b >= 2:
                            dve.wait_ge(spread, b - 1)
                        for q in range(QT):
                            ins = nc.vector.scalar_tensor_tensor(out=on[:, b % 2, q, :], in0=iota[:], scalar=last[:, q, b:b + 1],
                                                                 in1=after[:, b % 2, q, :], op0=ALU.is_le, op1=ALU.mult)
                        ins.then_inc(laid, 1)
                        if b >= 1:
                            add(b - 1)
                    add(B - 1)


HID = 768
HC = HID // P
QSCALE = 1.0 / 127.0


def gated_ffn(nc, name, x, ident, rstd, mean, w_gate, w_up, w_down):
    with Scope(nc, name) as s:
        raw = {n: s.sb(f"raw_{n}", sh, I32) for n, sh in (("g", [P, DC, HID]), ("u", [P, DC, HID]), ("d", [P, HC, D]))}
        W = {n: s.sb(f"w_{n}", list(t.shape)) for n, t in raw.items()}
        xn, xnT = s.sb("xn", [P, 2, QT, D]), s.sb("xnT", [P, 2, DC, S])
        act_g = s.sb("act_g", [P, 2, 2 * S])
        hT = s.sb("hT", [P, 2, HC, S])
        psT, psY = s.ps("psT", [P, 512]), s.ps("psY", [P, QT, D])
        psG, psU = [s.ps(f"psG{i}", [P, 512]) for i in range(2)], [s.ps(f"psU{i}", [P, 512]) for i in range(2)]
        w_in = [s.sem(f"w_in{n}") for n in "gud"]
        w_set, x_norm, t_done, t_read, gu_done, silu_done, h_done, y_ps, x_done = (
            s.sem(n) for n in ("w_set", "x_norm", "t_done", "t_read", "gu_done", "silu_done", "h_done", "y_ps", "x_done"))
        G = HC // 2
        def par(b, p, q):
            return (p * G + q) % 2

        block = s.block()

        @block.sync
        def _(sp):
            for q, (n, src) in enumerate((("g", w_gate), ("u", w_up), ("d", w_down))):
                sp.dma_start(raw[n][:], src.rearrange("(c p) n -> p c n", p=P)).then_inc(w_in[q], 16)

        @block.tensor
        def _(pe):
            def up(b, p, again):
                pe.wait_ge(x_norm, b + 1)
                pe.wait_ge(t_read, b)
                for c in range(DC):
                    for t in range(QT):
                        mm = nc.tensor.transpose(psT[:, c * S + t * P:c * S + t * P + P], xn[:, p, t, c * P:c * P + P], ident[:])
                mm.then_inc(t_done, 1)
                pe.wait_ge(t_read, b + 1)
                for q in range(G):
                    if again or q >= 2:
                        pe.wait_ge(h_done, G * b + q - 1)
                    for ps, w in ((psG, W["g"]), (psU, W["u"])):
                        for f in range(2):
                            for c in range(DC):
                                o = (2 * q + f) * P
                                mm = nc.tensor.matmul(ps[par(b, p, q)][:, f * S:f * S + S], w[:, c, o:o + P], xnT[:, p, c, :],
                                                      start=(c == 0), stop=(c == DC - 1))
                    mm.then_inc(gu_done, 1)

            def down(b, p):
                pe.wait_ge(h_done, G * (b + 1))
                pe.wait_ge(x_done, b)
                for t in range(QT):
                    for f in range(HC):
                        mm = nc.tensor.matmul(psY[:, t, :], hT[:, p, f, t * P:t * P + P], W["d"][:, f, :],
                                              start=(f == 0), stop=(f == HC - 1))
                mm.then_inc(y_ps, 1)

            pe.wait_ge(w_set, 3)
            up(0, 0, False)
            up(1, 1, True)
            down(0, 0)
            up(2, 0, True)
            down(1, 1)
            with pe.Fori(1, B // 2 - 1) as i:
                up(i * 2 + 1, 1, True)
                down(i * 2, 0)
                up(i * 2 + 2, 0, True)
                down(i * 2 + 1, 1)
            up(B - 1, 1, True)
            down(B - 2, 0)
            down(B - 1, 1)

        @block.scalar
        def _(act):
            def silu(b, p, again):
                for q in range(G):
                    k = par(b, p, q)
                    act.wait_ge(gu_done, G * b + q + 1)
                    if again or q >= 2:
                        act.wait_ge(h_done, G * b + q - 1)
                    nc.scalar.activation(act_g[:, k, :], psG[k][:], ACT.Silu).then_inc(silu_done, 1)

            silu(0, 0, False)
            silu(1, 1, True)
            with act.Fori(1, B // 2) as i:
                for k in range(2):
                    silu(i * 2 + k, k, True)

        @block.vector
        def _(dve):
            def normalise(b, p, again):
                if again:
                    dve.wait_ge(t_done, b - 1)
                for t in range(QT):
                    ins = nc.vector.tensor_scalar(xn[:, p, t, :], x[:, b * QT + t, :], mean[:, bass.ds(b * QT + t, 1)],
                                                  rstd[:, bass.ds(b * QT + t, 1)], ALU.subtract, ALU.mult)
                ins.then_inc(x_norm, 1)

            def hidden(b, p, again):
                dve.wait_ge(t_done, b + 1)
                if again:
                    dve.wait_ge(gu_done, G * (b - 1))
                nc.vector.tensor_copy(xnT[:, p, :, :].rearrange("p c n -> p (c n)"), psT[:]).then_inc(t_read, 1)
                if again:
                    dve.wait_ge(y_ps, b - 1)
                for q in range(G):
                    k = par(b, p, q)
                    dve.wait_ge(silu_done, G * b + q + 1)
                    nc.vector.tensor_tensor(hT[:, p, 2 * q:2 * q + 2, :].rearrange("p f n -> p (f n)"), psU[k][:],
                                            act_g[:, k, :], ALU.mult).then_inc(h_done, 1)

            def add(b):
                dve.wait_ge(y_ps, b + 1)
                nc.vector.tensor_tensor(x[:, bass.ds(b * QT, QT), :], psY[:], x[:, bass.ds(b * QT, QT), :], ALU.add)\
                    .then_inc(x_done, 1)

            normalise(0, 0, False)
            normalise(1, 1, False)
            for q, n in enumerate("gud"):
                dve.wait_ge(w_in[q], 16)
                k_ = W[n].shape[1] * W[n].shape[2]
                nc.vector.tensor_scalar(W[n][:].rearrange("p c n -> p (c n)"), raw[n][:].rearrange("p c n -> p (c n)"),
                                        QSCALE, None, ALU.mult).then_inc(w_set, 1)
            hidden(0, 0, False)
            hidden(1, 1, False)
            normalise(2, 0, True)
            add(0)
            hidden(2, 0, True)
            normalise(3, 1, True)
            add(1)
            with dve.Fori(1, B // 2 - 1) as i:
                hidden(i * 2 + 1, 1, True)
                normalise(i * 2 + 2, 0, True)
                add(i * 2)
                hidden(i * 2 + 2, 0, True)
                normalise(i * 2 + 3, 1, True)
                add(i * 2 + 1)
            hidden(B - 1, 1, True)
            add(B - 2)
            add(B - 1)


def find_groups(nc, name, x, ident, rstd, mean, wq, qg, regs, flags):
    with Scope(nc, name) as s:
        wq_sb, g_sb, reg = s.sb("wq", [P, DC, D]), s.sb("g", [P, H, DK]), s.sb("reg", [P, NT])
        xn, xT = s.sb("xn", [P, 2, D]), s.sb("xT", [P, 2, DC, P])
        q = s.sb("q", [P, NT, D])
        big = s.sb("big", [P, NT * H, DK])
        n2, dot = s.sb("n2", [P, NT * H]), s.sb("dot", [P, NT * H])
        g2, gn, gr, gq = s.sb("g2", [P, H, DK]), s.sb("gn", [P, H]), s.sb("gr", [P, H]), s.sb("gq", [P, H, DK])
        gs, root = s.sb("gs", [P, H]), s.sb("root", [P, NT * H])
        sim, t1 = s.sb("sim", [P, NT]), s.sb("t1", [P, NT])
        ends, ends_all = s.sb("ends", [P, 2]), s.sb("ends_all", [P, 2])
        span, inv = s.sb("span", [P, 1]), s.sb("inv", [P, 1])
        col = s.sb("col", [P, 4, NT])
        rows = s.sb("rows", [4 * NT, P], BF16)
        psT, psQ = [s.ps(f"psT{i}", [P, 512]) for i in range(2)], [s.ps(f"psQ{i}", [P, 512]) for i in range(2)]
        psF = s.ps("psF", [P, P])
        (w_in, x_norm, t_done, t_read, q_ps, q_read, step, g_in, g_out, n_in, n_out, e_in, e_out, c_done, f_done, r_done,
         stored) = (s.sem(n) for n in ("w_in", "x_norm", "t_done", "t_read", "q_ps", "q_read", "step", "g_in", "g_out",
                                       "n_in", "n_out", "e_in", "e_out", "c_done", "f_done", "r_done", "stored"))
        block = s.block()

        @block.sync
        def _(sp):
            sp.dma_start(wq_sb[:], wq.rearrange("(c p) n -> p c n", p=P)).then_inc(w_in, 16)
            sp.dma_start(g_sb[:], qg.rearrange("p (h d) -> p h d", h=H)).then_inc(w_in, 16)
            sp.dma_start(reg[:], regs).then_inc(w_in, 16)
            sp.wait_ge(r_done, 1)
            sp.dma_start(flags.rearrange("f (t p) -> (f t) p", p=P), rows[:]).then_inc(stored, 16)
            sp.wait_ge(stored, 16)

        @block.tensor
        def _(pe):
            pe.wait_ge(w_in, 48)

            def tile(t, k, again):
                pe.wait_ge(x_norm, t + 1)
                if again:
                    pe.wait_ge(t_read, t - 1)
                for c in range(DC):
                    mm = nc.tensor.transpose(psT[k][:, c * P:c * P + P], xn[:, k, c * P:c * P + P], ident[:])
                mm.then_inc(t_done, 1)
                pe.wait_ge(t_read, t + 1)
                if again:
                    pe.wait_ge(q_read, t - 1)
                for c in range(DC):
                    mm = nc.tensor.matmul(psQ[k][:, 0:D], xT[:, k, c, :], wq_sb[:, c, :], start=(c == 0), stop=(c == DC - 1))
                mm.then_inc(q_ps, 1)

            tile(0, 0, False)
            tile(1, 1, False)
            with pe.Fori(1, NT // 2) as i:
                for k in range(2):
                    tile(i * 2 + k, k, True)
            pe.wait_ge(c_done, 1)
            nc.tensor.transpose(psF[0:4 * NT, :], col[:].rearrange("p f t -> p (f t)"), ident[:]).then_inc(f_done, 1)

        @block.scalar
        def _(act):
            act.wait_ge(g_in, 1)
            nc.scalar.activation(gs[:], gn[:], ACT.Sqrt).then_inc(g_out, 1)
            with act.Fori(0, NT // 2) as i:
                for k in range(2):
                    act.wait_ge(q_ps, i * 2 + k + 1)
                    nc.scalar.activation(q[:, i * 2 + k, :], psQ[k][:, 0:D], ACT.Copy).then_inc(q_read, 1)
            act.wait_ge(n_in, 1)
            nc.scalar.activation(root[:], n2[:], ACT.Sqrt).then_inc(n_out, 1)

        @block.gpsimd
        def _(pool):
            pool.wait_ge(e_in, 1)
            nc.gpsimd.partition_all_reduce(ends_all[:], ends[:], P, bass.bass_isa.ReduceOp.max).then_inc(e_out, 1)

        @block.vector
        def _(dve):
            n = [0]

            def then(ins):
                n[0] += 1
                ins.then_inc(step, 1)
                dve.wait_ge(step, n[0])

            dve.wait_ge(w_in, 48)
            then(nc.vector.tensor_tensor(g2[:], g_sb[:], g_sb[:], ALU.mult))
            nc.vector.tensor_reduce(gn[:], g2[:], AX.X, ALU.add).then_inc(g_in, 1)
            dve.wait_ge(g_out, 1)
            then(nc.vector.reciprocal(gr[:], gs[:]))
            then(nc.vector.tensor_tensor(gq[:], g_sb[:], gr[:].unsqueeze(2).to_broadcast([P, H, DK]), ALU.mult))

            def tile(t, k, again):
                if again:
                    dve.wait_ge(t_done, t - 1)
                nc.vector.tensor_scalar(xn[:, k, :], x[:, t, :], mean[:, bass.ds(t, 1)], rstd[:, bass.ds(t, 1)],
                                        ALU.subtract, ALU.mult).then_inc(x_norm, 1)
                dve.wait_ge(t_done, t + 1)
                if again:
                    dve.wait_ge(q_ps, t - 1)
                nc.vector.tensor_copy(xT[:, k, :, :].rearrange("p c n -> p (c n)"), psT[k][:, 0:D]).then_inc(t_read, 1)

            tile(0, 0, False)
            tile(1, 1, False)
            with dve.Fori(1, NT // 2) as i:
                for k in range(2):
                    tile(i * 2 + k, k, True)
            dve.wait_ge(q_read, NT)
            q4 = q[:].rearrange("p t (h d) -> p t h d", h=H)
            q3 = q[:].rearrange("p t (h d) -> p (t h) d", h=H)
            then(nc.vector.tensor_tensor(big[:], q3, q3, ALU.mult))
            nc.vector.tensor_reduce(n2[:], big[:], AX.X, ALU.add).then_inc(n_in, 1)
            dve.wait_ge(n_in, 1)
            big4 = big[:].rearrange("p (t m) d -> p t (m d)", t=NT)
            then(nc.vector.tensor_tensor(big4, q[:], gq[:].rearrange("p h d -> p (h d)").unsqueeze(1).to_broadcast([P, NT, D]),
                                         ALU.mult))
            then(nc.vector.tensor_reduce(dot[:], big[:], AX.X, ALU.add))
            dve.wait_ge(n_out, 1)
            then(nc.vector.reciprocal(root[:], root[:]))
            then(nc.vector.tensor_tensor(dot[:], dot[:], root[:], ALU.mult))
            then(nc.vector.tensor_reduce(sim[:], dot[:].rearrange("p (t h) -> p t h", t=NT), AX.X, ALU.add))
            then(nc.vector.tensor_scalar(sim[:], sim[:], 1.0 / H, None, ALU.mult))
            then(nc.vector.scalar_tensor_tensor(out=t1[:], in0=reg[:], scalar=-BIG, in1=sim[:], op0=ALU.mult, op1=ALU.add))
            then(nc.vector.tensor_reduce(ends[:, 0:1], t1[:], AX.X, ALU.max))
            then(nc.vector.scalar_tensor_tensor(out=t1[:], in0=reg[:], scalar=BIG, in1=sim[:], op0=ALU.mult, op1=ALU.add))
            then(nc.vector.tensor_reduce(ends[:, 1:2], t1[:], AX.X, ALU.min))
            nc.vector.tensor_scalar(ends[:, 1:2], ends[:, 1:2], -1.0, None, ALU.mult).then_inc(e_in, 1)
            dve.wait_ge(e_out, 1)
            then(nc.vector.tensor_tensor(span[:], ends_all[:, 0:1], ends_all[:, 1:2], ALU.add))
            then(nc.vector.reciprocal(inv[:], span[:]))
            then(nc.vector.tensor_scalar(t1[:], sim[:], ends_all[:, 1:2], inv[:, 0:1], ALU.add, ALU.mult))
            then(nc.vector.tensor_scalar(t1[:], t1[:], 0.9, None, ALU.is_gt))
            then(nc.vector.tensor_tensor(col[:, 0, :], t1[:], reg[:], ALU.max))
            then(nc.vector.tensor_scalar(col[:, 1, :], col[:, 0, :], -1.0, 1.0, ALU.mult, ALU.add))
            then(nc.vector.tensor_scalar(col[:, 2, :], col[:, 1, :], -BIG, None, ALU.mult))
            then(nc.vector.tensor_tensor(t1[:], col[:, 0, :], reg[:], ALU.subtract))
            nc.vector.tensor_scalar(col[:, 3, :], t1[:], -BIG, None, ALU.mult).then_inc(c_done, 1)
            dve.wait_ge(f_done, 1)
            nc.vector.tensor_copy(rows[:], psF[0:4 * NT, :]).then_inc(r_done, 1)



def program(nc, t, out):
    with Scope(nc, "all") as s:
        x = s.sb("x", [P, NT, D])
        ident = s.sb("ident", [P, P])
        rstd, mean = s.sb("rstd", [P, NT]), s.sb("mean", [P, NT])
        parts_at = nc.dram_tensor("parts_at", (2, 2, 3, D, S), BF16, kind="Internal").ap()
        consts = {"before": s.sb("before", [P, P]), "ones": s.sb("ones", [P, P]), "iota": s.sb("iota", [P, S]),
                  "lane": s.sb("lane", [P, 1])}
        NB = moe_blocks(2)
        slots_x = nc.dram_tensor("slots_x", (NB * P, D), F32, kind="Internal").ap()
        slots_y = nc.dram_tensor("slots_y", (NB * P, D), F32, kind="Internal").ap()
        dma = {"scattered": Counted(s.sem("scattered")), "fetched_w1": [Counted(s.sem(f"fetched_w1{p}")) for p in range(2)],
               "fetched_w2": [Counted(s.sem(f"fetched_w2{p}")) for p in range(2)],
               "back": [Counted(s.sem(f"back{t_}")) for t_ in range(NT)]}
        with Scope(nc, "start") as s0:
            loaded = s0.sem("loaded")
            block = s0.block()

            @block.sync
            def _(sp):
                sp.dma_start(x[:], t["x"].rearrange("b (t p) d -> p (b t) d", p=P)).then_inc(loaded, 16)
                sp.dma_start(ident[:], t["c_ident"]).then_inc(loaded, 16)
                for n, a in consts.items():
                    sp.dma_start(a[:], t[f"c_{n}"]).then_inc(loaded, 16)
                sp.wait_ge(loaded, 32 + 16 * len(consts))

        def weights(pre, names):
            return {k: t[f"{pre}{n}"] for k, n in names.items()}

        layernorm_stats(nc, x, rstd, mean, "l0a")
        attention(nc, "l0a", x, ident, rstd, mean, DK ** -0.5,
                  weights("L0_", {k: k for k in ("wq", "wk", "wv", "wo", "bq", "bk", "bv", "bo")}), parts_at,
                  ctxT=t["ctxT"])

        layernorm_stats(nc, x, rstd, mean, "l0f")
        moe(nc, dma, "l0f", 1, x, ident, rstd, mean, consts, t["L0_wr"], t["L0_br"], (t["L0_table1"], t["L0_table2"]), slots_x, slots_y)

        layernorm_stats(nc, x, rstd, mean, "l1a")
        dist = nc.dram_tensor("dist", (B, S, S), F32, kind="Internal").ap()
        cost = nc.dram_tensor("cost", (B, S + 1, S + 1), F32, kind="Internal").ap()
        table = nc.dram_tensor("table", (B, S, S), BF16, kind="Internal").ap()
        alignment(nc, x, ident, rstd, mean, consts, t["ctx"], t["ctxT"], dist, cost, table)

        layernorm_stats(nc, x, rstd, mean, "l1f")
        gated_ffn(nc, "l1f", x, ident, rstd, mean, t["L1_gate"], t["L1_up"], t["L1_down"])
        layernorm_stats(nc, x, rstd, mean, "l2a")
        attention(nc, "l2a", x, ident, rstd, mean, 1.0,
                  weights("L2_", {k: k for k in ("wq", "wk", "wv", "wo", "wq_swap", "wk_swap")}), parts_at, ctxT=t["ctxT"],
                  rope=(t["c_cos"], t["c_sin"]))
        layernorm_stats(nc, x, rstd, mean, "l2f")
        moe(nc, dma, "l2f", 2, x, ident, rstd, mean, consts, t["L2_wr"], t["L2_br"], (t["L2_table1"], t["L2_table2"]), slots_x, slots_y)
        layernorm_stats(nc, x, rstd, mean, "l3a")
        attention(nc, "l3a", x, ident, rstd, mean, DK ** -0.5,
                  weights("L3_", {k: k for k in ("wq", "wk", "wv", "wo", "bq", "bk", "bv", "bo")}), parts_at, ctxT=t["ctxT"],
                  topk=t["mask"])
        layernorm_stats(nc, x, rstd, mean, "l3f")
        flags = nc.dram_tensor("flags", (4, TOK), BF16, kind="Internal").ap()
        find_groups(nc, "l3g", x, ident, rstd, mean, t["L3f_wq"], t["L3f_guide"], t["c_reg"], flags)
        w = weights("L3f_", {k: k for k in ("wq", "wk", "wv", "wo", "bo")})
        w.update({k: t[f"c_rg_{k}"] for k in ("sel", "own", "fold", "one")})
        attention(nc, "l3f", x, ident, rstd, mean, DK ** -0.5, w, parts_at, groups=flags)

        with Scope(nc, "end") as s1:
            stored = s1.sem("stored")
            block = s1.block()

            @block.sync
            def _(sp):
                sp.dma_start(out.rearrange("b (t p) d -> p (b t) d", p=P), x[:]).then_inc(stored, 16)
                sp.wait_ge(stored, 16)


def kernel(**inputs):
    import concourse.bacc as bacc
    from concourse.bass_utils import run_bass_kernel_spmd

    def c(a):
        return np.ascontiguousarray(a)

    def column(a):
        return c(np.asarray(a).reshape(DC, P).T)

    def rows(a):
        return c(np.broadcast_to(np.asarray(a).reshape(1, -1), (P, np.asarray(a).size)))

    g = {k: np.asarray(v) for k, v in inputs.items()}
    arrays = {
        "x": c(g["x"]),
        "c_ident": np.eye(P, dtype=np.float32),
        "ctx": c(g["ctx_1024"]),
        "c_before": np.triu(np.ones((P, P), np.float32), 1),
        "c_ones": np.ones((P, P), np.float32),
        "c_iota": c(np.broadcast_to(np.arange(S, dtype=np.float32), (P, S))),
        "c_lane": np.arange(P, dtype=np.float32).reshape(P, 1),
        "ctxT": c(g["ctx_1024"].reshape(TOK, DC, P).transpose(1, 2, 0)),
    }
    for n in ("wq", "wk", "wv", "wo"):
        arrays[f"L0_{n}"] = c(g[f"L0_xattn_{n}"].T)
    for n in ("bq", "bk"):
        arrays[f"L0_{n}"] = column(g[f"L0_xattn_{n}"])
    for n in ("bv", "bo"):
        arrays[f"L0_{n}"] = rows(g[f"L0_xattn_{n}"])

    arrays["L1_gate"], arrays["L1_up"], arrays["L1_down"] = (c(g[f"L1_ffn_w_{n}"].T) for n in ("gate", "up", "down"))
    kv = g["L2_xattn_Wkv"].reshape(H, 2, DK, D)
    wk, wv = kv[:, 0].reshape(D, D), kv[:, 1].reshape(D, D)
    swap = np.arange(D) ^ 1
    arrays["L2_wq"], arrays["L2_wk"], arrays["L2_wv"] = c(g["L2_xattn_Wq"].T), c(wk.T), c(wv.T)
    arrays["L2_wq_swap"], arrays["L2_wk_swap"] = c(g["L2_xattn_Wq"][swap].T), c(wk[swap].T)
    arrays["L2_wo"] = c(g["L2_xattn_Wo"].T)
    theta = np.power(np.float32(10000.0), np.float32(2.0) * np.arange(DK // 2, dtype=np.float32) / np.float32(DK))
    ang = (np.arange(S, dtype=np.float32)[:, None] / theta.astype(np.float32)).astype(np.float32)
    sign = np.where(np.arange(P) % 2 == 0, np.float32(-1), np.float32(1))[:, None]
    arrays["c_cos"] = c(np.tile(np.repeat(np.cos(ang), 2, axis=1).T, (P // DK, 1)))
    arrays["c_sin"] = c(np.tile(np.repeat(np.sin(ang), 2, axis=1).T, (P // DK, 1)) * sign)
    for n in ("q", "k", "v", "o"):
        arrays[f"L3_w{n}"] = c(g[f"L3_xattn_W{n}"].T)
        arrays[f"L3_b{n}"] = (column if n in "qk" else rows)(g[f"L3_xattn_b{n}"])
    arrays["mask"] = c(g["mask_BxSxS2_if1"].reshape(B * QT, P, S))
    for n, a in enumerate("qkv"):
        arrays[f"L3f_w{a}"] = c(g["L3_ffn_W_qkv"][:, n * D:(n + 1) * D])
    arrays["L3f_wo"], arrays["L3f_bo"] = c(g["L3_ffn_W_proj"]), rows(g["L3_ffn_b_proj"])
    arrays["L3f_guide"] = rows(g["L3_ffn_g_info"][0, 0])
    reg = np.zeros((P, NT), np.float32)
    reg[:REG, ::QT] = 1
    arrays["c_reg"] = reg
    head = np.arange(H)
    m = np.arange(RG)
    arrays["c_rg_sel"] = c((np.arange(P)[:, None, None] // DK + np.arange(DC)[None, :, None] * (P // DK)
                            == head[None, None, :]).astype(np.float32))
    arrays["c_rg_own"] = c((m[:, None] // REG == np.arange(D)[None, :] // DK).astype(np.float32))
    arrays["c_rg_fold"] = c((m[:, None] % REG == np.arange(REG)[None, :]).astype(np.float32))
    arrays["c_rg_one"] = c(np.stack([np.zeros(RG), np.ones(RG)]).astype(np.float32))
    for k, wr, br in (("L0", "Wr", "br"), ("L2", "Wg", "bg")):
        w1, b1, w2, b2 = (g[f"{k}_ffn_{n}"] for n in ("W1", "b1", "W2", "b2"))
        arrays[f"{k}_wr"], arrays[f"{k}_br"] = c(g[f"{k}_ffn_{wr}"]), rows(g[f"{k}_ffn_{br}"])
        arrays[f"{k}_table1"] = c(np.concatenate([
            w1.reshape(E, DC, P, F).transpose(0, 2, 1, 3).reshape(E * P, DC * F),
            b1.reshape(E, FC, P).transpose(0, 2, 1).reshape(E * P, FC)], axis=1))
        arrays[f"{k}_table2"] = c(np.concatenate([
            w2.reshape(E, FC, P, D).transpose(0, 2, 1, 3).reshape(E * P, FC * D),
            np.broadcast_to(b2.reshape(E, 1, D), (E, P, D)).reshape(E * P, D)], axis=1))

    nc = bacc.Bacc("TRN2", target_bir_lowering=False, num_devices=1)
    aps = {n: nc.dram_tensor(f"in_{n}", a.shape, mybir.dt.from_np(a.dtype), kind="ExternalInput").ap()
           for n, a in arrays.items()}
    out = nc.dram_tensor("out_x", (B, S, D), F32, kind="ExternalOutput").ap()
    program(nc, aps, out)
    r = run_bass_kernel_spmd(nc, [{f"in_{n}": a for n, a in arrays.items()}], core_ids=[0])
    return r.results[0]["out_x"]
```
